# Optimizing a Trainium2 kernel written in Bass

```python
import numpy as np
import jax
import jax.numpy as jnp

def _softmax(x, axis=-1):
    return jax.nn.softmax(x, axis=axis)

def _gelu(x):
    return jax.nn.gelu(x, approximate=True)

def _silu(x):
    return jax.nn.silu(x)

def _sigmoid(x):
    return jax.nn.sigmoid(x)

def _layernorm(x, axis=-1, eps=1e-05):
    m = jnp.mean(x, axis=axis, keepdims=True)
    v = jnp.var(x, axis=axis, keepdims=True)
    return (x - m) / jnp.sqrt(v + eps)

def _scatter_add(tgt, idx, src, axis=0):
    return tgt.at[idx].add(src)

def _segment_sum(src, seg, n):
    return jax.ops.segment_sum(src, seg, n)
kernel_name = 'mk_decoder_preln_d2_seqx_r8_1fea44'

def setup_inputs(seed: int=0):
    np.random.seed(seed)
    _w = jnp.asarray

    def _rec_inputs():
        import jax
        import jax.numpy as jnp
        _rk = jax.random.key(seed)
        x = 2.818e-05 + 1 * jax.random.normal(jax.random.fold_in(_rk, 1), (4, 256, 256), jnp.float32)
        _lenS = 256 - jax.random.randint(jax.random.fold_in(_rk, 7), (4,), 0, max(1, 256 // 4) + 1, jnp.int32)
        _lenS2 = 256 - jax.random.randint(jax.random.fold_in(_rk, 8), (4,), 0, max(1, 256 // 4) + 1, jnp.int32)
        _ctx_1024P = jax.random.normal(jax.random.fold_in(_rk, 11), (4, 16, 128), jnp.float32)
        _ctx_1024c = jax.random.dirichlet(jax.random.fold_in(_rk, 511), 0.3 * jnp.ones((16,), jnp.float32), (4, 256))
        _ctx_1024t = jnp.einsum('bsk,bkd->bsd', _ctx_1024c, _ctx_1024P)
        _ctx_1024t = _ctx_1024t * jax.lax.rsqrt(jnp.mean(jnp.square(_ctx_1024t)) + 1e-12) * 0.953939
        ctx_1024 = 7.22013e-05 + 1.00017 * (_ctx_1024t + 0.3 * jax.random.normal(jax.random.fold_in(_rk, 611), (4, 256, 128), jnp.float32))
        return (x, ctx_1024)
    x, ctx_1024 = _rec_inputs()

    def _L0_attn_setup():
        import jax, jax.numpy as jnp
        import numpy as np
        B, S, HID = (2, 256, 256)
        H, KV, D = (8, 2, 32)
        SW = 64
        SCALAR = 256.0
        EPS = 1e-06
        THETA = 1000000.0
        SOFTCAP = 30.0

        def _layernorm_unit(x, eps=EPS):
            x = x.astype(jnp.float32)
            mu = jnp.mean(x, axis=-1, keepdims=True)
            xc = x - mu
            var = jnp.mean(xc * xc, axis=-1, keepdims=True)
            return xc * jax.lax.rsqrt(var + eps)

        def _rope_cache(seq_len, head_dim, theta):
            inv_freq = 1.0 / theta ** (jnp.arange(0, head_dim, 2, dtype=jnp.float32) / head_dim)
            pos = jnp.arange(seq_len, dtype=jnp.float32)
            freqs = pos[:, None] * inv_freq[None, :]
            emb = jnp.concatenate([freqs, freqs], axis=-1)
            return (jnp.cos(emb), jnp.sin(emb))

        def _rotate_half(x):
            x1, x2 = jnp.split(x, 2, axis=-1)
            return jnp.concatenate([-x2, x1], axis=-1)
        key = jax.random.key(seed)
        ks = jax.random.split(key, 5)
        sc = 0.02
        return {'hidden_states': jax.random.normal(ks[0], (B, S, HID), dtype=jnp.float32), 'Wq': jax.random.normal(ks[1], (H * D, HID), dtype=jnp.float32) * sc, 'Wk': jax.random.normal(ks[2], (KV * D, HID), dtype=jnp.float32) * sc, 'Wv': jax.random.normal(ks[3], (KV * D, HID), dtype=jnp.float32) * sc, 'Wo': jax.random.normal(ks[4], (HID, HID), dtype=jnp.float32) * sc}
    _L0_attn_all = _L0_attn_setup()
    _L0_attn_in = {k: v for k, v in _L0_attn_all.items() if k in ('Wq', 'Wk', 'Wv', 'Wo')}
    del _L0_attn_all

    def _L0_xattn_setup():
        import jax, jax.numpy as jnp
        import numpy as np
        B_, L_, D_MODEL = (4, 256, 128)
        D_STATE, D_CONV, EXPAND = (16, 4, 2)
        D_INNER = EXPAND * D_MODEL
        DT_RANK = (D_MODEL + 15) // 16

        def silu(x):
            return x * jax.nn.sigmoid(x)
        key = jax.random.key(seed)
        ks = jax.random.split(key, 10)
        f32 = jnp.float32
        hidden_states = jax.random.normal(ks[0], (B_, L_, D_MODEL), dtype=f32)
        z = jax.random.normal(ks[1], (B_, D_INNER, L_), dtype=f32)
        in_proj_w = jax.random.normal(ks[2], (D_INNER, D_MODEL), dtype=f32) * 0.02
        conv_w = jax.random.normal(ks[3], (D_INNER, 1, D_CONV), dtype=f32) * 0.1
        conv_b = jax.random.normal(ks[4], (D_INNER,), dtype=f32) * 0.02
        x_proj_w = jax.random.normal(ks[5], (DT_RANK + 2 * D_STATE, D_INNER), dtype=f32) * 0.02
        dt_proj_w = jax.random.uniform(ks[6], (D_INNER, DT_RANK), dtype=f32, minval=-DT_RANK ** (-0.5), maxval=DT_RANK ** (-0.5))
        dt = jnp.exp(jax.random.uniform(ks[7], (D_INNER,), dtype=f32, minval=np.log(0.001), maxval=np.log(0.1)))
        dt_proj_b = jnp.log(jnp.expm1(dt))
        A_log = jnp.log(jnp.broadcast_to(jnp.arange(1, D_STATE + 1, dtype=f32), (D_INNER, D_STATE)))
        D = jnp.ones((D_INNER,), f32)
        return {'hidden_states': hidden_states, 'z': z, 'in_proj_w': in_proj_w, 'conv_w': conv_w, 'conv_b': conv_b, 'x_proj_w': x_proj_w, 'dt_proj_w': dt_proj_w, 'dt_proj_b': dt_proj_b, 'A_log': A_log, 'D': D}
    _L0_xattn_all = _L0_xattn_setup()
    _L0_xattn_in = {k: v for k, v in _L0_xattn_all.items() if k in ('in_proj_w', 'conv_w', 'conv_b', 'x_proj_w', 'dt_proj_w', 'dt_proj_b', 'A_log', 'D')}
    del _L0_xattn_all

    def _L0_ffn_setup():
        import jax, jax.numpy as jnp
        import numpy as np
        HIDDEN = 256
        INTER = 704
        B, S = (2, 256)

        def _ternary(key, shape):
            return jax.random.randint(key, shape, -1, 2).astype(jnp.float32)
        key = jax.random.key(seed)
        ks = jax.random.split(key, 7)
        x = jax.random.normal(ks[0], (B, S, HIDDEN), dtype=jnp.float32)
        gate_w = _ternary(ks[1], (INTER, HIDDEN))
        up_w = _ternary(ks[2], (INTER, HIDDEN))
        down_w = _ternary(ks[3], (HIDDEN, INTER))
        gate_s = jax.random.uniform(ks[4], (INTER,), minval=0.01, maxval=0.1, dtype=jnp.float32)
        up_s = jax.random.uniform(ks[5], (INTER,), minval=0.01, maxval=0.1, dtype=jnp.float32)
        down_s = jax.random.uniform(ks[6], (HIDDEN,), minval=0.01, maxval=0.1, dtype=jnp.float32)
        return {'x': x, 'gate_w': gate_w, 'up_w': up_w, 'down_w': down_w, 'gate_s': gate_s, 'up_s': up_s, 'down_s': down_s}
    _L0_ffn_all = _L0_ffn_setup()
    _L0_ffn_in = {k: v for k, v in _L0_ffn_all.items() if k in ('gate_w', 'up_w', 'down_w', 'gate_s', 'up_s', 'down_s')}
    del _L0_ffn_all

    def _L1_attn_setup():
        import jax, jax.numpy as jnp
        import numpy as np
        B, S, HID = (2, 256, 256)
        H, HKV, D = (16, 4, 128)
        ROPE_BASE = 1000000.0
        EPS = 1e-05

        def _layernorm(x, g, b):
            mu = jnp.mean(x, axis=-1, keepdims=True)
            var = jnp.mean(jnp.square(x - mu), axis=-1, keepdims=True)
            return (x - mu) * jax.lax.rsqrt(var + EPS) * g + b

        def _rope_tables(seq_len, dim, base):
            inv_freq = 1.0 / base ** (jnp.arange(0, dim, 2, dtype=jnp.float32) / dim)
            t = jnp.arange(seq_len, dtype=jnp.float32)
            freqs = jnp.outer(t, inv_freq)
            cos = jnp.concatenate([jnp.cos(freqs), jnp.cos(freqs)], axis=-1)
            sin = jnp.concatenate([jnp.sin(freqs), jnp.sin(freqs)], axis=-1)
            return (cos, sin)

        def _rotate_half(x):
            x1, x2 = jnp.split(x, 2, axis=-1)
            return jnp.concatenate([-x2, x1], axis=-1)
        key = jax.random.key(seed)
        k1, k2, k3 = jax.random.split(key, 3)
        return {'x': jax.random.normal(k1, (B, S, HID), dtype=jnp.float32), 'w_qkv': jax.random.normal(k2, ((H + 2 * HKV) * D, HID), dtype=jnp.float32) * 0.02, 'w_o': jax.random.normal(k3, (HID, H * D), dtype=jnp.float32) * 0.02, 'qn_g': jnp.ones((D,), jnp.float32), 'qn_b': jnp.zeros((D,), jnp.float32), 'kn_g': jnp.ones((D,), jnp.float32), 'kn_b': jnp.zeros((D,), jnp.float32)}
    _L1_attn_all = _L1_attn_setup()
    _L1_attn_in = {k: v for k, v in _L1_attn_all.items() if k in ('w_qkv', 'w_o', 'qn_g', 'qn_b', 'kn_g', 'kn_b')}
    del _L1_attn_all

    def _L1_xattn_setup():
        import jax, jax.numpy as jnp
        import numpy as np
        import math
        B, L, DM = (2, 256, 128)
        DS, DC, EXP = (16, 4, 2)
        DI = EXP * DM
        DR = math.ceil(DM / 16)
        DT_MIN, DT_MAX, DT_FLOOR = (0.001, 0.1, 0.0001)

        def _ssm_forward(hidden_states, z, in_proj_w, conv_w, conv_b, x_proj_w, dt_proj_w, dt_proj_b, A_log, D):
            b = hidden_states.shape[0]
            x = jnp.einsum('ed,bld->bel', in_proj_w, hidden_states)
            xp = jnp.pad(x, ((0, 0), (0, 0), (DC - 1, 0)))
            xc = jax.lax.conv_general_dilated(xp, conv_w[:, None, :], window_strides=(1,), padding='VALID', dimension_numbers=('NCH', 'OIH', 'NCH'), feature_group_count=DI)
            u = jax.nn.silu(xc + conv_b[None, :, None])
            x_dbl = jnp.einsum('ke,bel->bkl', x_proj_w, u)
            dt_lo = x_dbl[:, :DR]
            Bm = x_dbl[:, DR:DR + DS]
            Cm = x_dbl[:, DR + DS:]
            delta = jax.nn.softplus(jnp.einsum('er,brl->bel', dt_proj_w, dt_lo) + dt_proj_b[None, :, None])
            A = -jnp.exp(A_log)

            def step(state, xs):
                d_t, B_t, C_t, u_t = xs
                dA = jnp.exp(d_t[..., None] * A)
                state = state * dA + (d_t * u_t)[..., None] * B_t[:, None, :]
                y_t = jnp.einsum('ben,bn->be', state, C_t)
                return (state, y_t)
            xs = (jnp.moveaxis(delta, -1, 0), jnp.moveaxis(Bm, -1, 0), jnp.moveaxis(Cm, -1, 0), jnp.moveaxis(u, -1, 0))
            state0 = jnp.zeros((b, DI, DS), delta.dtype)
            _, ys = jax.lax.scan(step, state0, xs)
            y = jnp.moveaxis(ys, 0, -1)
            y = y + D[None, :, None] * u
            y = y * jax.nn.silu(z)
            return jnp.swapaxes(y, 1, 2)
        key = jax.random.key(seed)
        ks = jax.random.split(key, 8)
        hidden_states = jax.random.normal(ks[0], (B, L, DM), jnp.float32)
        z = jax.random.normal(ks[1], (B, DI, L), jnp.float32)
        in_proj_w = jax.random.normal(ks[2], (DI, DM), jnp.float32) * DM ** (-0.5)
        conv_w = jax.random.normal(ks[3], (DI, DC), jnp.float32) * DC ** (-0.5)
        conv_b = jnp.zeros((DI,), jnp.float32)
        x_proj_w = jax.random.normal(ks[4], (DR + 2 * DS, DI), jnp.float32) * DI ** (-0.5)
        dt_std = DR ** (-0.5)
        dt_proj_w = jax.random.uniform(ks[5], (DI, DR), jnp.float32, -dt_std, dt_std)
        dt = jnp.exp(jax.random.uniform(ks[6], (DI,), jnp.float32) * (math.log(DT_MAX) - math.log(DT_MIN)) + math.log(DT_MIN))
        dt = jnp.clip(dt, DT_FLOOR)
        dt_proj_b = dt + jnp.log(-jnp.expm1(-dt))
        A_log = jnp.log(jnp.broadcast_to(jnp.arange(1, DS + 1, dtype=jnp.float32), (DI, DS)))
        D = jnp.ones((DI,), jnp.float32)
        return dict(hidden_states=hidden_states, z=z, in_proj_w=in_proj_w, conv_w=conv_w, conv_b=conv_b, x_proj_w=x_proj_w, dt_proj_w=dt_proj_w, dt_proj_b=dt_proj_b, A_log=A_log, D=D)
    _L1_xattn_all = _L1_xattn_setup()
    _L1_xattn_in = {k: v for k, v in _L1_xattn_all.items() if k in ('in_proj_w', 'conv_w', 'conv_b', 'x_proj_w', 'dt_proj_w', 'dt_proj_b', 'A_log', 'D')}
    del _L1_xattn_all

    def _L1_ffn_setup():
        import jax, jax.numpy as jnp
        import numpy as np
        D = 256
        M = 128
        E = 32
        K = 6
        G = 8
        KG = 4
        SH = 256
        SCALE = 2.5

        def _route(xf, Wr, br):
            T = xf.shape[0]
            s = jax.nn.sigmoid(xf @ Wr.T + br)
            sg = s.reshape(T, G, E // G)
            group_w = jax.lax.top_k(sg, 2)[0].sum(-1)
            top_g = jax.lax.top_k(group_w, KG)[1]
            gmask = jnp.zeros((T, G), bool).at[jnp.arange(T)[:, None], top_g].set(True)
            masked = jnp.where(gmask[:, :, None], sg, 0.0).reshape(T, E)
            idx = jax.lax.top_k(masked, K)[1]
            w = jnp.take_along_axis(s, idx, axis=1)
            w = w / (w.sum(-1, keepdims=True) + 1e-20)
            return (idx, w * SCALE)
        key = jax.random.key(seed)
        ks = jax.random.split(key, 7)
        w = 0.02
        return {'hidden_tensor': jax.random.normal(ks[0], (2, 256, D), dtype=jnp.float32), 'Wr': jax.random.normal(ks[1], (E, D), dtype=jnp.float32) * w, 'br': jax.random.normal(ks[2], (E,), dtype=jnp.float32) * w, 'W1': jax.random.normal(ks[3], (E, M, D), dtype=jnp.float32) * w, 'W2': jax.random.normal(ks[4], (E, D, M), dtype=jnp.float32) * w, 'Ws1': jax.random.normal(ks[5], (SH, D), dtype=jnp.float32) * w, 'Ws2': jax.random.normal(ks[6], (D, SH), dtype=jnp.float32) * w}
    _L1_ffn_all = _L1_ffn_setup()
    _L1_ffn_in = {k: v for k, v in _L1_ffn_all.items() if k in ('Wr', 'br', 'W1', 'W2', 'Ws1', 'Ws2')}
    del _L1_ffn_all
    return {'x': x, 'ctx_1024': ctx_1024, 'L0_attn_Wq': _L0_attn_in['Wq'], 'L0_attn_Wk': _L0_attn_in['Wk'], 'L0_attn_Wv': _L0_attn_in['Wv'], 'L0_attn_Wo': _L0_attn_in['Wo'], 'L0_xattn_in_proj_w': _L0_xattn_in['in_proj_w'], 'L0_xattn_conv_w': _L0_xattn_in['conv_w'], 'L0_xattn_conv_b': _L0_xattn_in['conv_b'], 'L0_xattn_x_proj_w': _L0_xattn_in['x_proj_w'], 'L0_xattn_dt_proj_w': _L0_xattn_in['dt_proj_w'], 'L0_xattn_dt_proj_b': _L0_xattn_in['dt_proj_b'], 'L0_xattn_A_log': _L0_xattn_in['A_log'], 'L0_xattn_D': _L0_xattn_in['D'], 'L0_ffn_gate_w': _L0_ffn_in['gate_w'], 'L0_ffn_up_w': _L0_ffn_in['up_w'], 'L0_ffn_down_w': _L0_ffn_in['down_w'], 'L0_ffn_gate_s': _L0_ffn_in['gate_s'], 'L0_ffn_up_s': _L0_ffn_in['up_s'], 'L0_ffn_down_s': _L0_ffn_in['down_s'], 'L1_attn_w_qkv': _L1_attn_in['w_qkv'], 'L1_attn_w_o': _L1_attn_in['w_o'], 'L1_attn_qn_g': _L1_attn_in['qn_g'], 'L1_attn_qn_b': _L1_attn_in['qn_b'], 'L1_attn_kn_g': _L1_attn_in['kn_g'], 'L1_attn_kn_b': _L1_attn_in['kn_b'], 'L1_xattn_in_proj_w': _L1_xattn_in['in_proj_w'], 'L1_xattn_conv_w': _L1_xattn_in['conv_w'], 'L1_xattn_conv_b': _L1_xattn_in['conv_b'], 'L1_xattn_x_proj_w': _L1_xattn_in['x_proj_w'], 'L1_xattn_dt_proj_w': _L1_xattn_in['dt_proj_w'], 'L1_xattn_dt_proj_b': _L1_xattn_in['dt_proj_b'], 'L1_xattn_A_log': _L1_xattn_in['A_log'], 'L1_xattn_D': _L1_xattn_in['D'], 'L1_ffn_Wr': _L1_ffn_in['Wr'], 'L1_ffn_br': _L1_ffn_in['br'], 'L1_ffn_W1': _L1_ffn_in['W1'], 'L1_ffn_W2': _L1_ffn_in['W2'], 'L1_ffn_Ws1': _L1_ffn_in['Ws1'], 'L1_ffn_Ws2': _L1_ffn_in['Ws2']}

def reference(x, ctx_1024, L0_attn_Wq, L0_attn_Wk, L0_attn_Wv, L0_attn_Wo, L0_xattn_in_proj_w, L0_xattn_conv_w, L0_xattn_conv_b, L0_xattn_x_proj_w, L0_xattn_dt_proj_w, L0_xattn_dt_proj_b, L0_xattn_A_log, L0_xattn_D, L0_ffn_gate_w, L0_ffn_up_w, L0_ffn_down_w, L0_ffn_gate_s, L0_ffn_up_s, L0_ffn_down_s, L1_attn_w_qkv, L1_attn_w_o, L1_attn_qn_g, L1_attn_qn_b, L1_attn_kn_g, L1_attn_kn_b, L1_xattn_in_proj_w, L1_xattn_conv_w, L1_xattn_conv_b, L1_xattn_x_proj_w, L1_xattn_dt_proj_w, L1_xattn_dt_proj_b, L1_xattn_A_log, L1_xattn_D, L1_ffn_Wr, L1_ffn_br, L1_ffn_W1, L1_ffn_W2, L1_ffn_Ws1, L1_ffn_Ws2):
    import jax
    import jax.numpy as jnp

    def _L0_attn_ref(hidden_states, Wq, Wk, Wv, Wo):
        import jax, jax.numpy as jnp
        import numpy as np
        B, S, HID = (2, 256, 256)
        H, KV, D = (8, 2, 32)
        SW = 64
        SCALAR = 256.0
        EPS = 1e-06
        THETA = 1000000.0
        SOFTCAP = 30.0

        def _layernorm_unit(x, eps=EPS):
            x = x.astype(jnp.float32)
            mu = jnp.mean(x, axis=-1, keepdims=True)
            xc = x - mu
            var = jnp.mean(xc * xc, axis=-1, keepdims=True)
            return xc * jax.lax.rsqrt(var + eps)

        def _rope_cache(seq_len, head_dim, theta):
            inv_freq = 1.0 / theta ** (jnp.arange(0, head_dim, 2, dtype=jnp.float32) / head_dim)
            pos = jnp.arange(seq_len, dtype=jnp.float32)
            freqs = pos[:, None] * inv_freq[None, :]
            emb = jnp.concatenate([freqs, freqs], axis=-1)
            return (jnp.cos(emb), jnp.sin(emb))

        def _rotate_half(x):
            x1, x2 = jnp.split(x, 2, axis=-1)
            return jnp.concatenate([-x2, x1], axis=-1)
        b, s, _ = hidden_states.shape
        q = jnp.einsum('bsh,oh->bso', hidden_states, Wq).reshape(b, s, H, D).transpose(0, 2, 1, 3)
        k = jnp.einsum('bsh,oh->bso', hidden_states, Wk).reshape(b, s, KV, D).transpose(0, 2, 1, 3)
        v = jnp.einsum('bsh,oh->bso', hidden_states, Wv).reshape(b, s, KV, D).transpose(0, 2, 1, 3)
        cos, sin = _rope_cache(s, D, THETA)
        cos = cos[None, None]
        sin = sin[None, None]
        q = q * cos + _rotate_half(q) * sin
        k = k * cos + _rotate_half(k) * sin
        q = _layernorm_unit(q) * SCALAR
        k = _layernorm_unit(k)
        v = _layernorm_unit(v)
        rep = H // KV
        k = jnp.repeat(k, rep, axis=1)
        v = jnp.repeat(v, rep, axis=1)
        scores = jnp.einsum('bhqd,bhkd->bhqk', q, k) / jnp.sqrt(jnp.float32(D))
        i = jnp.arange(s)[:, None]
        j = jnp.arange(s)[None, :]
        allowed = (j <= i) & (j > i - SW)
        mask = jnp.where(allowed, 0.0, -jnp.inf).astype(scores.dtype)
        scores = scores + mask
        scores = jnp.tanh(scores / SOFTCAP) * SOFTCAP
        probs = jax.nn.softmax(scores.astype(jnp.float32), axis=-1).astype(v.dtype)
        out = jnp.einsum('bhqk,bhkd->bhqd', probs, v)
        out = out.transpose(0, 2, 1, 3).reshape(b, s, H * D)
        return jnp.einsum('bso,ho->bsh', out, Wo)

    def _L0_xattn_ref(hidden_states, z, in_proj_w, conv_w, conv_b, x_proj_w, dt_proj_w, dt_proj_b, A_log, D):
        import jax, jax.numpy as jnp
        import numpy as np
        B_, L_, D_MODEL = (4, 256, 128)
        D_STATE, D_CONV, EXPAND = (16, 4, 2)
        D_INNER = EXPAND * D_MODEL
        DT_RANK = (D_MODEL + 15) // 16

        def silu(x):
            return x * jax.nn.sigmoid(x)
        Bsz, L, _ = hidden_states.shape
        d_inner, _, d_conv = conv_w.shape
        dt_rank = dt_proj_w.shape[1]
        d_state = A_log.shape[1]
        x = jnp.einsum('bld,ed->bel', hidden_states, in_proj_w)
        xc = jax.lax.conv_general_dilated(x, conv_w, window_strides=(1,), padding=[(d_conv - 1, 0)], feature_group_count=d_inner, dimension_numbers=('NCH', 'OIH', 'NCH'))
        x = silu(xc + conv_b[None, :, None])
        x_dbl = jnp.einsum('bdl,ed->bel', x, x_proj_w)
        dt_low, Bm, Cm = jnp.split(x_dbl, [dt_rank, dt_rank + d_state], axis=1)
        dt = jnp.einsum('brl,dr->bdl', dt_low, dt_proj_w)
        dt = jax.nn.softplus(dt + dt_proj_b[None, :, None])
        A = -jnp.exp(A_log)
        dt_t = jnp.moveaxis(dt, -1, 0)
        B_t = jnp.moveaxis(Bm, -1, 0)
        C_t = jnp.moveaxis(Cm, -1, 0)
        u_t = jnp.moveaxis(x, -1, 0)

        def step(state, inp):
            d, b, c, u = inp
            dA = jnp.exp(d[..., None] * A)
            state = state * dA + (d * u)[..., None] * b[:, None, :]
            y = jnp.einsum('bdn,bn->bd', state, c)
            return (state, y)
        state0 = jnp.zeros((Bsz, d_inner, d_state), x.dtype)
        _, ys = jax.lax.scan(step, state0, (dt_t, B_t, C_t, u_t))
        y = jnp.moveaxis(ys, 0, 2)
        y = y + D[None, :, None] * x
        y = y * silu(z)
        return jnp.swapaxes(y, 1, 2)

    def _L0_ffn_ref(x, gate_w, up_w, down_w, gate_s, up_s, down_s):
        import jax, jax.numpy as jnp
        import numpy as np
        HIDDEN = 256
        INTER = 704
        B, S = (2, 256)

        def _ternary(key, shape):
            return jax.random.randint(key, shape, -1, 2).astype(jnp.float32)
        b, s, h = x.shape
        xf = x.reshape(b * s, h)
        g = jnp.einsum('th,ih->ti', xf, gate_w) * gate_s
        u = jnp.einsum('th,ih->ti', xf, up_w) * up_s
        hdn = jax.nn.silu(g) * u
        out = jnp.einsum('ti,hi->th', hdn, down_w) * down_s
        return out.reshape(b, s, -1)

    def _L1_attn_ref(x, w_qkv, w_o, qn_g, qn_b, kn_g, kn_b):
        import jax, jax.numpy as jnp
        import numpy as np
        B, S, HID = (2, 256, 256)
        H, HKV, D = (16, 4, 128)
        ROPE_BASE = 1000000.0
        EPS = 1e-05

        def _layernorm(x, g, b):
            mu = jnp.mean(x, axis=-1, keepdims=True)
            var = jnp.mean(jnp.square(x - mu), axis=-1, keepdims=True)
            return (x - mu) * jax.lax.rsqrt(var + EPS) * g + b

        def _rope_tables(seq_len, dim, base):
            inv_freq = 1.0 / base ** (jnp.arange(0, dim, 2, dtype=jnp.float32) / dim)
            t = jnp.arange(seq_len, dtype=jnp.float32)
            freqs = jnp.outer(t, inv_freq)
            cos = jnp.concatenate([jnp.cos(freqs), jnp.cos(freqs)], axis=-1)
            sin = jnp.concatenate([jnp.sin(freqs), jnp.sin(freqs)], axis=-1)
            return (cos, sin)

        def _rotate_half(x):
            x1, x2 = jnp.split(x, 2, axis=-1)
            return jnp.concatenate([-x2, x1], axis=-1)
        b, s, _ = x.shape
        qkv = jnp.einsum('bsh,oh->bso', x, w_qkv)
        q, k, v = jnp.split(qkv, [H * D, (H + HKV) * D], axis=-1)
        q = q.reshape(b, s, H, D).transpose(0, 2, 1, 3)
        k = k.reshape(b, s, HKV, D).transpose(0, 2, 1, 3)
        v = v.reshape(b, s, HKV, D).transpose(0, 2, 1, 3)
        q = _layernorm(q, qn_g, qn_b)
        k = _layernorm(k, kn_g, kn_b)
        cos, sin = _rope_tables(s, D, ROPE_BASE)
        q = q * cos + _rotate_half(q) * sin
        k = k * cos + _rotate_half(k) * sin
        rep = H // HKV
        k = jnp.repeat(k, rep, axis=1)
        v = jnp.repeat(v, rep, axis=1)
        scores = jnp.einsum('bhqd,bhkd->bhqk', q, k) / jnp.sqrt(jnp.float32(D))
        causal = jnp.triu(jnp.ones((s, s), dtype=bool), k=1)
        scores = jnp.where(causal, -jnp.inf, scores)
        weights = jax.nn.softmax(scores, axis=-1)
        attn = jnp.einsum('bhqk,bhkd->bhqd', weights, v)
        attn = attn.transpose(0, 2, 1, 3).reshape(b, s, H * D)
        return jnp.einsum('bsd,od->bso', attn, w_o)

    def _L1_xattn_ref(hidden_states, z, in_proj_w, conv_w, conv_b, x_proj_w, dt_proj_w, dt_proj_b, A_log, D):
        import jax, jax.numpy as jnp
        import numpy as np
        import math
        B, L, DM = (2, 256, 128)
        DS, DC, EXP = (16, 4, 2)
        DI = EXP * DM
        DR = math.ceil(DM / 16)
        DT_MIN, DT_MAX, DT_FLOOR = (0.001, 0.1, 0.0001)

        def _ssm_forward(hidden_states, z, in_proj_w, conv_w, conv_b, x_proj_w, dt_proj_w, dt_proj_b, A_log, D):
            b = hidden_states.shape[0]
            x = jnp.einsum('ed,bld->bel', in_proj_w, hidden_states)
            xp = jnp.pad(x, ((0, 0), (0, 0), (DC - 1, 0)))
            xc = jax.lax.conv_general_dilated(xp, conv_w[:, None, :], window_strides=(1,), padding='VALID', dimension_numbers=('NCH', 'OIH', 'NCH'), feature_group_count=DI)
            u = jax.nn.silu(xc + conv_b[None, :, None])
            x_dbl = jnp.einsum('ke,bel->bkl', x_proj_w, u)
            dt_lo = x_dbl[:, :DR]
            Bm = x_dbl[:, DR:DR + DS]
            Cm = x_dbl[:, DR + DS:]
            delta = jax.nn.softplus(jnp.einsum('er,brl->bel', dt_proj_w, dt_lo) + dt_proj_b[None, :, None])
            A = -jnp.exp(A_log)

            def step(state, xs):
                d_t, B_t, C_t, u_t = xs
                dA = jnp.exp(d_t[..., None] * A)
                state = state * dA + (d_t * u_t)[..., None] * B_t[:, None, :]
                y_t = jnp.einsum('ben,bn->be', state, C_t)
                return (state, y_t)
            xs = (jnp.moveaxis(delta, -1, 0), jnp.moveaxis(Bm, -1, 0), jnp.moveaxis(Cm, -1, 0), jnp.moveaxis(u, -1, 0))
            state0 = jnp.zeros((b, DI, DS), delta.dtype)
            _, ys = jax.lax.scan(step, state0, xs)
            y = jnp.moveaxis(ys, 0, -1)
            y = y + D[None, :, None] * u
            y = y * jax.nn.silu(z)
            return jnp.swapaxes(y, 1, 2)
        return _ssm_forward(hidden_states, z, in_proj_w, conv_w, conv_b, x_proj_w, dt_proj_w, dt_proj_b, A_log, D)

    def _L1_ffn_ref(hidden_tensor, Wr, br, W1, W2, Ws1, Ws2):
        import jax, jax.numpy as jnp
        import numpy as np
        D = 256
        M = 128
        E = 32
        K = 6
        G = 8
        KG = 4
        SH = 256
        SCALE = 2.5

        def _route(xf, Wr, br):
            T = xf.shape[0]
            s = jax.nn.sigmoid(xf @ Wr.T + br)
            sg = s.reshape(T, G, E // G)
            group_w = jax.lax.top_k(sg, 2)[0].sum(-1)
            top_g = jax.lax.top_k(group_w, KG)[1]
            gmask = jnp.zeros((T, G), bool).at[jnp.arange(T)[:, None], top_g].set(True)
            masked = jnp.where(gmask[:, :, None], sg, 0.0).reshape(T, E)
            idx = jax.lax.top_k(masked, K)[1]
            w = jnp.take_along_axis(s, idx, axis=1)
            w = w / (w.sum(-1, keepdims=True) + 1e-20)
            return (idx, w * SCALE)
        B, Tlen, C = hidden_tensor.shape
        xf = hidden_tensor.reshape(-1, C).astype(jnp.float32)
        T = xf.shape[0]
        idx, w = _route(xf, Wr, br)
        gate = jnp.zeros((T, E), w.dtype).at[jnp.arange(T)[:, None], idx].add(w)

        def step(acc, ew):
            w1, w2, g = ew
            h = jnp.square(jax.nn.relu(xf @ w1.T)) @ w2.T
            return (acc + g[:, None] * h, None)
        acc, _ = jax.lax.scan(step, jnp.zeros_like(xf), (W1, W2, gate.T))
        moe_out = acc.reshape(B, Tlen, C).astype(hidden_tensor.dtype)
        shared = jnp.square(jax.nn.relu(hidden_tensor @ Ws1.T)) @ Ws2.T
        return shared + moe_out
    x = x + _L0_attn_ref(_layernorm(x, axis=-1), L0_attn_Wq, L0_attn_Wk, L0_attn_Wv, L0_attn_Wo)
    x = x + _L0_xattn_ref(ctx_1024, _layernorm(x, axis=-1), L0_xattn_in_proj_w, L0_xattn_conv_w, L0_xattn_conv_b, L0_xattn_x_proj_w, L0_xattn_dt_proj_w, L0_xattn_dt_proj_b, L0_xattn_A_log, L0_xattn_D)
    x = x + _L0_ffn_ref(_layernorm(x, axis=-1), L0_ffn_gate_w, L0_ffn_up_w, L0_ffn_down_w, L0_ffn_gate_s, L0_ffn_up_s, L0_ffn_down_s)
    x = x + _L1_attn_ref(_layernorm(x, axis=-1), L1_attn_w_qkv, L1_attn_w_o, L1_attn_qn_g, L1_attn_qn_b, L1_attn_kn_g, L1_attn_kn_b)
    x = x + _L1_xattn_ref(ctx_1024, _layernorm(x, axis=-1), L1_xattn_in_proj_w, L1_xattn_conv_w, L1_xattn_conv_b, L1_xattn_x_proj_w, L1_xattn_dt_proj_w, L1_xattn_dt_proj_b, L1_xattn_A_log, L1_xattn_D)
    x = x + _L1_ffn_ref(_layernorm(x, axis=-1), L1_ffn_Wr, L1_ffn_br, L1_ffn_W1, L1_ffn_W2, L1_ffn_Ws1, L1_ffn_Ws2)
    return x

_drawn_inputs = setup_inputs


def setup_inputs(seed=0):
    import zlib

    import numpy as np

    out = dict(_drawn_inputs(seed))
    spreads = {'L0_xattn_D': (1.0, 0.6),
     'L1_attn_qn_g': (1.0, 0.6),
     'L1_attn_qn_b': (0.0, 0.8),
     'L1_attn_kn_g': (1.0, 0.6),
     'L1_attn_kn_b': (0.0, 0.8),
     'L1_xattn_conv_b': (0.0, 0.1),
     'L1_xattn_D': (1.0, 0.2)}
    factors = {'L0_xattn_in_proj_w': 3.803,
     'L0_xattn_conv_w': 3.955,
     'L0_xattn_conv_b': 8.0,
     'L0_xattn_x_proj_w': 8.0,
     'L0_xattn_dt_proj_w': 8.0,
     'L0_xattn_dt_proj_b': 8.0,
     'L0_xattn_A_log': 8.0,
     'L1_xattn_dt_proj_w': 6.563,
     'L1_xattn_dt_proj_b': 2.727,
     'L1_ffn_br': 8.0}
    for name, (base, spread) in spreads.items():
        noise = np.random.default_rng([zlib.crc32(name.encode()), seed]).standard_normal(out[name].shape)
        drawn = base * np.exp(spread * noise) if base else spread * noise
        out[name] = jnp.asarray(drawn.astype(out[name].dtype))
    for name, factor in factors.items():
        out[name] = (out[name] * factor).astype(out[name].dtype)
    return out
```

```python
from contextlib import ExitStack

import concourse.bass as bass
import numpy as np
from concourse import mybir

F32 = mybir.dt.float32
BF16 = mybir.dt.bfloat16
I32 = mybir.dt.int32
ALU = mybir.AluOpType
ACT = mybir.ActivationFunctionType
AX = mybir.AxisListType

P = 128
B, S, HID = 4, 256, 256
T = B * S
NT = T // P
HC = HID // P
DM, DI, DS, DC, DR = 128, 256, 16, 4, 8
DT = DI // P
H0, KV0, D0, WIN0 = 8, 2, 32, 64
REP0 = H0 // KV0
NQK0 = (H0 + KV0) * D0
NQKV0 = NQK0 + KV0 * D0
SCORE0 = 256.0 / (D0 ** 0.5) / 30.0
SOFTCAP = 30.0
W0 = P + WIN0
INTER = 704
NI = (INTER + P - 1) // P
H1, KV1, D1 = 16, 4, 128
REP1 = H1 // KV1
NQ1, NK1 = H1 * D1, KV1 * D1
E, G, KG, K, M, SH = 32, 8, 4, 6, 128, 256
EPG = E // G
ROUTE_SCALE = 2.5
SB_LOADS = 2
WRING = 4

PK_IN = 0
PK_CW = PK_IN + DI
PK_CB = PK_CW + DC * DI
PK_DB = PK_CB + DT
PK_A = PK_DB + DT
PK_X = PK_A + DT * DS
PK_N = PK_X + DT * (DR + 2 * DS)

C_ON_DVE = {0: [n for n in range(DS) if n % 3 != 1], 1: [n for n in range(DS) if n % 3 == 1]}


def c_step(g):
    mine = lambda q: q % DS in C_ON_DVE[q // DS]
    return ("c_dve" if mine(g) else "c_pool"), sum(mine(q) == mine(g) for q in range(g + 1))


def mlen(i):
    return min(P, INTER - i * P)


class Chain:

    def __init__(self, eng, sem):
        self.eng, self.sem, self.n = eng, sem, 0

    def step(self, ins):
        self.n += 1
        ins.then_inc(self.sem, 1)
        return self.n

    def wait(self, mark=None):
        self.eng.wait_ge(self.sem, self.n if mark is None else mark)

    def link(self, ins):
        self.step(ins)
        self.wait()


def build(nc, io, out):
    ctx = ExitStack()
    with ctx:
        def sb(name, shape, dt=F32):
            return ctx.enter_context(nc.sbuf_tensor(name, shape, dt))

        def sem(name):
            return ctx.enter_context(nc.semaphore(name))

        X = sb("X", [P, NT, HID])
        H = sb("H", [P, NT, HID])
        hT = sb("hT", [P, HC, T])
        ctxp = sb("ctxp", [P, B, S + DC - 1])
        pkb = sb("pkb", [P, PK_N])
        pk = [pkb, pkb]
        skip = sb("skip", [P, 2, DT])
        dtw = [sb(f"dtw{l}", [DR, DI]) for l in range(2)]
        LW = [pk[l][:, PK_CW:PK_CW + DC * DI].rearrange("p (k n) -> p k n", k=DC) for l in range(2)]
        DEL = sb("DEL", [P, DT, T])
        DU = sb("DU", [P, DT, T])
        ACC = sb("ACC", [P, DT, T])
        U = ACC
        dA = [sb(f"dA{s}", [P, DT, T]) for s in range(2)]
        hS = [sb(f"hS{s}", [P, DT, T]) for s in range(2)]
        BCb = [sb(f"BCb{s}", [P, 2, T]) for s in range(SB_LOADS)]
        negA = sb("negA", [P, DT * DS])
        cbh = sb("cbh", [P, DT])
        ident = sb("ident", [P, P])
        identb = sb("identb", [P, P], BF16)
        mask0 = sb("mask0", [P, W0 + P], BF16)
        mask1 = sb("mask1", [P, 3 * P], BF16)
        tabs = sb("tabs", [P, 6, 2, D1])
        lnst = sb("lnst", [P, NT, 6])
        lnmv = sb("lnmv", [P, NT, 2])
        lnve = sb("lnve", [P, NT])
        lnrs = sb("lnrs", [P, NT])
        mhalf = sb("mhalf", [P, NT])
        ones1 = sb("ones1", [1, P])
        WA = sb("WA", [P, H1 * HID])
        WGU = WA[:, 0:HC * 2 * INTER].rearrange("p (c n) -> p c n", c=HC)
        WO1 = WA[:, 0:H1 * HID].rearrange("p (h n) -> p h n", h=H1)
        fsc = sb("fsc", [P, 3, NI])
        dsc = sb("dsc", [P, HID])
        WB = sb("WB", [P, HC, NQ1 + 2 * NK1])
        WQKV0 = WB[:, 0, 0:HC * NQKV0].rearrange("p (c n) -> p c n", c=HC)
        WO0 = WB[:, 0, HC * NQKV0:HC * NQKV0 + HC * HID].rearrange("p (c n) -> p c n", c=HC)
        WE = [WB[:, 0, 512 * s:512 * s + 512] for s in range(WRING)]
        WS = [WB[:, 1, 512 * s:512 * s + 512] for s in range(2)]
        WRT = WB[:, 1, 1024:1024 + HC * E].rearrange("p (c e) -> p c e", c=HC)
        BR = WB[0:1, 1, 1024 + HC * E:1024 + HC * E + E]
        wmean = sb("wmean", [P, HC, H1 + KV1])
        arena = sb("arena", [P, 48 * 256])
        kb = 256

        def ar(k0, n):
            return arena[:, int(k0 * kb):int(k0 * kb) + n]

        Q0 = ar(0, NT * NQKV0).rearrange("p (t n) -> p t n", t=NT)
        RA = ar(12, NT * NQK0).rearrange("p (t n) -> p t n", t=NT)
        RB = ar(22, NT * NQK0).rearrange("p (t n) -> p t n", t=NT)
        SQ0 = ar(12, NT * NQKV0)
        K40 = ar(12, NT * KV0 * P).rearrange("p (t g n) -> p t g n", t=NT, g=KV0)
        cos0 = ar(32, 2 * NQK0).rearrange("p (h n) -> p h n", h=2)
        sin0 = ar(35, 2 * NQK0).rearrange("p (h n) -> p h n", h=2)
        qT0 = ar(32, KV0 * T).rearrange("p (g t) -> p g t", g=KV0)
        kT0 = ar(40, KV0 * T).rearrange("p (g t) -> p g t", g=KV0)
        TH0 = ar(12, REP0 * (W0 + P)).rearrange("p (r n) -> p r n", r=REP0)
        PT0 = [z.rearrange("p (r k q) -> p r k q", r=REP0, k=2) for z in (WB[:, 1, 0:REP0 * 2 * S], ar(22, REP0 * 2 * S))]
        st0 = ar(30, 4 * NT * NQKV0 // D0).rearrange("p (i n) -> p i n", i=4)
        ones32 = sb("ones32", [P, D0])
        rden0 = ar(17, S)
        aT0 = H[:].rearrange("p (g t) d -> p g (t d)", g=KV0)
        WDN = ar(40, NI * HID).rearrange("p (i n) -> p i n", i=NI)
        hid0 = ar(0, NI * T).rearrange("p (i t) -> p i t", i=NI)
        fth = [ar(24 + 2 * s, 512) for s in range(2)]
        ft1 = [ar(28 + 2 * s, 512) for s in range(2)]
        rope1 = ar(32, 8 * D1).rearrange("p (i h d) -> p i h d", i=4, h=2)
        gains = ar(36, 8 * D1).rearrange("p (i d) -> p i d", i=8)
        SQ = ar(0, 1024).rearrange("p (t n) -> p t n", t=2)
        JA = ar(4, 1024).rearrange("p (t n) -> p t n", t=2)
        JB = ar(8, 1024).rearrange("p (t n) -> p t n", t=2)
        R = ar(12, 1024).rearrange("p (t n) -> p t n", t=2)
        KT = [ar(16 + 4 * s, 1024).rearrange("p (h q) -> p h q", h=KV1) for s in range(2)]
        QT = [ar(24 + 4 * s, 1024).rearrange("p (h q) -> p h q", h=REP1) for s in range(2)]
        V1 = [ar(32 + 4 * s, 1024).rearrange("p (t n) -> p t n", t=2) for s in range(2)]
        P1 = [ar(40 + 1.5 * s, 384) for s in range(2)]
        PT1 = [ar(43 + 1.5 * s, 384) for s in range(2)]
        aT1 = [ar(46 + s, 256) for s in range(2)]
        jst = sb("jst", [P, 3, 8])
        nm1 = sb("nm1", [P, 2, 2])
        sum1 = sb("sum1", [P, 2, 2])
        rc1 = sb("rc1", [P, 2, 2])
        GB = [ar(4 * s, T) for s in range(WRING)]
        MR = [ar(16 + 4 * s, T) for s in range(2)]
        MG = [ar(24 + 4 * s, T) for s in range(2)]
        MH = [ar(32 + 4 * s, T) for s in range(2)]
        gT = ar(40, T)[0:E, :]
        at = [24 * kb]

        def router(*shape):
            n = int(np.prod(shape))
            at[0] += n
            z = arena[:, at[0] - n:at[0]]
            return z if len(shape) == 1 else z.rearrange("p (t n) -> p t n", t=shape[0])

        rS, rW, rGate = router(NT, E), router(NT, E), router(NT, E)
        rg = [router(NT * G) for i in range(6)]
        rGW, rGM = router(NT, G + 4), router(NT, G + 4)
        rMS, rME = router(NT, E + 2), router(NT, E + 2)
        rM8, rT8, rE8 = router(NT, 8), router(NT, 8), router(NT, 8)
        rsum = router(2, NT)
        ps = ctx.enter_context(nc.psum_tensor("ps", [P, 8, 512], F32))

        bc_dram = nc.dram_tensor("bc_dram", [2, DS, 2, T], F32, kind="Internal").ap()
        gate_dram = nc.dram_tensor("gate_dram", [E, T], F32, kind="Internal").ap()

        ld = {n: sem("ld_" + n) for n in ("ctx", "pk0", "pk1", "x", "ident", "masks", "rope0", "rope1", "wqkv0",
                                          "wo0", "ffn", "wdn", "wqkv1", "wo1", "shared", "route")}
        ld_bc = [sem(f"ld_bc{s}") for s in range(SB_LOADS)]
        ld_we = [sem(f"ld_we{s}") for s in range(WRING)]
        ld_gb = [sem(f"ld_gb{s}") for s in range(WRING)]
        names = """act_chain dve_chain pool_chain init lw_ready conv_mm conv_tanh u_ready xdbl_mm dt_low_copied bc_copied bc_stored
            dtpre_mm sp_abs sp_exp sp_ln delta_ready da_cols_zero da_ready dbu_ready scan_done c_dve c_pool ssm_acc
            ln_mv ln_rstd ln_h ln_tr_mm ln_tr_act ln_tr_dve qkv0_mm qkv0_copied rope0_rot rope0_sq rope0_done k4_ready tr0_mm tr0_copied
            s0_mm s0_tanh s0_exp pv0_mm at0_ready o0_mm x_new gate_tanh gate_y gate_mm nega_exp nega_ready pt0_fill
            f_mm f_tanh f_hid fd_mm wdn_ready w1_mean w1_centered tabs_ready job_mm job_sq job_rot job_sum job_rstd job_add job_rope
            job_tr_mm job_tr_copied v_mm v_copied s1_mm s1_max s1_exp s1_norm pt1_mm pt1_copied pv1_mm at1_copied o1_mm
            r_mm r_exp r_gate gt_mm gt_copied gate_stored m_mm m_relu m_gated m_hid m_out out_done""".split()
        s = {n: sem(n) for n in names}
        block = ctx.enter_context(nc.Block())

        bands = lambda a: a.rearrange("p (b s) -> p b s", b=B)
        xr = io["x"].rearrange("b (h p) d -> p (b h) d", p=P)
        outr = out.rearrange("b (h p) d -> p (b h) d", p=P)

        XN_ATT0, XN_GATE0, XN_FFN, XN_ATT1, XN_GATE1 = 2, 4, 6, 10, 12
        XN = {0: 0, 1: XN_ATT0, 2: XN_GATE0, 3: XN_FFN, 4: XN_ATT1, 5: XN_GATE1}
        TR_LNS = [0, 2, 3, 5]

        @block.sync
        def _(sp):
            sp.dma_start(ctxp[:], io["ctxp"]).then_inc(ld["ctx"], 16)
            sp.dma_start(pk[0][:], io["pk0"]).then_inc(ld["pk0"], 16)
            sp.dma_start(dtw[0][:], io["dtw0"]).then_inc(ld["pk0"], 16)
            sp.dma_start(skip[:], io["skip"]).then_inc(ld["pk0"], 16)
            sp.dma_start(X[:], xr).then_inc(ld["x"], 16)
            sp.dma_start(ident[:], io["ident"]).then_inc(ld["ident"], 16)
            sp.dma_start(WQKV0, io["wqkv0"]).then_inc(ld["wqkv0"], 16)
            sp.dma_start(cos0, io["cos0"]).then_inc(ld["rope0"], 16)
            sp.dma_start(sin0, io["sin0"]).then_inc(ld["rope0"], 16)
            sp.dma_start(identb[:], io["identb"]).then_inc(ld["masks"], 16)
            sp.dma_start(mask0[:], io["mask0"]).then_inc(ld["masks"], 16)
            sp.dma_start(mask1[:], io["mask1"]).then_inc(ld["masks"], 16)

            def load_bc(g):
                sp.wait_ge(s["bc_stored"], 16 * (g // DS + 1))
                if g >= SB_LOADS:
                    sp.wait_ge(s["dbu_ready"], g - SB_LOADS + 1)
                    who, count = c_step(g - SB_LOADS)
                    sp.wait_ge(s[who], count)
                src = bc_dram[g // DS, g % DS].rearrange("r t -> (r t)").partition_broadcast(P)
                sp.dma_start(BCb[g % SB_LOADS][:].rearrange("p r t -> p (r t)"), src).then_inc(ld_bc[g % SB_LOADS], 16)

            sp.dma_start(WO0, io["wo0"]).then_inc(ld["wo0"], 16)
            sp.wait_ge(s["delta_ready"], 1)
            sp.wait_ge(s["sp_exp"], 1)
            sp.wait_ge(s["nega_exp"], 1)
            sp.dma_start(pk[1][:], io["pk1"]).then_inc(ld["pk1"], 16)
            sp.dma_start(dtw[1][:], io["dtw1"]).then_inc(ld["pk1"], 16)
            sp.dma_start(WA[:, 0:HC * 2 * INTER], io["ffn"]).then_inc(ld["ffn"], 16)
            sp.dma_start(fsc[:, 0:2, :], io["fsc"]).then_inc(ld["ffn"], 16)
            sp.dma_start(dsc[:], io["dsc"]).then_inc(ld["ffn"], 16)
            for g in range(DS):
                load_bc(g)
            sp.wait_ge(s["o0_mm"], 2)
            sp.dma_start(WDN, io["wdn"]).then_inc(ld["wdn"], 16)
            sp.dma_start(rope1, io["rope1"]).then_inc(ld["rope1"], 16)
            sp.dma_start(gains, io["gains"]).then_inc(ld["rope1"], 16)
            sp.dma_start(WB[:], io["wqkv1"]).then_inc(ld["wqkv1"], 16)
            for g in range(DS, 2 * DS):
                load_bc(g)
            sp.wait_ge(s["job_mm"], 5 * B)
            sp.wait_ge(s["v_mm"], B)
            for i in range(2):
                sp.dma_start(WS[i], io["we"][E + i]).then_inc(ld["shared"], 16)
            sp.dma_start(WRT, io["wrt"]).then_inc(ld["route"], 16)
            sp.dma_start(BR, io["br"]).then_inc(ld["route"], 16)
            for e in range(WRING):
                sp.dma_start(WE[e], io["we"][e]).then_inc(ld_we[e], 16)
            sp.wait_ge(s["gate_stored"], 16)
            for e in range(WRING):
                sp.dma_start(GB[e], gate_dram[e].partition_broadcast(P)).then_inc(ld_gb[e], 16)
            with sp.Fori(1, E // WRING, 1) as i:
                for k in range(WRING):
                    sp.wait_ge(s["m_out"], WRING * i + (k - WRING + 3))
                    sp.dma_start(WE[k], io["we"][bass.ds(WRING * i + k, 1)].rearrange("a p n -> (a p) n")).then_inc(ld_we[k], 16)
                    sp.dma_start(GB[k], gate_dram[bass.ds(WRING * i + k, 1)].rearrange("a t -> (a t)").partition_broadcast(P)).then_inc(ld_gb[k], 16)
            for hf in range(2):
                sp.wait_ge(s["x_new"], XN_GATE1 + 1 + hf)
                sp.dma_start(outr[:, 4 * hf:4 * hf + 4, :], X[:, 4 * hf:4 * hf + 4, :]).then_inc(s["out_done"], 16)
            sp.wait_ge(s["out_done"], 32)

        @block.gpsimd
        def _(pool):
            gp = nc.gpsimd
            ch = Chain(pool, s["pool_chain"])
            gp.memset(mhalf[:], -0.5).then_inc(s["init"], 1)
            gp.memset(ones32[:], 1.0).then_inc(s["init"], 1)
            gp.memset(ones1[:], 1.0).then_inc(s["init"], 1)
            floor = float(np.exp(np.float32(-SOFTCAP)))
            gp.memset(PT0[0][:, :, 0, W0:S], floor).then_inc(s["pt0_fill"], 1)
            gp.memset(PT0[0][:, :, 1, 0:P], floor).then_inc(s["pt0_fill"], 1)
            pool.wait_ge(s["init"], 3)

            def ln_rstd(L, eps):
                pool.wait_ge(s["ln_mv"], NT * (L + 1))
                ch.link(gp.tensor_scalar(lnve[:], lnmv[:, :, 1], eps, None, ALU.add))
                gp.tensor_tensor(lnrs[:], lnve[:], mhalf[:], ALU.pow).then_inc(s["ln_rstd"], 1)

            def zero_cols(l):
                pool.wait_ge(s["delta_ready"], l + 1)
                for slot in range(2):
                    gp.memset(dA[slot][:].rearrange("p d (b s) -> p (d b) s", b=B)[:, :, 0:1], 0.0).then_inc(s["da_cols_zero"], 1)

            def ssm_step(l, n):
                g = DS * l + n
                h = hS[g % 2]
                cb = BCb[g % SB_LOADS][:, 1, :]
                if n in C_ON_DVE[l]:
                    pool.wait_ge(s["c_dve"], c_step(g)[1])
                else:
                    pool.wait_ge(s["scan_done"], g + 1)
                    pool.wait_ge(ld_bc[g % SB_LOADS], 16 * (g // SB_LOADS + 1))
                    gp.tensor_tensor(h[:], h[:], cb.unsqueeze(1).broadcast_to([P, DT, T]), ALU.mult).then_inc(s["c_pool"], 1)
                    pool.wait_ge(s["c_pool"], c_step(g)[1])
                if n == 0:
                    pool.wait_ge(s["delta_ready"], l + 1)
                if g:
                    pool.wait_ge(s["ssm_acc"], g)
                if True:
                    gp.tensor_tensor(ACC[:], ACC[:], h[:], ALU.add).then_inc(s["ssm_acc"], 1)

            ln_rstd(0, 1e-5)
            zero_cols(0)
            pool.wait_ge(s["rope0_done"], 1)
            gp.memset(PT0[1][:, :, 0, W0:S], floor).then_inc(s["pt0_fill"], 1)
            gp.memset(PT0[1][:, :, 1, 0:P], floor).then_inc(s["pt0_fill"], 1)
            for n in range(DS):
                ssm_step(0, n)
            pool.wait_ge(ld["wdn"], 16)
            pool.wait_ge(ld["ffn"], 48)
            for i in range(NI):
                m = mlen(i)
                gp.tensor_tensor(WDN[0:m, i, :], WDN[0:m, i, :], dsc[0:m, :], ALU.mult).then_inc(s["wdn_ready"], 1)
            ln_rstd(1, 1e-5)
            ln_rstd(2, 1e-5)
            pool.wait_ge(s["w1_mean"], 1)
            for c in range(HC):
                w = WB[:, c, 0:NQ1 + NK1].rearrange("p (h d) -> p h d", d=D1)
                gp.tensor_tensor(w, w, wmean[:, c, :].unsqueeze(2).broadcast_to([P, H1 + KV1, D1]), ALU.add).then_inc(s["w1_centered"], 1)
            zero_cols(1)
            step = iter(range(DS))
            for _ in range(SSM1_IN_FFN):
                ssm_step(1, next(step))
            ln_rstd(3, 1e-5)

            def job(j):
                pool.wait_ge(s["job_sum"], j + 1)
                ch.link(gp.tensor_scalar(jst[:, 1, :], jst[:, 0, :], 1.0 / D1, 1e-5, ALU.mult, ALU.add))
                gp.tensor_tensor(jst[:, 2, :], jst[:, 1, :], mhalf[:], ALU.pow).then_inc(s["job_rstd"], 1)
                pool.wait_ge(s["job_rot"], 3 * (j + 1))
                gp.tensor_tensor(JA, JA, JB, ALU.add).then_inc(s["job_add"], 1)

            left = DS - SSM1_IN_FFN
            for kind, a in ATT1_PLAN:
                if kind == "job" and a[1] > 0:
                    job(5 * a[0] + a[1] - 1)
                if kind == "ssm":
                    ssm_step(1, a)
            ln_rstd(4, 1e-5)
            ln_rstd(5, 1e-5)

        @block.scalar
        def _(act):
            sc = nc.scalar
            ch = Chain(act, s["act_chain"])

            def conv_tanh(l, d):
                act.wait_ge(s["conv_mm"], DT * l + d + 1)
                act.wait_ge(s["lw_ready"], l + 1)
                sc.activation(DEL[:, d, :], ps[:, 2 * d:2 * d + 2, :].rearrange("p a b -> p (a b)"), ACT.Tanh,
                              bias=cbh[:, d:d + 1], scale=0.5).then_inc(s["conv_tanh"], 1)

            def xdbl_copy(l):
                act.wait_ge(s["xdbl_mm"], 2 * l + 1)
                sc.copy(dA[0][0:DR, 0, :], ps[0:DR, 0:2, :].rearrange("p a b -> p (a b)")).then_inc(s["dt_low_copied"], 1)
                act.wait_ge(s["xdbl_mm"], 2 * l + 2)
                sc.copy(dA[1][0:2 * DS, 0, :], ps[0:2 * DS, 2:4, :].rearrange("p a b -> p (a b)")).then_inc(s["bc_copied"], 1)
                act.wait_ge(s["bc_copied"], l + 1)
                act.dma_start(bc_dram[l].rearrange("n r t -> (n r) t"), dA[1][0:2 * DS, 0, :]).then_inc(s["bc_stored"], 16)

            def softplus(l):
                for d in range(DT):
                    act.wait_ge(s["dtpre_mm"], DT * l + d + 1)
                    sc.activation(hS[0][:, d, :], ps[:, 2 * d:2 * d + 2, :].rearrange("p a b -> p (a b)"), ACT.Abs,
                                  bias=pk[l][:, PK_DB + d:PK_DB + d + 1]).then_inc(s["sp_abs"], 1)
                act.wait_ge(s["sp_abs"], DT * (l + 1))
                sc.activation(hS[0][:], hS[0][:], ACT.Exp, scale=-1.0).then_inc(s["sp_exp"], 1)
                act.wait_ge(s["bc_stored"], 16 * (l + 1))
                act.wait_ge(s["sp_exp"], l + 1)
                sc.activation(dA[1][:], hS[0][:], ACT.Ln, bias=1.0).then_inc(s["sp_ln"], 1)

            def neg_a(l):
                act.wait_ge(ld[f"pk{l}"], 48 - 16 * l)
                if l:
                    act.wait_ge(s["da_ready"], 2 * DS)
                sc.activation(negA[:], pk[l][:, PK_A:PK_A + DT * DS], ACT.Exp).then_inc(s["nega_exp"], 1)
                act.wait_ge(s["nega_exp"], l + 1)
                sc.mul(negA[:], negA[:], -1.0).then_inc(s["nega_ready"], 1)

            def ssm_step(l, n):
                g = DS * l + n
                if n == 0:
                    act.wait_ge(s["delta_ready"], l + 1)
                    act.wait_ge(s["nega_ready"], l + 1)
                    act.wait_ge(s["da_cols_zero"], 2 * (l + 1))
                if n >= 2:
                    act.wait_ge(s["scan_done"], g - 1)
                for d in range(DT):
                    o = bands(dA[g % 2][:, d, :])[:, :, 1:S]
                    sc.activation(o, bands(DEL[:, d, :])[:, :, 1:S], ACT.Exp,
                                  scale=negA[:, d * DS + n:d * DS + n + 1]).then_inc(s["da_ready"], 1)

            def ln_tr_copy(i):
                for hf in range(2):
                    act.wait_ge(s["ln_tr_mm"], 4 * i + 2 * hf + 1)
                    sc.copy(hT[:, 0, 512 * hf:512 * hf + 512], ps[:, 4 + 2 * hf, :]).then_inc(s["ln_tr_act"], 1)

            neg_a(0)
            for d in range(DT):
                conv_tanh(0, d)
            ln_tr_copy(0)
            xdbl_copy(0)
            softplus(0)
            for t in range(NT):
                act.wait_ge(s["qkv0_mm"], t + 1)
                sc.copy(Q0[:, t, :], ps[:, 4 + t % 4, 0:NQKV0]).then_inc(s["qkv0_copied"], 1)
            ssm_step(0, 0)
            ssm_step(0, 1)
            act.wait_ge(s["rope0_rot"], 1)
            sc.activation(SQ0, Q0.rearrange("p t n -> p (t n)"), ACT.Square).then_inc(s["rope0_sq"], 1)
            act.wait_ge(s["rope0_done"], 1)
            for g in range(KV0):
                c = H0 * D0 + D0 * g
                sc.copy(K40[:, :, g, :].rearrange("p t (r d) -> p t r d", d=D0),
                        Q0[:, :, c:c + D0].unsqueeze(2).broadcast_to([P, NT, 4, D0])).then_inc(s["k4_ready"], 1)
            for i in range(8):
                act.wait_ge(s["tr0_mm"], i + 1)
                g, part, hf = i // 4, (i // 2) % 2, i % 2
                dst = (qT0, kT0)[part][:, g, 512 * hf:512 * hf + 512]
                sc.copy(dst, ps[:, 4 + i % 4, :]).then_inc(s["tr0_copied"], 1)
            nstep = 2
            for u in range(B * KV0):
                act.wait_ge(s["s0_mm"], u + 1)
                if u:
                    act.wait_ge(s["s0_exp"], 2 * u)
                sc.activation(TH0, ps[:, 0:REP0, 0:W0 + P], ACT.Tanh, scale=SCORE0).then_inc(s["s0_tanh"], 1)
                act.wait_ge(s["s0_tanh"], u + 1)
                act.wait_ge(s["pt0_fill"], 4)
                if u >= 2:
                    act.wait_ge(s["pv0_mm"], u - 1)
                pt = PT0[u % 2]
                sc.activation(pt[:, :, 0, 0:W0], TH0[:, :, 0:W0], ACT.Exp, scale=SOFTCAP).then_inc(s["s0_exp"], 1)
                sc.activation(pt[:, :, 1, P:S], TH0[:, :, W0:W0 + P], ACT.Exp, scale=SOFTCAP).then_inc(s["s0_exp"], 1)
                for _ in range(2):
                    if nstep < DS:
                        ssm_step(0, nstep)
                        nstep += 1
            while nstep < DS:
                ssm_step(0, nstep)
                nstep += 1

            def gate_tanh(l):
                act.wait_ge(s["ln_h"], NT * (3 * l + 2))
                sc.activation(hT[:].rearrange("p a b -> p (a b)"), H[:].rearrange("p a b -> p (a b)"), ACT.Tanh,
                              scale=0.5).then_inc(s["gate_tanh"], 1)

            gate_tanh(0)
            neg_a(1)
            act.wait_ge(s["gate_y"], 2)
            for d in range(DT):
                conv_tanh(1, d)
            xdbl_copy(1)
            softplus(1)
            ln_tr_copy(1)
            step = iter(range(DS))
            for j in range(2 * NI):
                m = mlen(j // 2)
                act.wait_ge(s["f_mm"], j + 1)
                if j >= 2:
                    act.wait_ge(s["f_hid"], 2 * (j - 1))
                sc.activation(fth[j % 2][0:m, :], ps[0:m, 2 * (j % 2), :], ACT.Tanh,
                              scale=fsc[0:m, 2, j // 2:j // 2 + 1]).then_inc(s["f_tanh"], 1)
                if j in FFN_SSM_AT:
                    ssm_step(1, next(step))
            act.wait_ge(s["fd_mm"], 4)
            act.dma_start(WO1, io["wo1"]).then_inc(ld["wo1"], 16)
            ln_tr_copy(2)

            def job_sq(j):
                act.wait_ge(s["job_mm"], j + 1)
                if j:
                    act.wait_ge(s["job_sum"], j)
                sc.activation(SQ, ps[:, 0:2, :], ACT.Square).then_inc(s["job_sq"], 1)

            def job_copy(b, i):
                j = 5 * b + i
                if i == 0:
                    dst = KT[b % 2]
                else:
                    dst = QT[(4 * b + i - 1) % 2]
                for x in range(2):
                    act.wait_ge(s["job_tr_mm"], 2 * j + x + 1)
                    if i == 0 and b >= 2:
                        act.wait_ge(s["s1_mm"], H1 * (b - 1))
                    if i > 0 and 4 * b + i - 1 >= 2:
                        act.wait_ge(s["s1_mm"], 4 * (4 * b + i - 2))
                    sc.copy(dst[:, 2 * x:2 * x + 2, :].rearrange("p a b -> p (a b)"), ps[:, 2, :]).then_inc(s["job_tr_copied"], 1)

            def v_copy(b):
                act.wait_ge(s["v_mm"], b + 1)
                if b >= 2:
                    act.wait_ge(s["pv1_mm"], H1 * (b - 1))
                sc.copy(V1[b % 2], ps[:, 0:2, :]).then_inc(s["v_copied"], 1)

            def exp1(u):
                p = u % 2
                act.wait_ge(s["s1_max"], u + 1)
                if u >= 2:
                    act.wait_ge(s["pt1_mm"], u - 1)
                sc.activation(P1[p][:, 0:P], ps[:, 3 + p, 0:P], ACT.Exp, bias=nm1[:, p, 0:1],
                              accum_out=sum1[:, p, 0:1]).then_inc(s["s1_exp"], 1)
                sc.activation(P1[p][:, P:3 * P], ps[:, 3 + p, P:3 * P], ACT.Exp, bias=nm1[:, p, 1:2],
                              accum_out=sum1[:, p, 1:2]).then_inc(s["s1_exp"], 1)

            def pt_copy(u):
                act.wait_ge(s["pt1_mm"], u + 1)
                if u >= 2:
                    act.wait_ge(s["pv1_mm"], u - 1)
                sc.copy(PT1[u % 2], ps[:, 5, 0:3 * P]).then_inc(s["pt1_copied"], 1)

            def at_copy(u):
                act.wait_ge(s["pv1_mm"], u + 1)
                if u >= 2:
                    act.wait_ge(s["o1_mm"], u - 1)
                sc.copy(aT1[u % 2], ps[:, 6, 0:S]).then_inc(s["at1_copied"], 1)

            for kind, a in ATT1_PLAN:
                if kind == "job":
                    b, i = a
                    if i == 0:
                        v_copy(b)
                    else:
                        job_sq(5 * b + i - 1)
                elif kind == "jobtr":
                    job_copy(*a)
                elif kind == "exp":
                    exp1(a)
                elif kind == "pt":
                    pt_copy(a)
                elif kind == "at":
                    at_copy(a)
                elif kind == "ssm":
                    ssm_step(1, a)
            gate_tanh(1)
            ln_tr_copy(3)
            act.wait_ge(s["r_mm"], 1)
            sc.activation(rS.rearrange("p t e -> p (t e)"), ps[:, 0, 0:NT * E], ACT.Exp, scale=-1.0).then_inc(s["r_exp"], 1)

            def relu(x, p):
                sc.activation(MR[p], ps[:, 2 * p:2 * p + 2, :].rearrange("p a b -> p (a b)"), ACT.Relu).then_inc(s["m_relu"], 1)

            act.wait_ge(s["m_mm"], 1)
            relu(0, 1)
            act.wait_ge(s["m_mm"], 2)
            relu(1, 0)
            act.wait_ge(s["gt_mm"], 1)
            sc.copy(gT, ps[0:E, 2:4, :].rearrange("p a b -> p (a b)")).then_inc(s["gt_copied"], 1)
            act.wait_ge(s["gt_copied"], 1)
            act.dma_start(gate_dram, gT).then_inc(s["gate_stored"], 16)
            with act.Fori(0, E // WRING, 1) as i:
                for k in range(WRING):
                    act.wait_ge(s["m_mm"], WRING * i + (k + 3))
                    act.wait_ge(s["m_hid"], WRING * i + (k + 1))
                    relu(0, (k + 1) % 2)

        @block.vector
        def _(dve):
            v = nc.vector
            ch = Chain(dve, s["dve_chain"])

            def lw(l):
                dve.wait_ge(ld[f"pk{l}"], 48 - 16 * l)
                if l:
                    dve.wait_ge(s["conv_tanh"], DT)
                ch.step(v.tensor_scalar(cbh[:], pk[l][:, PK_CB:PK_CB + DT], 0.5, None, ALU.mult))
                w = pk[l][:, PK_IN:PK_IN + DI].unsqueeze(1).broadcast_to([P, DC, DI])
                ch.wait()
                v.tensor_tensor(LW[l], LW[l], w, ALU.mult).then_inc(s["lw_ready"], 1)

            def u_calc(l):
                for d in range(DT):
                    dve.wait_ge(s["conv_tanh"], DT * l + d + 1)
                    ch.link(v.tensor_scalar(DU[:, d, :], ps[:, 2 * d:2 * d + 2, :].rearrange("p a b -> p (a b)"),
                                            pk[l][:, PK_CB + d:PK_CB + d + 1], 0.5, ALU.add, ALU.mult))
                    v.scalar_tensor_tensor(U[:, d, :], DEL[:, d, :], 1.0, DU[:, d, :], ALU.add, ALU.mult).then_inc(s["u_ready"], 1)

            def delta_calc(l):
                for d in range(DT):
                    dve.wait_ge(s["sp_abs"], DT * l + d + 1)
                    ch.step(v.tensor_scalar(DEL[:, d, :], ps[:, 2 * d:2 * d + 2, :].rearrange("p a b -> p (a b)"),
                                            pk[l][:, PK_DB + d:PK_DB + d + 1], 0.0, ALU.add, ALU.max))
                dve.wait_ge(s["sp_exp"], l + 1)
                ch.link(v.tensor_scalar(hS[1][:], hS[0][:], 1.0, None, ALU.add))
                ch.link(v.scalar_tensor_tensor(hS[1][:].rearrange("p a b -> p (a b)"), hS[1][:].rearrange("p a b -> p (a b)"), -1.0,
                                               hS[0][:].rearrange("p a b -> p (a b)"), ALU.add, ALU.subtract))
                dve.wait_ge(s["sp_ln"], l + 1)
                ch.link(v.tensor_tensor(DEL[:], DEL[:], dA[1][:], ALU.add))
                ch.link(v.tensor_tensor(DEL[:], DEL[:], hS[1][:], ALU.subtract))
                ch.link(v.tensor_tensor(DU[:], DEL[:], U[:], ALU.mult))
                for d in range(DT):
                    last = v.tensor_scalar(ACC[:, d, :], U[:, d, :], skip[:, l, d:d + 1], None, ALU.mult)
                last.then_inc(s["delta_ready"], 1)

            def ssm_step(l, n):
                g = DS * l + n
                bcb, h, a = BCb[g % SB_LOADS], hS[g % 2], dA[g % 2]
                dve.wait_ge(ld_bc[g % SB_LOADS], 16 * (g // SB_LOADS + 1))
                if n == 0:
                    dve.wait_ge(s["delta_ready"], l + 1)
                if g >= 2:
                    dve.wait_ge(s["ssm_acc"], g - 1)
                v.tensor_tensor(h[:], DU[:], bcb[:, 0:1, :].broadcast_to([P, DT, T]), ALU.mult).then_inc(s["dbu_ready"], 1)
                dve.wait_ge(s["dbu_ready"], g + 1)
                dve.wait_ge(s["da_ready"], 2 * (g + 1))
                f = lambda z: z[:].rearrange("p d t -> p (d t)")
                v.tensor_tensor_scan(f(h), f(a), f(h), 0.0, ALU.mult, ALU.add).then_inc(s["scan_done"], 1)
                if n in C_ON_DVE[l]:
                    dve.wait_ge(s["scan_done"], g + 1)
                    v.tensor_tensor(h[:], h[:], bcb[:, 1:2, :].broadcast_to([P, DT, T]), ALU.mult).then_inc(s["c_dve"], 1)

            def ln_stats(L):
                for t in range(NT):
                    if L == 0:
                        dve.wait_ge(ld["x"], 16)
                    elif L == 4:
                        dve.wait_ge(s["x_new"], XN_FFN + t // 2 + 1)
                    else:
                        dve.wait_ge(s["x_new"], XN[L] - 1 + t // 4)
                    ch.step(v.bn_stats(lnst[:, t, :], X[:, t, :]))
                base = ch.n - NT
                for t in range(NT):
                    ch.wait(base + t + 1)
                    v.bn_aggr(lnmv[:, t, :], lnst[:, t, :]).then_inc(s["ln_mv"], 1)

            def ln_apply(L):
                dve.wait_ge(s["ln_rstd"], L + 1)
                for t in range(NT):
                    v.tensor_scalar(H[:, t, :], X[:, t, :], lnmv[:, t, 0:1], lnrs[:, t:t + 1], ALU.subtract,
                                    ALU.mult).then_inc(s["ln_h"], 1)

            def ln_tr_copy(i):
                for hf in range(2):
                    dve.wait_ge(s["ln_tr_mm"], 4 * i + 2 * hf + 2)
                    v.tensor_copy(hT[:, 1, 512 * hf:512 * hf + 512], ps[:, 5 + 2 * hf, :]).then_inc(s["ln_tr_dve"], 1)

            def residual(bank0, ready, counts):
                for hf in range(2):
                    dve.wait_ge(s[ready], counts[hf])
                    x = X[:, 4 * hf:4 * hf + 4, :].rearrange("p t d -> p (t d)")
                    v.tensor_tensor(x, x, ps[:, bank0 + 2 * hf:bank0 + 2 * hf + 2, :].rearrange("p a b -> p (a b)"),
                                    ALU.add).then_inc(s["x_new"], 1)

            lw(0)
            ln_stats(0)
            u_calc(0)
            ln_apply(0)
            ln_tr_copy(0)
            delta_calc(0)

            dve.wait_ge(s["qkv0_copied"], NT)
            dve.wait_ge(ld["rope0"], 32)
            qk = Q0[:, :, 0:NQK0]
            tb = lambda a: a.rearrange("p (b h) n -> p b h n", h=2)
            ch.step(v.tensor_tensor(tb(RA), tb(qk), cos0.unsqueeze(1).broadcast_to([P, B, 2, NQK0]), ALU.mult))
            for hf in range(2):
                for x in range(2):
                    pick = lambda a, y: tb(a)[:, :, hf, :].rearrange("p b (n d) -> p b n d", d=D0)[:, :, :, 16 * y:16 * y + 16]
                    sn = sin0[:, hf, :].rearrange("p (n d) -> p n d", d=D0)[:, :, 16 * x:16 * x + 16]
                    ch.step(v.tensor_tensor(pick(RB, x), pick(qk, 1 - x), sn.unsqueeze(1).broadcast_to([P, B, H0 + KV0, 16]), ALU.mult))
            ch.wait()
            ch.link(v.tensor_tensor(qk, RA, RB, ALU.add))
            nh = NT * NQKV0 // D0
            q3 = Q0.rearrange("p t (n d) -> p (t n) d", d=D0)
            wide = lambda a: a.unsqueeze(2).broadcast_to([P, nh, D0])
            ch.link(v.tensor_reduce(st0[:, 0, :], q3, AX.X, ALU.add))
            ch.link(v.tensor_scalar(st0[:, 0, :], st0[:, 0, :], 1.0 / D0, None, ALU.mult))
            v.tensor_tensor(q3, q3, wide(st0[:, 0, :]), ALU.subtract).then_inc(s["rope0_rot"], 1)
            dve.wait_ge(s["rope0_sq"], 1)
            ch.link(v.tensor_reduce(st0[:, 1, :], SQ0.rearrange("p (n d) -> p n d", d=D0), AX.X, ALU.add))
            ch.link(v.tensor_scalar(st0[:, 1, :], st0[:, 1, :], 1.0 / D0, 1e-6, ALU.mult, ALU.add))
            ch.link(v.tensor_single_scalar(st0[:, 2, :].bitcast(I32), st0[:, 1, :].bitcast(I32), 1, ALU.arith_shift_right))
            ch.link(v.tensor_scalar(st0[:, 2, :].bitcast(I32), st0[:, 2, :].bitcast(I32), -1.0, float(0x5F3759DF), ALU.mult, ALU.add))
            for _ in range(4):
                ch.link(v.tensor_tensor(st0[:, 3, :], st0[:, 2, :], st0[:, 2, :], ALU.mult))
                ch.link(v.scalar_tensor_tensor(st0[:, 3, :], st0[:, 3, :], -0.5, st0[:, 1, :], ALU.mult, ALU.mult))
                ch.link(v.scalar_tensor_tensor(st0[:, 2, :], st0[:, 3, :], 1.5, st0[:, 2, :], ALU.add, ALU.mult))
            v.tensor_tensor(q3, q3, wide(st0[:, 2, :]), ALU.mult).then_inc(s["rope0_done"], 1)

            def at0(u):
                b, g = u // KV0, u % KV0
                dve.wait_ge(s["pv0_mm"], u + 1)
                ch.link(v.reciprocal(rden0, ps[:, 5, 0:S]))
                v.tensor_tensor(aT0[:, g, S * b:S * b + S], ps[:, 4, 0:S], rden0, ALU.mult).then_inc(s["at0_ready"], 1)

            for n in range(DS):
                ssm_step(0, n)
                if n % 2 == 1:
                    at0(n // 2)
            residual(0, "o0_mm", (1, 2))

            def gate(l):
                ln_stats(1 + 3 * l)
                dve.wait_ge(s["ssm_acc"], DS * (l + 1))
                ln_apply(1 + 3 * l)
                dve.wait_ge(s["gate_tanh"], l + 1)
                flat = H[:].rearrange("p a b -> p (a b)")
                ch.link(v.scalar_tensor_tensor(flat, hT[:].rearrange("p a b -> p (a b)"), 1.0, flat, ALU.add, ALU.mult))
                for d in range(DT):
                    gt = H[:].rearrange("p (b h) n -> p b h n", h=2)[:, :, d, :]
                    a = bands(ACC[:, d, :])
                    v.scalar_tensor_tensor(a, a, 0.5, gt, ALU.mult, ALU.mult).then_inc(s["gate_y"], 1)

            gate(0)
            lw(1)
            dve.wait_ge(s["gate_mm"], 2)
            u_calc(1)
            residual(4, "gate_mm", (1, 2))
            ln_stats(2)
            dve.wait_ge(ld["ffn"], 48)
            ch.link(v.tensor_scalar(fsc[:, 2, :], fsc[:, 0, :], 0.5, None, ALU.mult))
            ch.step(v.tensor_tensor(fsc[:, 1, :], fsc[:, 1, :], fsc[:, 2, :], ALU.mult))
            dve.wait_ge(s["ln_rstd"], 3)
            ln_apply(2)
            delta_calc(1)
            ln_tr_copy(1)
            dve.wait_ge(ld["wqkv1"], 16)
            for c in range(HC):
                ch.step(v.tensor_reduce(wmean[:, c, :], WB[:, c, 0:NQ1 + NK1].rearrange("p (h d) -> p h d", d=D1), AX.X, ALU.add))
            ch.wait()
            v.tensor_scalar(wmean[:], wmean[:], -1.0 / D1, None, ALU.mult).then_inc(s["w1_mean"], 1)
            step = iter(range(DS))
            for j in range(2 * NI):
                m, i, hf = mlen(j // 2), j // 2, j % 2
                dve.wait_ge(s["f_tanh"], j + 1)
                v.scalar_tensor_tensor(ft1[j % 2][0:m, :], fth[j % 2][0:m, :], 1.0, ps[0:m, 2 * (j % 2), :], ALU.add,
                                       ALU.mult).then_inc(s["f_hid"], 1)
                dve.wait_ge(s["f_hid"], 2 * j + 1)
                v.scalar_tensor_tensor(hid0[0:m, i, 512 * hf:512 * hf + 512], ps[0:m, 2 * (j % 2) + 1, :], fsc[0:m, 1, i:i + 1],
                                       ft1[j % 2][0:m, :], ALU.mult, ALU.mult).then_inc(s["f_hid"], 1)
                if j in FFN_SSM_AT:
                    ssm_step(1, next(step))
            residual(4, "fd_mm", (2, 4))
            ln_stats(3)
            dve.wait_ge(ld["rope1"], 32)
            for x in range(2):
                row = lambda i: gains[:, 4 * x + i, :].unsqueeze(1).broadcast_to([P, 2, D1])
                cs, sn = rope1[:, 2 * x, :, :], rope1[:, 2 * x + 1, :, :]
                t = lambda i: tabs[:, 3 * x + i, :, :]
                ch.step(v.tensor_tensor(t(0), cs, row(0), ALU.mult))
                ch.step(v.tensor_tensor(t(1), sn, row(2), ALU.mult))
                ch.step(v.tensor_tensor(t(2), cs, row(1), ALU.mult))
                ch.link(v.tensor_tensor(sn, sn, row(3), ALU.mult))
                ch.link(v.tensor_tensor(t(2), t(2), sn, ALU.add))
            ln_apply(3)
            ln_tr_copy(2)

            def job(b, i):
                j, x = 5 * b + i, 0 if i else 1
                pj = ps[:, 0:2, :].rearrange("p t (h d) -> p t h d", d=D1)
                bc = lambda a: a.unsqueeze(2).broadcast_to([P, 2, REP1, a.shape[-1]])
                h4 = lambda a: a.rearrange("p t (h d) -> p t h d", d=D1)
                dve.wait_ge(s["job_sq"], j + 1)
                if j:
                    dve.wait_ge(s["job_rope"], 8 * j)
                hd = D1 // 2
                v.tensor_tensor(h4(JA), pj, bc(tabs[:, 3 * x, :, :]), ALU.mult).then_inc(s["job_rot"], 1)
                for y in range(2):
                    v.tensor_tensor(h4(JB)[:, :, :, hd * y:hd * y + hd], pj[:, :, :, hd * (1 - y):hd * (1 - y) + hd],
                                    bc(tabs[:, 3 * x + 1, :, hd * y:hd * y + hd]), ALU.mult).then_inc(s["job_rot"], 1)
                if j:
                    dve.wait_ge(s["job_rstd"], j)
                v.tensor_reduce(jst[:, 0, :], SQ.rearrange("p t (h d) -> p (t h) d", d=D1), AX.X, ALU.add).then_inc(s["job_sum"], 1)

            def job_rope(b, i):
                j, x = 5 * b + i, 0 if i else 1
                dve.wait_ge(s["job_add"], j + 1)
                dve.wait_ge(s["job_rstd"], j + 1)
                if j:
                    dve.wait_ge(s["job_tr_mm"], 2 * j)
                for t in range(2):
                    for h in range(REP1):
                        c = slice(D1 * h, D1 * h + D1)
                        v.scalar_tensor_tensor(R[:, t, c], JA[:, t, c], jst[:, 2, REP1 * t + h:REP1 * t + h + 1],
                                               tabs[:, 3 * x + 2, t, :], ALU.mult, ALU.add).then_inc(s["job_rope"], 1)

            def max1(u):
                p = u % 2
                dve.wait_ge(s["s1_mm"], u + 1)
                if u >= 2:
                    dve.wait_ge(s["s1_exp"], 2 * (u - 1))
                ch.step(v.tensor_reduce(nm1[:, p, 0:1], ps[:, 3 + p, 0:P], AX.X, ALU.max, negate=True))
                v.tensor_reduce(nm1[:, p, 1:2], ps[:, 3 + p, P:3 * P], AX.X, ALU.max, negate=True).then_inc(s["s1_max"], 1)

            def norm1(u):
                p = u % 2
                dve.wait_ge(s["s1_exp"], 2 * (u + 1))
                ch.link(v.reciprocal(rc1[:, p, :], sum1[:, p, :]))
                v.tensor_scalar(P1[p][:, 0:P], P1[p][:, 0:P], rc1[:, p, 0:1], None, ALU.mult).then_inc(s["s1_norm"], 1)
                v.tensor_scalar(P1[p][:, P:3 * P], P1[p][:, P:3 * P], rc1[:, p, 1:2], None, ALU.mult).then_inc(s["s1_norm"], 1)

            for kind, a in ATT1_PLAN:
                if kind == "job" and a[1] > 0:
                    job(a[0], a[1] - 1)
                elif kind == "rope":
                    job_rope(*a)
                elif kind == "exp":
                    max1(a)
                elif kind == "norm":
                    norm1(a)
                elif kind == "ssm":
                    ssm_step(1, a)
                elif kind == "res":
                    dve.wait_ge(s["o1_mm"], H1 * (a + 1))
                    x = X[:, 2 * a:2 * a + 2, :].rearrange("p t d -> p (t d)")
                    v.tensor_tensor(x, x, ps[:, 7, :], ALU.add).then_inc(s["x_new"], 1)
            gate(1)
            residual(4, "gate_mm", (3, 4))
            ln_stats(5)
            ln_apply(5)
            ln_tr_copy(3)

            def shared_hidden(x, p):
                dve.wait_ge(s["m_relu"], x + 1)
                f = ps[:, 2 * p:2 * p + 2, :].rearrange("p a b -> p (a b)")
                v.scalar_tensor_tensor(MH[p], f, 0.0, MR[p], ALU.max, ALU.mult).then_inc(s["m_hid"], 1)

            dve.wait_ge(s["r_exp"], 1)
            for z in (rGW, rMS, rT8, rE8):
                ch.step(v.memset(z, -1.0))
            ch.link(v.tensor_scalar(rS, rS, 1.0, None, ALU.add))
            ch.link(v.reciprocal(rS, rS))
            q4 = rS.rearrange("p t (g e) -> p (t g) e", e=EPG)
            col = lambda i: q4[:, :, i]
            ch.step(v.tensor_tensor(rg[0], col(0), col(1), ALU.max))
            ch.step(v.tensor_tensor(rg[1], col(0), col(1), ALU.min))
            ch.step(v.tensor_tensor(rg[2], col(2), col(3), ALU.max))
            ch.link(v.tensor_tensor(rg[3], col(2), col(3), ALU.min))
            ch.step(v.tensor_tensor(rg[4], rg[0], rg[2], ALU.max))
            ch.step(v.tensor_tensor(rg[5], rg[0], rg[2], ALU.min))
            ch.link(v.tensor_tensor(rg[1], rg[1], rg[3], ALU.max))
            ch.link(v.tensor_tensor(rg[1], rg[1], rg[5], ALU.max))
            ch.link(v.tensor_tensor(rGW[:, :, 0:G], rg[4].rearrange("p (t g) -> p t g", g=G),
                                    rg[1].rearrange("p (t g) -> p t g", g=G), ALU.add))
            for t in range(NT):
                ch.step(v.max(rM8[:, t, :], rGW[:, t, 0:G]))
            ch.wait()
            ch.link(v.tensor_copy(rT8[:, :, 0:KG], rM8[:, :, 0:KG]))
            for t in range(NT):
                ch.step(v.match_replace(rGM[:, t, :], rT8[:, t, :], rGW[:, t, :], -2.0))
            ch.wait()
            ch.link(v.tensor_scalar(rGM, rGM, -2.0, None, ALU.is_equal))
            ch.link(v.tensor_tensor(rW.rearrange("p t (g e) -> p t g e", e=EPG), rS.rearrange("p t (g e) -> p t g e", e=EPG),
                                    rGM[:, :, 0:G].unsqueeze(3).broadcast_to([P, NT, G, EPG]), ALU.mult))
            ch.link(v.tensor_copy(rMS[:, :, 0:E], rW))
            for t in range(NT):
                ch.step(v.max(rM8[:, t, :], rMS[:, t, 0:E]))
            ch.wait()
            ch.link(v.tensor_copy(rE8[:, :, 0:K], rM8[:, :, 0:K]))
            for t in range(NT):
                ch.step(v.match_replace(rME[:, t, :], rE8[:, t, :], rMS[:, t, :], -2.0))
            ch.wait()
            ch.link(v.tensor_scalar(rME, rME, -2.0, None, ALU.is_equal))
            ch.link(v.tensor_tensor(rW, rS, rME[:, :, 0:E], ALU.mult))
            ch.link(v.tensor_reduce(rsum[:, 0, :], rW, AX.X, ALU.add))
            ch.link(v.tensor_scalar(rsum[:, 0, :], rsum[:, 0, :], 1e-20, None, ALU.add))
            ch.link(v.reciprocal(rsum[:, 1, :], rsum[:, 0, :]))
            ch.link(v.tensor_tensor(rW, rW, rsum[:, 1, :].unsqueeze(2).broadcast_to([P, NT, E]), ALU.mult))
            v.tensor_scalar(rGate, rW, ROUTE_SCALE, None, ALU.mult).then_inc(s["r_gate"], 1)
            shared_hidden(0, 1)
            shared_hidden(1, 0)
            with dve.Fori(0, E // WRING, 1) as i:
                for k in range(WRING):
                    p = (k + 1) % 2
                    f = ps[:, 2 * p:2 * p + 2, :].rearrange("p a b -> p (a b)")
                    dve.wait_ge(ld_gb[k], 16 * i + 16)
                    dve.wait_ge(s["m_relu"], WRING * i + (k + 3))
                    v.scalar_tensor_tensor(MG[p], f, 0.0, GB[k], ALU.max, ALU.mult).then_inc(s["m_gated"], 1)
                    dve.wait_ge(s["m_gated"], WRING * i + (k + 1))
                    dve.wait_ge(s["m_out"], WRING * i + (k + 1))
                    v.tensor_tensor(MH[p], MG[p], MR[p], ALU.mult).then_inc(s["m_hid"], 1)
            residual(4, "m_out", (E + 2, E + 2))

        @block.tensor
        def _(pe):
            mm, tr = nc.tensor.matmul, nc.tensor.transpose

            def conv(l):
                pe.wait_ge(s["lw_ready"], l + 1)
                pe.wait_ge(ld["ctx"], 16)
                for d in range(DT):
                    for hf in range(2):
                        for k in range(DC):
                            last = mm(ps[:, 2 * d + hf, :], LW[l][:, k, P * d:P * d + P], ctxp[:, 2 * hf:2 * hf + 2, k:k + S],
                                      start=(k == 0), stop=(k == DC - 1))
                    last.then_inc(s["conv_mm"], 1)

            def xdbl(l):
                pe.wait_ge(s["u_ready"], DT * (l + 1))
                xp = pk[l][:, PK_X:PK_N].rearrange("p (d n) -> p d n", d=DT)
                for bank, c0, n in ((0, 0, DR), (2, DR, 2 * DS)):
                    for hf in range(2):
                        for d in range(DT):
                            last = mm(ps[0:n, bank + hf, :], xp[:, d, c0:c0 + n], U[:, d, 512 * hf:512 * hf + 512],
                                      start=(d == 0), stop=(d == DT - 1))
                    last.then_inc(s["xdbl_mm"], 1)

            def dtpre(l):
                pe.wait_ge(s["dt_low_copied"], l + 1)
                pe.wait_ge(s["bc_copied"], l + 1)
                for d in range(DT):
                    for hf in range(2):
                        last = mm(ps[:, 2 * d + hf, :], dtw[l][:, P * d:P * d + P], dA[0][0:DR, 0, 512 * hf:512 * hf + 512],
                                  start=True, stop=True)
                    last.then_inc(s["dtpre_mm"], 1)

            def ln_tr(i):
                L = TR_LNS[i]
                for hf in range(2):
                    pe.wait_ge(s["ln_h"], NT * L + 4 * hf + 4)
                    for c in range(HC):
                        for t in range(4):
                            last = tr(ps[:, 4 + 2 * hf + c, P * t:P * t + P], H[:, 4 * hf + t, P * c:P * c + P], ident[:])
                        last.then_inc(s["ln_tr_mm"], 1)

            def ln_ready(i, hf):
                pe.wait_ge(s["ln_tr_act"], 2 * i + hf + 1)
                pe.wait_ge(s["ln_tr_dve"], 2 * i + hf + 1)

            conv(0)
            pe.wait_ge(ld["ident"], 16)
            ln_tr(0)
            xdbl(0)
            pe.wait_ge(ld["wqkv0"], 16)
            dtpre(0)
            for t in range(NT):
                ln_ready(0, 1)
                if t >= 4:
                    pe.wait_ge(s["qkv0_copied"], t - 3)
                for c in range(HC):
                    last = mm(ps[:, 4 + t % 4, 0:NQKV0], hT[:, c, P * t:P * t + P], WQKV0[:, c, :], start=(c == 0), stop=(c == HC - 1))
                last.then_inc(s["qkv0_mm"], 1)
            pe.wait_ge(s["rope0_done"], 1)
            for i in range(8):
                g, part, hf = i // 4, (i // 2) % 2, i % 2
                pe.wait_ge(s["tr0_copied"], i - 3) if i >= 4 else pe.wait_ge(s["qkv0_copied"], NT)
                for t in range(4):
                    tile = Q0[:, 4 * hf + t, :]
                    if part == 0:
                        src = tile[:, P * g:P * g + P]
                    else:
                        pe.wait_ge(s["k4_ready"], g + 1)
                        src = K40[:, 4 * hf + t, g, :]
                    last = tr(ps[:, 4 + i % 4, P * t:P * t + P], src, ident[:])
                last.then_inc(s["tr0_mm"], 1)
            pe.wait_ge(ld["masks"], 48)
            pe.wait_ge(s["delta_ready"], 1)

            def s0(u):
                b, g = u // KV0, u % KV0
                pe.wait_ge(s["tr0_copied"], 4 * g + 4)
                if u:
                    pe.wait_ge(s["s0_tanh"], u)
                q0 = S * b
                for r in range(REP0):
                    rows = slice(D0 * r, D0 * r + D0)
                    mm(ps[:, r, 0:W0 + P], identb[:], mask0[:], start=True, stop=True, skip_group_check=True)
                    mm(ps[:, r, 0:W0], kT0[rows, g, q0:q0 + P], qT0[rows, g, q0:q0 + W0], start=False, stop=True, skip_group_check=True)
                    last = mm(ps[:, r, W0:W0 + P], kT0[rows, g, q0 + P:q0 + S], qT0[rows, g, q0 + P:q0 + S], start=False, stop=True,
                              skip_group_check=True)
                last.then_inc(s["s0_mm"], 1)

            def pv0(u):
                b, g = u // KV0, u % KV0
                pe.wait_ge(s["s0_exp"], 2 * (u + 1))
                pe.wait_ge(s["init"], 3)
                pe.wait_ge(s["at0_ready"], u) if u else pe.wait_ge(s["tr0_copied"], 8)
                vc = NQK0 + D0 * g
                for r in range(REP0):
                    for kb_ in range(2):
                        w = PT0[u % 2][:, r, kb_, :]
                        mm(ps[D0 * r:D0 * r + D0, 4, 0:S], Q0[:, 2 * b + kb_, vc:vc + D0], w, start=(kb_ == 0), stop=(kb_ == 1))
                        last = mm(ps[D0 * r:D0 * r + D0, 5, 0:S], ones32[:], w, start=(kb_ == 0), stop=(kb_ == 1))
                last.then_inc(s["pv0_mm"], 1)

            s0(0)
            for u in range(B * KV0):
                if u + 1 < B * KV0:
                    s0(u + 1)
                pv0(u)
            pe.wait_ge(ld["wo0"], 16)
            pe.wait_ge(s["s0_tanh"], B * KV0)
            pe.wait_ge(s["at0_ready"], B * KV0)
            for t in range(NT):
                for g in range(KV0):
                    last = mm(ps[:, t // 2, 256 * (t % 2):256 * (t % 2) + 256], aT0[:, g, P * t:P * t + P], WO0[:, g, :],
                              start=(g == 0), stop=(g == KV0 - 1))
                if t % 4 == 3:
                    last.then_inc(s["o0_mm"], 1)

            def gate_tr(l):
                pe.wait_ge(s["gate_y"], DT * (l + 1))
                for t in range(NT):
                    for d in range(DT):
                        last = tr(ps[:, 4 + t // 2, 256 * (t % 2) + P * d:256 * (t % 2) + P * d + P], ACC[:, d, P * t:P * t + P], ident[:])
                    if t % 4 == 3:
                        last.then_inc(s["gate_mm"], 1)

            pe.wait_ge(s["x_new"], XN_ATT0)
            conv(1)
            gate_tr(0)
            xdbl(1)
            dtpre(1)
            pe.wait_ge(s["x_new"], XN_GATE0)
            ln_tr(1)
            pe.wait_ge(s["delta_ready"], 2)
            ln_ready(1, 1)
            pe.wait_ge(ld["ffn"], 48)
            for j in range(2 * NI):
                m, i, hf = mlen(j // 2), j // 2, j % 2
                if j >= 2:
                    pe.wait_ge(s["f_hid"], 2 * (j - 1))
                for x in range(2):
                    for c in range(HC):
                        last = mm(ps[0:m, 2 * (j % 2) + x, :], WGU[:, c, INTER * x + P * i:INTER * x + P * i + m],
                                  hT[:, c, 512 * hf:512 * hf + 512], start=(c == 0), stop=(c == HC - 1))
                last.then_inc(s["f_mm"], 1)
            pe.wait_ge(s["f_hid"], 4 * NI)
            pe.wait_ge(s["wdn_ready"], NI)
            for t in range(NT):
                for i in range(NI):
                    m = mlen(i)
                    last = mm(ps[:, 4 + t // 2, 256 * (t % 2):256 * (t % 2) + 256], hid0[0:m, i, P * t:P * t + P], WDN[0:m, i, :],
                              start=(i == 0), stop=(i == NI - 1))
                if t % 2 == 1:
                    last.then_inc(s["fd_mm"], 1)
            pe.wait_ge(s["x_new"], XN_FFN)
            ln_tr(2)
            ln_ready(2, 1)
            pe.wait_ge(s["w1_centered"], HC)

            def project(b, c0):
                for t in range(2):
                    for c in range(HC):
                        last = mm(ps[:, t, :], hT[:, c, P * (2 * b + t):P * (2 * b + t) + P], WB[:, c, c0:c0 + 512],
                                  start=(c == 0), stop=(c == HC - 1))
                return last

            def v_job(b):
                if b:
                    pe.wait_ge(s["job_rot"], 3 * 5 * b)
                project(b, NQ1 + NK1).then_inc(s["v_mm"], 1)

            def rope_job(b, i):
                j = 5 * b + i
                if i == 0:
                    pe.wait_ge(s["v_copied"], b + 1)
                else:
                    pe.wait_ge(s["job_rot"], 3 * j)
                    pe.wait_ge(s["job_sq"], j)
                project(b, NQ1 if i == 0 else NK1 * (i - 1)).then_inc(s["job_mm"], 1)

            def job_tr(b, i):
                j = 5 * b + i
                pe.wait_ge(s["job_rope"], 8 * (j + 1))
                for x in range(2):
                    if j or x:
                        pe.wait_ge(s["job_tr_copied"], 2 * j + x)
                    for h in range(2):
                        for t in range(2):
                            last = tr(ps[:, 2, S * h + P * t:S * h + P * t + P], R[:, t, D1 * (2 * x + h):D1 * (2 * x + h) + D1], ident[:])
                    last.then_inc(s["job_tr_mm"], 1)

            def s1(u):
                b, h = u // H1, u % H1
                g, p = h // REP1, u % 2
                pe.wait_ge(s["job_tr_copied"], 2 * (5 * b + 1 + g) + 2)
                if u >= 2:
                    pe.wait_ge(s["s1_exp"], 2 * (u - 1))
                q, k = QT[(4 * b + g) % 2], KT[b % 2]
                mm(ps[:, 3 + p, 0:3 * P], identb[:], mask1[:], start=True, stop=True, skip_group_check=True)
                mm(ps[:, 3 + p, 0:P], q[:, h % REP1, 0:P], k[:, g, 0:P], start=False, stop=True, skip_group_check=True)
                mm(ps[:, 3 + p, P:3 * P], q[:, h % REP1, P:S], k[:, g, :], start=False, stop=True, skip_group_check=True).then_inc(s["s1_mm"], 1)

            def pt1(u):
                pe.wait_ge(s["s1_norm"], 2 * (u + 1))
                if u:
                    pe.wait_ge(s["pt1_copied"], u)
                for x in range(3):
                    last = tr(ps[:, 5, P * x:P * x + P], P1[u % 2][:, P * x:P * x + P], ident[:])
                last.then_inc(s["pt1_mm"], 1)

            def pv1(u):
                b, h = u // H1, u % H1
                g = h // REP1
                pe.wait_ge(s["pt1_copied"], u + 1)
                pe.wait_ge(s["v_copied"], b + 1)
                if u:
                    pe.wait_ge(s["at1_copied"], u)
                va = V1[b % 2]
                mm(ps[:, 6, 0:S], va[:, 0, D1 * g:D1 * g + D1], PT1[u % 2][:, 0:S], start=True, stop=True, skip_group_check=True)
                mm(ps[:, 6, P:S], va[:, 1, D1 * g:D1 * g + D1], PT1[u % 2][:, S:3 * P], start=False, stop=True,
                   skip_group_check=True).then_inc(s["pv1_mm"], 1)

            def o1(u):
                b, h = u // H1, u % H1
                pe.wait_ge(s["at1_copied"], u + 1)
                if u == 0:
                    pe.wait_ge(ld["wo1"], 16)
                if h == 0 and b:
                    pe.wait_ge(s["x_new"], XN_FFN + b)
                for t in range(2):
                    last = mm(ps[:, 7, 256 * t:256 * t + 256], aT1[u % 2][:, P * t:P * t + P], WO1[:, h, :], start=(h == 0 and t == 0),
                              stop=(h == H1 - 1), skip_group_check=True)
                last.then_inc(s["o1_mm"], 1)

            for kind, a in ATT1_PLAN:
                if kind == "job":
                    v_job(a[0]) if a[1] == 0 else rope_job(a[0], a[1] - 1)
                elif kind == "jobtr":
                    job_tr(*a)
                elif kind == "exp":
                    s1(a)
                elif kind == "norm":
                    pt1(a)
                elif kind == "pv":
                    pv1(a)
                elif kind == "o":
                    o1(a)
            pe.wait_ge(s["x_new"], XN_ATT1)
            gate_tr(1)
            pe.wait_ge(s["x_new"], XN_GATE1)
            ln_tr(3)
            pe.wait_ge(ld["route"], 32)
            pe.wait_ge(s["init"], 3)
            ln_ready(3, 1)
            for t in range(NT):
                o = ps[:, 0, E * t:E * t + E]
                mm(o, ones1[:], BR, start=True, stop=False)
                for c in range(HC):
                    last = mm(o, hT[:, c, P * t:P * t + P], WRT[:, c, :], start=False, stop=(c == HC - 1))
            last.then_inc(s["r_mm"], 1)

            def w1(p, w):
                for hf in range(2):
                    for c in range(HC):
                        last = mm(ps[:, 2 * p + hf, :], w[:, M * c:M * c + M], hT[:, c, 512 * hf:512 * hf + 512],
                                  start=(c == 0), stop=(c == HC - 1))
                last.then_inc(s["m_mm"], 1)

            def w2(p, w, first=False, final=False):
                for t in range(NT):
                    last = mm(ps[:, 4 + t // 2, 256 * (t % 2):256 * (t % 2) + 256], MH[p][:, P * t:P * t + P], w[:, HC * M:HC * M + HID],
                              start=(first and t % 2 == 0), stop=final, skip_group_check=True)
                last.then_inc(s["m_out"], 1)

            pe.wait_ge(ld["shared"], 32)
            w1(1, WS[0])
            pe.wait_ge(s["r_exp"], 1)
            w1(0, WS[1])
            pe.wait_ge(s["r_gate"], 1)
            pe.wait_ge(s["m_hid"], 1)
            for t in range(NT):
                last = tr(ps[0:E, 2 + t // 4, P * (t % 4):P * (t % 4) + P], rGate[:, t, :], ident[:])
            last.then_inc(s["gt_mm"], 1)
            w2(1, WS[0], first=True)
            pe.wait_ge(s["gt_copied"], 1)
            pe.wait_ge(ld_we[0], 16)
            w1(1, WE[0])
            pe.wait_ge(s["m_hid"], 2)
            w2(0, WS[1])
            with pe.Fori(0, E // WRING - 1, 1) as i:
                for k in range(WRING):
                    p = (k + 1) % 2
                    kn = (k + 1) % WRING
                    pe.wait_ge(ld_we[kn], 16 * i + (16 if kn else 32))
                    pe.wait_ge(s["m_hid"], WRING * i + (k + 2))
                    w1(1 - p, WE[kn])
                    pe.wait_ge(s["m_hid"], WRING * i + (k + 3))
                    w2(p, WE[k])
            for k in range(WRING):
                e = E - WRING + k
                p = (k + 1) % 2
                if k + 1 < WRING:
                    pe.wait_ge(ld_we[k + 1], 16 * (E // WRING))
                    pe.wait_ge(s["m_hid"], e + 2)
                    w1(1 - p, WE[k + 1])
                pe.wait_ge(s["m_hid"], e + 3)
                w2(p, WE[k], final=(k == WRING - 1))


SSM1_IN_FFN = 4
FFN_SSM_AT = [2, 5, 8, 11][:SSM1_IN_FFN]


def att1_plan():
    plan = []
    units = B * H1
    jobs = [(b, i) for b in range(B) for i in range(6)]
    rest = DS - SSM1_IN_FFN
    ssm = list(range(SSM1_IN_FFN, DS))

    def job(j, split=False):
        b, i = j
        plan.append(("job", j))
        if i:
            plan.append(("rope", (b, i - 1)))
            plan.append(("jobtr", (b, i - 1)))

    for j in jobs[0:3]:
        job(j)
    nxt = 3
    for u in range(units + 3):
        if u < units:
            plan.append(("exp", u))
        if 1 <= u <= units:
            plan.append(("norm", u - 1))
        if u < units:
            b, h = u // H1, u % H1
            g, r = h // REP1, h % REP1
            if r == 0 and nxt < len(jobs):
                cur = [jobs[nxt]]
                nxt += 1
                if jobs[nxt - 1][1] == 0:
                    plan.append(("job", cur[0]))
                    cur = [jobs[nxt], jobs[nxt + 1]]
                    nxt += 2
                todo = []
                for (jb, ji) in cur:
                    todo += [("job", (jb, ji)), ("rope", (jb, ji - 1)), ("jobtr", (jb, ji - 1))]
                pend = todo
            if r < 3:
                k = (len(pend) + (2 - r)) // (3 - r) if pend else 0
                for _ in range(k):
                    plan.append(pend.pop(0))
        if 1 <= u <= units:
            plan.append(("pt", u - 1))
            plan.append(("pv", u - 1))
            plan.append(("at", u - 1))
        if u >= 2 and u - 2 < units:
            plan.append(("o", u - 2))
            if (u - 2) % H1 == H1 - 1:
                plan.append(("res", (u - 2) // H1))
        if u < units and ssm and (u + 1) * rest // units > u * rest // units:
            plan.append(("ssm", ssm.pop(0)))
    for n in ssm:
        plan.append(("ssm", n))
    return plan


ATT1_PLAN = att1_plan()

_ORDER = ["x", "ctxp", "pk0", "pk1", "dtw0", "dtw1", "ident", "identb", "mask0", "mask1", "cos0", "sin0", "rope1", "gains",
          "wqkv0", "wo0", "ffn", "wdn", "skip", "fsc", "dsc", "wqkv1", "wo1", "we", "wrt", "br"]


def _layout(i):
    bf16 = mybir.dt.np(BF16)
    f = np.float32
    a = {k: np.asarray(v) for k, v in i.items()}
    o = {"x": a["x"]}
    c = np.zeros((P, B, S + DC - 1), f)
    c[:, :, DC - 1:] = a["ctx_1024"].transpose(2, 0, 1)
    o["ctxp"] = c
    chan = lambda z: z.reshape(DT, P, -1).transpose(1, 0, 2).reshape(P, -1)
    rows = lambda z: np.broadcast_to(z.reshape(1, -1), (P, z.size))
    for l in range(2):
        q = lambda n: a[f"L{l}_xattn_{n}"]
        cw = q("conv_w").reshape(DI, DC)
        xp = q("x_proj_w")
        order = list(range(DR)) + [DR + DS * r + n for n in range(DS) for r in range(2)]
        o[f"pk{l}"] = np.concatenate([q("in_proj_w").T, rows(cw.T), chan(q("conv_b")), chan(q("dt_proj_b")),
                                      chan(q("A_log")), chan(xp[order].T)], 1)
        o[f"dtw{l}"] = q("dt_proj_w").T
    wt = lambda w: w.T.reshape(-1, P, w.shape[0]).transpose(1, 0, 2)
    o["wqkv0"] = wt(np.concatenate([a["L0_attn_Wq"], a["L0_attn_Wk"], a["L0_attn_Wv"]], 0))
    o["wo0"] = wt(a["L0_attn_Wo"])
    gu = wt(np.concatenate([a["L0_ffn_gate_w"], a["L0_ffn_up_w"]], 0)).reshape(P, -1)
    dn = np.zeros((NI * P, HID), f)
    dn[:INTER] = a["L0_ffn_down_w"].T
    o["ffn"], o["wdn"] = gu, dn.reshape(NI, P, HID).transpose(1, 0, 2)
    o["skip"] = np.stack([chan(a[f"L{l}_xattn_D"]) for l in range(2)], 1)
    sc = np.zeros((2, NI * P), f)
    sc[0, :INTER], sc[1, :INTER] = a["L0_ffn_gate_s"], a["L0_ffn_up_s"]
    o["fsc"] = sc.reshape(2, NI, P).transpose(2, 0, 1)
    o["dsc"] = rows(a["L0_ffn_down_s"])
    o["wqkv1"] = wt(a["L1_attn_w_qkv"])
    o["wo1"] = wt(a["L1_attn_w_o"])
    w1 = np.concatenate([a["L1_ffn_W1"], a["L1_ffn_Ws1"].reshape(2, M, HID)], 0)
    w2 = np.concatenate([a["L1_ffn_W2"], a["L1_ffn_Ws2"].reshape(HID, 2, M).transpose(1, 0, 2)], 0)
    w1 = w1.transpose(0, 2, 1).reshape(E + 2, HC, P, M).transpose(0, 2, 1, 3).reshape(E + 2, P, HC * M)
    o["we"] = np.concatenate([w1, w2.transpose(0, 2, 1)], 2)
    o["wrt"] = wt(a["L1_ffn_Wr"])
    o["br"] = a["L1_ffn_br"].reshape(1, E)
    g = [a["L1_attn_" + n] for n in ("qn_g", "qn_b", "kn_g", "kn_b")]
    sw = lambda z: np.concatenate([z[D1 // 2:], z[:D1 // 2]])
    o["gains"] = np.stack([rows(z) for z in (g[0], g[1], sw(g[0]), sw(g[1]), g[2], g[3], sw(g[2]), sw(g[3]))], 1)
    o["ident"] = np.eye(P, dtype=f)
    o["identb"] = np.eye(P).astype(bf16)
    k, qn = np.arange(P)[:, None], np.arange(W0)[None, :]
    m0 = np.where((k <= qn) & (k > qn - WIN0), 0.0, -100.0)
    o["mask0"] = np.concatenate([m0, m0[:, :P]], 1).astype(bf16)
    tri = np.where(np.arange(P)[None, :] <= k, 0.0, -1e30)
    o["mask1"] = np.concatenate([tri, np.zeros((P, P)), tri], 1).astype(bf16)

    def rope(dim):
        inv = (f(1.0) / (f(1e6) ** (np.arange(0, dim, 2, dtype=f) / f(dim)))).astype(f)
        fr = np.arange(S, dtype=f)[:, None] * inv[None, :]
        cs, sn = np.cos(fr), np.sin(fr)
        return np.concatenate([cs, cs], 1).astype(f), np.concatenate([-sn, sn], 1).astype(f)

    half = lambda z: z.reshape(2, P, -1).transpose(1, 0, 2)
    cs, sn = rope(D0)
    o["cos0"], o["sin0"] = half(np.tile(cs, (1, H0 + KV0))), half(np.tile(sn, (1, H0 + KV0)))
    cs, sn = rope(D1)
    qs = f(D1 ** -0.5)
    o["rope1"] = np.stack([half(cs * qs), half(sn * qs), half(cs), half(sn)], 1)
    return {n: np.ascontiguousarray(o[n]) for n in _ORDER}


def kernel(**inputs):
    import concourse.bacc as bacc
    from concourse.bass_utils import run_bass_kernel_spmd as run

    arrays = _layout(inputs)
    nc = bacc.Bacc("TRN2", target_bir_lowering=False, num_devices=1)
    io = {n: nc.dram_tensor("in_" + n, z.shape, mybir.dt.from_np(z.dtype), kind="ExternalInput").ap() for n, z in arrays.items()}
    out = nc.dram_tensor("out_0", (B, S, HID), F32, kind="ExternalOutput").ap()
    build(nc, io, out)
    r = run(nc, [{"in_" + n: z for n, z in arrays.items()}], core_ids=[0])
    return r.results[0]["out_0"]
```

```python
from contextlib import ExitStack

import concourse.bass as bass
import numpy as np
from concourse import mybir

F32 = mybir.dt.float32
BF16 = mybir.dt.bfloat16
F32R = mybir.dt.float32r
I32 = mybir.dt.int32
ALU = mybir.AluOpType
ACT = mybir.ActivationFunctionType
AX = mybir.AxisListType

P = 128
B, S, HID = 4, 256, 256
T = B * S
NT = T // P
HC = HID // P
DM, DI, DS, DC, DR = 128, 256, 16, 4, 8
DT = DI // P
H0, KV0, D0, WIN0 = 8, 2, 32, 64
REP0 = H0 // KV0
NQK0 = (H0 + KV0) * D0
NQKV0 = NQK0 + KV0 * D0
SCORE0 = 256.0 / (D0 ** 0.5) / 30.0
SOFTCAP = 30.0
W0 = P + WIN0
INTER = 704
NI = (INTER + P - 1) // P
H1, KV1, D1 = 16, 4, 128
REP1 = H1 // KV1
NQ1, NK1 = H1 * D1, KV1 * D1
E, G, KG, K, M, SH = 32, 8, 4, 6, 128, 256
EPG = E // G
ROUTE_SCALE = 2.5
SB_LOADS = 2
WRING = 4

PK_IN = 0
PK_CW = PK_IN + DI
PK_CB = PK_CW + DC * DI
PK_DB = PK_CB + DT
PK_A = PK_DB + DT
PK_X = PK_A + DT * DS
PK_N = PK_X + DT * (DR + 2 * DS)

C_ON_DVE = {0: [n for n in range(DS) if n % 3 != 1], 1: [n for n in range(DS) if n % 3 == 1]}


def c_step(g):
    mine = lambda q: q % DS in C_ON_DVE[q // DS]
    return ("c_dve" if mine(g) else "c_pool"), sum(mine(q) == mine(g) for q in range(g + 1))


def mlen(i):
    return min(P, INTER - i * P)


class Chain:

    def __init__(self, eng, sem):
        self.eng, self.sem, self.n = eng, sem, 0

    def step(self, ins):
        self.n += 1
        ins.then_inc(self.sem, 1)
        return self.n

    def wait(self, mark=None):
        self.eng.wait_ge(self.sem, self.n if mark is None else mark)

    def link(self, ins):
        self.step(ins)
        self.wait()


def build(nc, io, out):
    ctx = ExitStack()
    with ctx:
        def sb(name, shape, dt=F32):
            return ctx.enter_context(nc.sbuf_tensor(name, shape, dt))

        def sem(name):
            return ctx.enter_context(nc.semaphore(name))

        X = sb("X", [P, NT, HID])
        H = sb("H", [P, NT, HID])
        hT = sb("hT", [P, HC, T])
        ctxp = sb("ctxp", [P, B, S + DC - 1])
        pkb = sb("pkb", [P, PK_N])
        pk = [pkb, pkb]
        skip = sb("skip", [P, 2, DT])
        dtw = [sb(f"dtw{l}", [DR, DI]) for l in range(2)]
        LW = [pk[l][:, PK_CW:PK_CW + DC * DI].rearrange("p (k n) -> p k n", k=DC) for l in range(2)]
        scan_base = nc.sbuf_base
        DEL = sb("DEL", [P, DT, T])
        DU = sb("DU", [P, DT, T])
        ACC = sb("ACC", [P, DT, T])
        U = ACC
        dA = [sb(f"dA{s}", [P, DT, T]) for s in range(2)]
        hS = [sb(f"hS{s}", [P, DT, T]) for s in range(2)]
        BCb = [sb(f"BCb{s}", [P, 2, T]) for s in range(SB_LOADS)]
        def split(name, place, shape):
            return nc.alloc_sbuf_tensor_at(name, shape, F32R, offset=scan_base + place * DT * T * 4)

        hTh, hTl = split("hTh", 0, [P, HC, T]), split("hTl", 1, [P, HC, T])
        MHh, MHl = split("MHh", 2, [P, 2, T]), split("MHl", 3, [P, 2, T])
        Wh, Wl = split("Wh", 4, [P, WRING, 512]), split("Wl", 5, [P, WRING, 512])
        negA = sb("negA", [P, DT * DS])
        cbh = sb("cbh", [P, DT])
        ident = sb("ident", [P, P])
        identb = sb("identb", [P, P], BF16)
        mask0 = sb("mask0", [P, W0 + P], BF16)
        mask1 = sb("mask1", [P, 3 * P], BF16)
        tabs = sb("tabs", [P, 6, 2, D1])
        lnst = sb("lnst", [P, NT, 6])
        lnmv = sb("lnmv", [P, NT, 2])
        lnve = sb("lnve", [P, NT])
        lnrs = sb("lnrs", [P, NT])
        mhalf = sb("mhalf", [P, NT])
        ones1 = sb("ones1", [1, P])
        WA = sb("WA", [P, H1 * HID])
        WGU = WA[:, 0:HC * 2 * INTER].rearrange("p (c n) -> p c n", c=HC)
        WO1 = WA[:, 0:H1 * HID].rearrange("p (h n) -> p h n", h=H1)
        fsc = sb("fsc", [P, 3, NI])
        dsc = sb("dsc", [P, HID])
        WB = sb("WB", [P, HC, NQ1 + 2 * NK1])
        WQKV0 = WB[:, 0, 0:HC * NQKV0].rearrange("p (c n) -> p c n", c=HC)
        WO0 = WB[:, 0, HC * NQKV0:HC * NQKV0 + HC * HID].rearrange("p (c n) -> p c n", c=HC)
        WE = [WB[:, 0, 512 * s:512 * s + 512] for s in range(WRING)]
        WS = [WB[:, 1, 512 * s:512 * s + 512] for s in range(2)]
        WRT = WB[:, 1, 1024:1024 + HC * E].rearrange("p (c e) -> p c e", c=HC)
        BR = WB[0:E, 1, 1024 + HC * E:1024 + HC * E + 1]
        wmean = sb("wmean", [P, HC, H1 + KV1])
        arena = sb("arena", [P, 48 * 256])
        kb = 256

        def ar(k0, n):
            return arena[:, int(k0 * kb):int(k0 * kb) + n]

        Q0 = ar(0, NT * NQKV0).rearrange("p (t n) -> p t n", t=NT)
        RA = ar(12, NT * NQK0).rearrange("p (t n) -> p t n", t=NT)
        RB = ar(22, NT * NQK0).rearrange("p (t n) -> p t n", t=NT)
        SQ0 = ar(12, NT * NQKV0)
        K40 = ar(12, NT * KV0 * P).rearrange("p (t g n) -> p t g n", t=NT, g=KV0)
        cos0 = ar(32, 2 * NQK0).rearrange("p (h n) -> p h n", h=2)
        sin0 = ar(35, 2 * NQK0).rearrange("p (h n) -> p h n", h=2)
        qT0 = ar(32, KV0 * T).rearrange("p (g t) -> p g t", g=KV0)
        kT0 = ar(40, KV0 * T).rearrange("p (g t) -> p g t", g=KV0)
        TH0 = ar(12, REP0 * (W0 + P)).rearrange("p (r n) -> p r n", r=REP0)
        PT0 = [z.rearrange("p (r k q) -> p r k q", r=REP0, k=2) for z in (WB[:, 1, 0:REP0 * 2 * S], ar(22, REP0 * 2 * S))]
        st0 = ar(30, 4 * NT * NQKV0 // D0).rearrange("p (i n) -> p i n", i=4)
        ones32 = sb("ones32", [P, D0])
        rden0 = ar(17, S)
        aT0 = H[:].rearrange("p (g t) d -> p g (t d)", g=KV0)
        WDN = ar(40, NI * HID).rearrange("p (i n) -> p i n", i=NI)
        hid0 = ar(0, NI * T).rearrange("p (i t) -> p i t", i=NI)
        fth = [ar(24 + 2 * s, 512) for s in range(2)]
        ft1 = [ar(28 + 2 * s, 512) for s in range(2)]
        rope1 = ar(32, 8 * D1).rearrange("p (i h d) -> p i h d", i=4, h=2)
        gains = ar(36, 8 * D1).rearrange("p (i d) -> p i d", i=8)
        SQ = ar(0, 1024).rearrange("p (t n) -> p t n", t=2)
        JA = ar(4, 1024).rearrange("p (t n) -> p t n", t=2)
        JB = ar(8, 1024).rearrange("p (t n) -> p t n", t=2)
        R = ar(12, 1024).rearrange("p (t n) -> p t n", t=2)
        KT = [ar(16 + 4 * s, 1024).rearrange("p (h q) -> p h q", h=KV1) for s in range(2)]
        QT = [ar(24 + 4 * s, 1024).rearrange("p (h q) -> p h q", h=REP1) for s in range(2)]
        V1 = [ar(32 + 4 * s, 1024).rearrange("p (t n) -> p t n", t=2) for s in range(2)]
        P1 = [ar(40 + 1.5 * s, 384) for s in range(2)]
        PT1 = [ar(43 + 1.5 * s, 384) for s in range(2)]
        aT1 = [ar(46 + s, 256) for s in range(2)]
        jst = sb("jst", [P, 2, 3, 8])
        nm1 = sb("nm1", [P, 2, 2])
        sum1 = sb("sum1", [P, 2, 2])
        rc1 = sb("rc1", [P, 2, 2])
        job_bank = lambda j: 6 if j == 1 else 0
        job_a = lambda j: (KT[1].rearrange("p h q -> p (h q)").rearrange("p (t n) -> p t n", t=2)) if j == 1 else JA
        job_b = lambda j: V1[1] if j == 1 else JB
        job_s = lambda j: (QT[1].rearrange("p h q -> p (h q)").rearrange("p (t n) -> p t n", t=2)) if j == 1 else SQ
        v_bank = lambda b: 0 if b else 3
        GB = [ar(4 * s, T) for s in range(WRING)]
        MR = [ar(16 + 4 * s, T) for s in range(2)]
        MG = [ar(24 + 4 * s, T) for s in range(2)]
        MH = [ar(32 + 4 * s, T) for s in range(2)]
        gT = ar(40, T)[0:E, :]
        rET = ar(44, T)[0:E, :]
        at = [0]

        def router(*shape):
            n = int(np.prod(shape))
            at[0] += n
            z = arena[:, at[0] - n:at[0]]
            return z if len(shape) == 1 else z.rearrange("p (t n) -> p t n", t=shape[0])

        rS, rW, rGate = router(NT, E), router(NT, E), router(NT, E)
        rg = [router(NT * G) for i in range(6)]
        rGW, rGM = router(NT, G + 4), router(NT, G + 4)
        rMS, rME = router(NT, E + 2), router(NT, E + 2)
        rM8, rT8, rE8 = router(NT, 8), router(NT, 8), router(NT, 8)
        rsum = router(2, NT)
        ps = ctx.enter_context(nc.psum_tensor("ps", [P, 8, 512], F32))

        bc_dram = nc.dram_tensor("bc_dram", [2, DS, 2, T], F32, kind="Internal").ap()
        gate_dram = nc.dram_tensor("gate_dram", [E, T], F32, kind="Internal").ap()

        ld = {n: sem("ld_" + n) for n in ("ctx", "pk0", "pk1", "x", "ident", "masks", "rope0", "rope1", "wqkv0",
                                          "wo0", "ffn", "wdn", "wqkv1", "wo1", "shared", "route")}
        ld_bc = [sem(f"ld_bc{s}") for s in range(SB_LOADS)]
        ld_we = [sem(f"ld_we{s}") for s in range(WRING)]
        ld_gb = [sem(f"ld_gb{s}") for s in range(WRING)]
        names = """act_chain dve_chain pool_chain init lw_ready conv_mm conv_tanh u_ready xdbl_mm dt_low_copied bc_copied bc_stored
            dtpre_mm sp_abs sp_exp sp_ln delta_ready da_cols_zero da_ready dbu_ready scan_done c_dve c_pool ssm_acc
            ln_mv ln_rstd ln_h ln_tr_mm ln_tr_act ln_tr_dve qkv0_mm qkv0_copied rope0_rot rope0_sq rope0_done k4_ready tr0_mm tr0_copied
            s0_mm s0_tanh s0_exp pv0_mm at0_ready o0_mm x_new fsc_ready gate_tanh gate_y gate_mm nega_exp nega_ready pt0_fill
            f_mm f_tanh f_hid fd_mm wdn_ready w1_mean w1_centered tabs_ready job_mm job_sq job_rot job_sum job_rstd job_add job_rope
            job_tr_mm job_tr_copied v_mm v_copied s1_mm s1_max s1_exp s1_norm pt1_mm pt1_copied pv1_mm at1_copied o1_mm
            r_bias r_mm r_exp r_tr r_sum r_gate gt_mm gt_copied gate_stored h_hi h_lo_dve h_lo_pool w_hi w_lo
            m_mm m_relu m_sq m_gated m_hid m_hi m_lo m_out out_done""".split()
        s = {n: sem(n) for n in names}
        block = ctx.enter_context(nc.Block())

        bands = lambda a: a.rearrange("p (b s) -> p b s", b=B)
        xr = io["x"].rearrange("b (h p) d -> p (b h) d", p=P)
        outr = out.rearrange("b (h p) d -> p (b h) d", p=P)

        XN_ATT0, XN_GATE0, XN_FFN, XN_ATT1, XN_GATE1 = 2, 4, 6, 10, 12
        XN = {0: 0, 1: XN_ATT0, 2: XN_GATE0, 3: XN_FFN, 4: XN_ATT1, 5: XN_GATE1}
        TR_LNS = [0, 2, 3, 5]
        TR_BANK = [(4, 6), (0, 2), (2, 2), (0, 2)]
        CONV_BANK = [0, 4]

        @block.sync
        def _(sp):
            sp.dma_start(ctxp[:], io["ctxp"]).then_inc(ld["ctx"], 16)
            sp.dma_start(pk[0][:], io["pk0"]).then_inc(ld["pk0"], 16)
            sp.dma_start(dtw[0][:], io["dtw0"]).then_inc(ld["pk0"], 16)
            sp.dma_start(skip[:], io["skip"]).then_inc(ld["pk0"], 16)
            sp.dma_start(X[:], xr).then_inc(ld["x"], 16)
            sp.dma_start(ident[:], io["ident"]).then_inc(ld["ident"], 16)
            sp.dma_start(WQKV0, io["wqkv0"]).then_inc(ld["wqkv0"], 16)
            sp.dma_start(cos0, io["cos0"]).then_inc(ld["rope0"], 16)
            sp.dma_start(sin0, io["sin0"]).then_inc(ld["rope0"], 16)
            sp.dma_start(identb[:], io["identb"]).then_inc(ld["masks"], 16)
            sp.dma_start(mask0[:], io["mask0"]).then_inc(ld["masks"], 16)
            sp.dma_start(mask1[:], io["mask1"]).then_inc(ld["masks"], 16)

            def load_bc(g):
                sp.wait_ge(s["bc_stored"], 16 * (g // DS + 1))
                if g >= SB_LOADS:
                    sp.wait_ge(s["dbu_ready"], g - SB_LOADS + 1)
                    who, count = c_step(g - SB_LOADS)
                    sp.wait_ge(s[who], count)
                src = bc_dram[g // DS, g % DS].rearrange("r t -> (r t)").partition_broadcast(P)
                sp.dma_start(BCb[g % SB_LOADS][:].rearrange("p r t -> p (r t)"), src).then_inc(ld_bc[g % SB_LOADS], 16)

            sp.dma_start(WO0, io["wo0"]).then_inc(ld["wo0"], 16)
            sp.wait_ge(s["delta_ready"], 1)
            sp.wait_ge(s["sp_exp"], 1)
            sp.wait_ge(s["nega_exp"], 1)
            sp.dma_start(pk[1][:], io["pk1"]).then_inc(ld["pk1"], 16)
            sp.dma_start(dtw[1][:], io["dtw1"]).then_inc(ld["pk1"], 16)
            sp.dma_start(WA[:, 0:HC * 2 * INTER], io["ffn"]).then_inc(ld["ffn"], 16)
            sp.dma_start(fsc[:, 0:2, :], io["fsc"]).then_inc(ld["ffn"], 16)
            sp.dma_start(dsc[:], io["dsc"]).then_inc(ld["ffn"], 16)
            for g in range(DS):
                load_bc(g)
            sp.wait_ge(s["o0_mm"], 2)
            sp.dma_start(WDN, io["wdn"]).then_inc(ld["wdn"], 16)
            sp.dma_start(rope1, io["rope1"]).then_inc(ld["rope1"], 16)
            sp.dma_start(gains, io["gains"]).then_inc(ld["rope1"], 16)
            sp.dma_start(WB[:], io["wqkv1"]).then_inc(ld["wqkv1"], 16)
            for g in range(DS, 2 * DS):
                load_bc(g)
            sp.wait_ge(s["job_mm"], len(JOB))
            sp.wait_ge(s["v_mm"], B)
            for i in range(2):
                sp.dma_start(WS[i], io["we"][E + i]).then_inc(ld["shared"], 16)
            sp.dma_start(WRT, io["wrt"]).then_inc(ld["route"], 16)
            sp.dma_start(BR, io["br"]).then_inc(ld["route"], 16)
            for e in range(WRING):
                sp.dma_start(WE[e], io["we"][e]).then_inc(ld_we[e], 16)
            sp.wait_ge(s["gate_stored"], 16)
            for e in range(WRING):
                sp.dma_start(GB[e], gate_dram[e].partition_broadcast(P)).then_inc(ld_gb[e], 16)
            with sp.Fori(1, E // WRING, 1) as i:
                for k in range(WRING):
                    sp.wait_ge(s["m_lo"], WRING * i + (k - WRING + 3))
                    sp.dma_start(WE[k], io["we"][bass.ds(WRING * i + k, 1)].rearrange("a p n -> (a p) n")).then_inc(ld_we[k], 16)
                    sp.dma_start(GB[k], gate_dram[bass.ds(WRING * i + k, 1)].rearrange("a t -> (a t)").partition_broadcast(P)).then_inc(ld_gb[k], 16)
            for hf in range(2):
                sp.wait_ge(s["x_new"], XN_GATE1 + 1 + hf)
                sp.dma_start(outr[:, 4 * hf:4 * hf + 4, :], X[:, 4 * hf:4 * hf + 4, :]).then_inc(s["out_done"], 16)
            sp.wait_ge(s["out_done"], 32)

        @block.gpsimd
        def _(pool):
            gp = nc.gpsimd
            ch = Chain(pool, s["pool_chain"])
            gp.memset(mhalf[:], -0.5).then_inc(s["init"], 1)
            gp.memset(ones32[:], 1.0).then_inc(s["init"], 1)
            gp.memset(ones1[:], 1.0).then_inc(s["init"], 1)
            floor = float(np.exp(np.float32(-SOFTCAP)))
            gp.memset(PT0[0][:, :, 0, W0:S], floor).then_inc(s["pt0_fill"], 1)
            gp.memset(PT0[0][:, :, 1, 0:P], floor).then_inc(s["pt0_fill"], 1)
            pool.wait_ge(s["init"], 3)

            def ln_rstd(L):
                for hf in range(2):
                    z = slice(4 * hf, 4 * hf + 4)
                    pool.wait_ge(s["ln_mv"], NT * L + 4 * hf + 4)
                    ch.link(gp.tensor_scalar(lnve[:, z], lnmv[:, z, 1], 1e-5, None, ALU.add))
                    gp.tensor_tensor(lnrs[:, z], lnve[:, z], mhalf[:, z], ALU.pow).then_inc(s["ln_rstd"], 1)

            def zero_cols(l):
                pool.wait_ge(s["delta_ready"], l + 1)
                for slot in range(2):
                    gp.memset(dA[slot][:].rearrange("p d (b s) -> p (d b) s", b=B)[:, :, 0:1], 0.0).then_inc(s["da_cols_zero"], 1)

            def ssm_step(l, n):
                g = DS * l + n
                h = hS[g % 2]
                cb = BCb[g % SB_LOADS][:, 1, :]
                if n in C_ON_DVE[l]:
                    pool.wait_ge(s["c_dve"], c_step(g)[1])
                else:
                    pool.wait_ge(s["scan_done"], g + 1)
                    pool.wait_ge(ld_bc[g % SB_LOADS], 16 * (g // SB_LOADS + 1))
                    gp.tensor_tensor(h[:], h[:], cb.unsqueeze(1).broadcast_to([P, DT, T]), ALU.mult).then_inc(s["c_pool"], 1)
                    pool.wait_ge(s["c_pool"], c_step(g)[1])
                if n == 0:
                    pool.wait_ge(s["delta_ready"], l + 1)
                if g:
                    pool.wait_ge(s["ssm_acc"], g)
                if True:
                    gp.tensor_tensor(ACC[:], ACC[:], h[:], ALU.add).then_inc(s["ssm_acc"], 1)

            ln_rstd(0)
            zero_cols(0)
            pool.wait_ge(s["rope0_done"], 1)
            gp.memset(PT0[1][:, :, 0, W0:S], floor).then_inc(s["pt0_fill"], 1)
            gp.memset(PT0[1][:, :, 1, 0:P], floor).then_inc(s["pt0_fill"], 1)
            for n in range(DS):
                ssm_step(0, n)
            pool.wait_ge(ld["wdn"], 16)
            pool.wait_ge(ld["ffn"], 48)
            for i in range(NI):
                m = mlen(i)
                gp.tensor_tensor(WDN[0:m, i, :], WDN[0:m, i, :], dsc[0:m, :], ALU.mult).then_inc(s["wdn_ready"], 1)
            ln_rstd(1)
            ln_rstd(2)
            pool.wait_ge(s["w1_mean"], 1)
            for c in range(HC):
                w = WB[:, c, 0:NQ1 + NK1].rearrange("p (h d) -> p h d", d=D1)
                gp.tensor_tensor(w, w, wmean[:, c, :].unsqueeze(2).broadcast_to([P, H1 + KV1, D1]), ALU.add).then_inc(s["w1_centered"], 1)
            zero_cols(1)
            step = iter(range(DS))
            for _ in range(SSM1_IN_FFN - 1):
                ssm_step(1, next(step))
            ln_rstd(3)
            ssm_step(1, next(step))

            def job(j):
                pool.wait_ge(s["job_sum"], j + 1)
                st = jst[:, j % 2]
                ch.link(gp.tensor_scalar(st[:, 1, :], st[:, 0, :], 1.0 / D1, 1e-5, ALU.mult, ALU.add))
                gp.tensor_tensor(st[:, 2, :], st[:, 1, :], mhalf[:], ALU.pow).then_inc(s["job_rstd"], 1)
                pool.wait_ge(s["job_rot"], 3 * (j + 1))
                gp.tensor_tensor(job_a(j), job_a(j), job_b(j), ALU.add).then_inc(s["job_add"], 1)

            left = DS - SSM1_IN_FFN
            for kind, a in ATT1_PLAN:
                if kind == "sum":
                    job(JOB[a])
                if kind == "scan":
                    ssm_step(1, a)
            ln_rstd(4)
            ln_rstd(5)

            def w_low(x, src):
                slot = x % WRING
                gp.tensor_tensor(Wl[:, slot, :], src, Wh[:, slot, :].bitcast(F32), ALU.subtract).then_inc(s["w_lo"], 1)

            def hid_low(p):
                gp.tensor_tensor(MHl[:, p, :], MH[p], MHh[:, p, :].bitcast(F32), ALU.subtract).then_inc(s["m_lo"], 1)

            for x in range(2):
                pool.wait_ge(s["w_hi"], x + 1)
                w_low(x, WS[x])
            pool.wait_ge(s["h_hi"], 2)
            z = slice(512, 1024)
            gp.tensor_tensor(hTl[:, :, z], hT[:, :, z], hTh[:, :, z].bitcast(F32), ALU.subtract).then_inc(s["h_lo_pool"], 1)
            for x in range(2, 4):
                pool.wait_ge(s["w_hi"], x + 1)
                w_low(x, WE[x - 2])
            for x in range(2):
                pool.wait_ge(s["m_hi"], x + 1)
                hid_low(x)
            with pool.Fori(0, E // WRING - 1, 1) as i:
                for k in range(WRING):
                    pool.wait_ge(s["w_hi"], WRING * i + (k + 5))
                    w_low(k, WE[(k + 2) % WRING])
                    pool.wait_ge(s["m_hi"], WRING * i + (k + 3))
                    hid_low(k % 2)
            for e in range(E - WRING, E):
                if e + 2 < E:
                    pool.wait_ge(s["w_hi"], e + 5)
                    w_low(e, WE[(e + 2) % WRING])
                pool.wait_ge(s["m_hi"], e + 3)
                hid_low(e % 2)

        @block.scalar
        def _(act):
            sc = nc.scalar
            ch = Chain(act, s["act_chain"])

            def conv_tanh(l, d):
                act.wait_ge(s["conv_mm"], DT * l + d + 1)
                act.wait_ge(s["lw_ready"], l + 1)
                c0 = CONV_BANK[l] + 2 * d
                if l:
                    act.wait_ge(s["da_ready"], 2 * DS)
                sc.activation(DEL[:, d, :], ps[:, c0:c0 + 2, :].rearrange("p a b -> p (a b)"), ACT.Tanh,
                              bias=cbh[:, d:d + 1], scale=0.5).then_inc(s["conv_tanh"], 1)

            def xdbl_copy(l):
                act.wait_ge(s["xdbl_mm"], 2 * l + 1)
                c0 = CONV_BANK[l]
                sc.copy(dA[0][0:DR, 0, :], ps[0:DR, c0:c0 + 2, :].rearrange("p a b -> p (a b)")).then_inc(s["dt_low_copied"], 1)
                act.wait_ge(s["xdbl_mm"], 2 * l + 2)
                sc.copy(dA[1][0:2 * DS, 0, :], ps[0:2 * DS, c0 + 2:c0 + 4, :].rearrange("p a b -> p (a b)")).then_inc(s["bc_copied"], 1)
                act.wait_ge(s["bc_copied"], l + 1)
                act.dma_start(bc_dram[l].rearrange("n r t -> (n r) t"), dA[1][0:2 * DS, 0, :]).then_inc(s["bc_stored"], 16)

            def softplus(l):
                for d in range(DT):
                    act.wait_ge(s["dtpre_mm"], DT * l + d + 1)
                    c0 = CONV_BANK[l] + 2 * d
                    sc.activation(hS[0][:, d, :], ps[:, c0:c0 + 2, :].rearrange("p a b -> p (a b)"), ACT.Abs,
                                  bias=pk[l][:, PK_DB + d:PK_DB + d + 1]).then_inc(s["sp_abs"], 1)
                act.wait_ge(s["sp_abs"], DT * (l + 1))
                sc.activation(hS[0][:], hS[0][:], ACT.Exp, scale=-1.0).then_inc(s["sp_exp"], 1)

            def softplus_ln(l):
                act.wait_ge(s["bc_stored"], 16 * (l + 1))
                act.wait_ge(s["sp_exp"], l + 1)
                sc.activation(dA[1][:], hS[0][:], ACT.Ln, bias=1.0).then_inc(s["sp_ln"], 1)

            def neg_a(l):
                act.wait_ge(ld[f"pk{l}"], 48 - 16 * l)
                if l:
                    act.wait_ge(s["da_ready"], 2 * DS)
                sc.activation(negA[:], pk[l][:, PK_A:PK_A + DT * DS], ACT.Exp).then_inc(s["nega_exp"], 1)
                act.wait_ge(s["nega_exp"], l + 1)
                sc.mul(negA[:], negA[:], -1.0).then_inc(s["nega_ready"], 1)

            def ssm_step(l, n):
                g = DS * l + n
                if n == 0:
                    act.wait_ge(s["delta_ready"], l + 1)
                    act.wait_ge(s["nega_ready"], l + 1)
                    act.wait_ge(s["da_cols_zero"], 2 * (l + 1))
                if n >= 2:
                    act.wait_ge(s["scan_done"], g - 1)
                for d in range(DT):
                    o = bands(dA[g % 2][:, d, :])[:, :, 1:S]
                    sc.activation(o, bands(DEL[:, d, :])[:, :, 1:S], ACT.Exp,
                                  scale=negA[:, d * DS + n:d * DS + n + 1]).then_inc(s["da_ready"], 1)

            def ln_tr_copy(i, halves=(0, 1)):
                for hf in halves:
                    act.wait_ge(s["ln_tr_mm"], 4 * i + 2 * hf + 1)
                    sc.copy(hT[:, 0, 512 * hf:512 * hf + 512], ps[:, TR_BANK[i][hf], :]).then_inc(s["ln_tr_act"], 1)

            neg_a(0)
            for d in range(DT):
                conv_tanh(0, d)
            ln_tr_copy(0)
            xdbl_copy(0)
            softplus(0)
            softplus_ln(0)
            for t in range(NT):
                act.wait_ge(s["qkv0_mm"], t + 1)
                sc.copy(Q0[:, t, :], ps[:, 4 + t % 4, 0:NQKV0]).then_inc(s["qkv0_copied"], 1)
            ssm_step(0, 0)
            ssm_step(0, 1)
            act.wait_ge(s["rope0_rot"], 1)
            sc.activation(SQ0, Q0.rearrange("p t n -> p (t n)"), ACT.Square).then_inc(s["rope0_sq"], 1)
            act.wait_ge(s["rope0_done"], 1)
            for g in range(KV0):
                c = H0 * D0 + D0 * g
                sc.copy(K40[:, :, g, :].rearrange("p t (r d) -> p t r d", d=D0),
                        Q0[:, :, c:c + D0].unsqueeze(2).broadcast_to([P, NT, 4, D0])).then_inc(s["k4_ready"], 1)
            for i in range(8):
                act.wait_ge(s["tr0_mm"], i + 1)
                g, part, hf = i // 4, (i // 2) % 2, i % 2
                dst = (qT0, kT0)[part][:, g, 512 * hf:512 * hf + 512]
                sc.copy(dst, ps[:, 4 + i % 4, :]).then_inc(s["tr0_copied"], 1)
            nstep = 2
            for u in range(B * KV0):
                act.wait_ge(s["s0_mm"], u + 1)
                if u:
                    act.wait_ge(s["s0_exp"], 2 * u)
                sc.activation(TH0, ps[:, 0:REP0, 0:W0 + P], ACT.Tanh, scale=SCORE0).then_inc(s["s0_tanh"], 1)
                act.wait_ge(s["s0_tanh"], u + 1)
                act.wait_ge(s["pt0_fill"], 4)
                if u >= 2:
                    act.wait_ge(s["pv0_mm"], u - 1)
                pt = PT0[u % 2]
                sc.activation(pt[:, :, 0, 0:W0], TH0[:, :, 0:W0], ACT.Exp, scale=SOFTCAP).then_inc(s["s0_exp"], 1)
                sc.activation(pt[:, :, 1, P:S], TH0[:, :, W0:W0 + P], ACT.Exp, scale=SOFTCAP).then_inc(s["s0_exp"], 1)
                for _ in range(2):
                    if nstep < DS:
                        ssm_step(0, nstep)
                        nstep += 1
            while nstep < DS:
                ssm_step(0, nstep)
                nstep += 1

            def gate_tanh(l):
                for hf in range(2):
                    act.wait_ge(s["ln_h"], NT * (3 * l + 1) + 4 * hf + 4)
                    sc.activation(hT[:, hf, :], H[:, 4 * hf:4 * hf + 4, :].rearrange("p a b -> p (a b)"), ACT.Tanh,
                                  scale=0.5).then_inc(s["gate_tanh"], 1)

            neg_a(1)
            gate_tanh(0)
            for d in range(DT):
                conv_tanh(1, d)
            ln_tr_copy(1)
            step = iter(range(DS))
            for j in range(2 * NI):
                m = mlen(j // 2)
                act.wait_ge(s["f_mm"], j + 1)
                act.wait_ge(s["fsc_ready"], 1)
                if j >= 2:
                    act.wait_ge(s["f_hid"], 2 * (j - 1))
                sc.activation(fth[j % 2][0:m, :], ps[0:m, 2 * (j % 2), :], ACT.Tanh,
                              scale=fsc[0:m, 2, j // 2:j // 2 + 1]).then_inc(s["f_tanh"], 1)
                if j == PREP_XDBL:
                    xdbl_copy(1)
                if j == PREP_DT:
                    softplus(1)
                if j == PREP_DT + 1:
                    softplus_ln(1)
                if j in FFN_SSM_AT:
                    ssm_step(1, next(step))
            for n in step:
                if n < SSM1_IN_FFN:
                    ssm_step(1, n)
            ln_tr_copy(2, (0,))

            def job_sq(j):
                act.wait_ge(s["job_mm"], j + 1)
                if j:
                    act.wait_ge(s["job_sum"], j)
                k = job_bank(j)
                sc.activation(job_s(j), ps[:, k:k + 2, :], ACT.Square).then_inc(s["job_sq"], 1)

            def job_copy(b, i, x):
                j = JOB[b, i]
                dst = KT[b % 2] if i == 0 else QT[(4 * b + i - 1) % 2]
                act.wait_ge(s["job_tr_mm"], 2 * j + x + 1)
                if i == 0 and b >= 2:
                    act.wait_ge(s["s1_mm"], H1 * (b - 1))
                if i > 0 and 4 * b + i - 1 >= 2:
                    act.wait_ge(s["s1_mm"], 4 * (4 * b + i - 2))
                sc.copy(dst[:, 2 * x:2 * x + 2, :].rearrange("p a b -> p (a b)"), ps[:, 2, :]).then_inc(s["job_tr_copied"], 1)

            def v_copy(b):
                act.wait_ge(s["v_mm"], b + 1)
                if b >= 2:
                    act.wait_ge(s["pv1_mm"], H1 * (b - 1))
                k = v_bank(b)
                sc.copy(V1[b % 2], ps[:, k:k + 2, :]).then_inc(s["v_copied"], 1)

            def exp1(u):
                p = u % 2
                act.wait_ge(s["s1_max"], u + 1)
                if u >= 2:
                    act.wait_ge(s["pt1_mm"], u - 1)
                sc.activation(P1[p][:, 0:P], ps[:, 3 + p, 0:P], ACT.Exp, bias=nm1[:, p, 0:1],
                              accum_out=sum1[:, p, 0:1]).then_inc(s["s1_exp"], 1)
                sc.activation(P1[p][:, P:3 * P], ps[:, 3 + p, P:3 * P], ACT.Exp, bias=nm1[:, p, 1:2],
                              accum_out=sum1[:, p, 1:2]).then_inc(s["s1_exp"], 1)

            def pt_copy(u):
                act.wait_ge(s["pt1_mm"], u + 1)
                if u >= 2:
                    act.wait_ge(s["pv1_mm"], u - 1)
                sc.copy(PT1[u % 2], ps[:, 5, 0:3 * P]).then_inc(s["pt1_copied"], 1)

            def at_copy(u):
                act.wait_ge(s["pv1_mm"], u + 1)
                if u >= 2:
                    act.wait_ge(s["o1_mm"], u - 1)
                sc.copy(aT1[u % 2], ps[:, 6, 0:S]).then_inc(s["at1_copied"], 1)

            for kind, a in ATT1_PLAN:
                if kind == "vc":
                    v_copy(a)
                elif kind == "ln1":
                    ln_tr_copy(2, (1,))
                elif kind == "wo1":
                    act.wait_ge(s["fd_mm"], 4)
                    act.dma_start(WO1, io["wo1"]).then_inc(ld["wo1"], 16)
                elif kind == "sq":
                    job_sq(JOB[a])
                elif kind == "trc":
                    job_copy(*a)
                elif kind == "exp":
                    exp1(a)
                elif kind == "ptc":
                    pt_copy(a)
                elif kind == "at":
                    at_copy(a)
                elif kind == "da":
                    ssm_step(1, a)
            gate_tanh(1)
            ln_tr_copy(3)
            for hf in range(2):
                act.wait_ge(s["ln_tr_dve"], 6 + hf + 1)
                act.wait_ge(s["ln_tr_act"], 6 + hf + 1)
                z = slice(512 * hf, 512 * hf + 512)
                sc.copy(hTh[:, :, z], hT[:, :, z]).then_inc(s["h_hi"], 1)

            def w_high(x, src):
                sc.copy(Wh[:, x % WRING, :], src).then_inc(s["w_hi"], 1)

            def relu(p):
                sc.activation(MR[p], ps[:, 2 * p:2 * p + 2, :].rearrange("p a b -> p (a b)"), ACT.Relu).then_inc(s["m_relu"], 1)

            def hid_high(p):
                sc.copy(MHh[:, p, :], MH[p]).then_inc(s["m_hi"], 1)

            act.wait_ge(ld["shared"], 32)
            for x in range(2):
                w_high(x, WS[x])
            act.wait_ge(ld["route"], 32)
            sc.mul(BR, BR, -1.0).then_inc(s["r_bias"], 1)
            act.wait_ge(s["r_mm"], 1)
            act.wait_ge(s["r_bias"], 1)
            sc.activation(rET, ps[0:E, 4:6, :].rearrange("p a b -> p (a b)"), ACT.Exp, scale=-1.0, bias=BR).then_inc(s["r_exp"], 1)
            for x in range(2, 4):
                act.wait_ge(ld_we[x - 2], 16)
                w_high(x, WE[x - 2])
            for x in range(2):
                act.wait_ge(s["m_mm"], x + 1)
                relu(x)
                act.wait_ge(s["m_relu"], x + 1)
                sc.activation(MH[x], MR[x], ACT.Square).then_inc(s["m_sq"], 1)
                act.wait_ge(s["m_sq"], x + 1)
                hid_high(x)
            act.wait_ge(s["gt_mm"], 1)
            sc.copy(gT, ps[0:E, 2:4, :].rearrange("p a b -> p (a b)")).then_inc(s["gt_copied"], 1)
            act.wait_ge(s["gt_copied"], 1)
            act.dma_start(gate_dram, gT).then_inc(s["gate_stored"], 16)

            def expert(e, k, load_count, ahead=True, first=False):
                act.wait_ge(s["m_mm"], e + 3)
                if not first:
                    act.wait_ge(s["m_hid"], e - 1)
                relu(k % 2)
                act.wait_ge(s["m_out"], e + 1)
                if ahead:
                    act.wait_ge(ld_we[(k + 2) % WRING], load_count)
                    w_high(k, WE[(k + 2) % WRING])
                act.wait_ge(s["m_hid"], e + 1)
                hid_high(k % 2)

            for e in range(WRING):
                expert(e, e, 16 * ((e + 2) // WRING + 1), first=(e < 2))
            with act.Fori(1, E // WRING - 1, 1) as i:
                for k in range(WRING):
                    expert(WRING * i + k, k, 16 * i + (16 if k < 2 else 32))
            for e in range(E - WRING, E):
                expert(e, e % WRING, 16 * ((e + 2) // WRING + 1), ahead=(e + 2 < E))

        @block.vector
        def _(dve):
            v = nc.vector
            ch = Chain(dve, s["dve_chain"])

            def lw(l):
                dve.wait_ge(ld[f"pk{l}"], 48 - 16 * l)
                if l:
                    dve.wait_ge(s["conv_tanh"], DT)
                ch.step(v.tensor_scalar(cbh[:], pk[l][:, PK_CB:PK_CB + DT], 0.5, None, ALU.mult))
                w = pk[l][:, PK_IN:PK_IN + DI].unsqueeze(1).broadcast_to([P, DC, DI])
                ch.wait()
                v.tensor_tensor(LW[l], LW[l], w, ALU.mult).then_inc(s["lw_ready"], 1)

            def u_half(l):
                for d in range(DT):
                    dve.wait_ge(s["conv_tanh"], DT * l + d + 1)
                    c0 = CONV_BANK[l] + 2 * d
                    ch.step(v.tensor_scalar(DU[:, d, :], ps[:, c0:c0 + 2, :].rearrange("p a b -> p (a b)"),
                                            pk[l][:, PK_CB + d:PK_CB + d + 1], 0.5, ALU.add, ALU.mult))
                return ch.n

            def u_calc(l, mark):
                for d in range(DT):
                    ch.wait(mark - DT + 1 + d)
                    v.scalar_tensor_tensor(U[:, d, :], DEL[:, d, :], 1.0, DU[:, d, :], ALU.add, ALU.mult).then_inc(s["u_ready"], 1)

            def delta_max(l):
                for d in range(DT):
                    dve.wait_ge(s["sp_abs"], DT * l + d + 1)
                    c0 = CONV_BANK[l] + 2 * d
                    ch.step(v.tensor_scalar(DEL[:, d, :], ps[:, c0:c0 + 2, :].rearrange("p a b -> p (a b)"),
                                            pk[l][:, PK_DB + d:PK_DB + d + 1], 0.0, ALU.add, ALU.max))

            def delta_round(l):
                dve.wait_ge(s["sp_exp"], l + 1)
                ch.link(v.tensor_scalar(hS[1][:], hS[0][:], 1.0, None, ALU.add))
                ch.step(v.scalar_tensor_tensor(hS[1][:].rearrange("p a b -> p (a b)"), hS[1][:].rearrange("p a b -> p (a b)"), -1.0,
                                               hS[0][:].rearrange("p a b -> p (a b)"), ALU.add, ALU.subtract))

            def delta_sum(l):
                ch.wait()
                dve.wait_ge(s["sp_ln"], l + 1)
                ch.link(v.tensor_tensor(DEL[:], DEL[:], dA[1][:], ALU.add))
                ch.step(v.tensor_tensor(DEL[:], DEL[:], hS[1][:], ALU.subtract))

            def delta_u(l):
                ch.wait()
                ch.link(v.tensor_tensor(DU[:], DEL[:], U[:], ALU.mult))
                for d in range(DT):
                    last = v.tensor_scalar(ACC[:, d, :], U[:, d, :], skip[:, l, d:d + 1], None, ALU.mult)
                last.then_inc(s["delta_ready"], 1)

            def ssm_dbu(l, n):
                g = DS * l + n
                bcb, h = BCb[g % SB_LOADS], hS[g % 2]
                dve.wait_ge(ld_bc[g % SB_LOADS], 16 * (g // SB_LOADS + 1))
                if n == 0:
                    dve.wait_ge(s["delta_ready"], l + 1)
                if g >= 2:
                    dve.wait_ge(s["ssm_acc"], g - 1)
                v.tensor_tensor(h[:], DU[:], bcb[:, 0:1, :].broadcast_to([P, DT, T]), ALU.mult).then_inc(s["dbu_ready"], 1)

            def ssm_scan(l, n):
                g = DS * l + n
                bcb, h, a = BCb[g % SB_LOADS], hS[g % 2], dA[g % 2]
                dve.wait_ge(s["dbu_ready"], g + 1)
                dve.wait_ge(s["da_ready"], 2 * (g + 1))
                f = lambda z: z[:].rearrange("p d t -> p (d t)")
                v.tensor_tensor_scan(f(h), f(a), f(h), 0.0, ALU.mult, ALU.add).then_inc(s["scan_done"], 1)
                if n in C_ON_DVE[l]:
                    dve.wait_ge(s["scan_done"], g + 1)
                    v.tensor_tensor(h[:], h[:], bcb[:, 1:2, :].broadcast_to([P, DT, T]), ALU.mult).then_inc(s["c_dve"], 1)

            def ssm_step(l, n):
                ssm_dbu(l, n)
                ssm_scan(l, n)

            def ln_stats(L, hf):
                tiles = range(4 * hf, 4 * hf + 4)
                for t in tiles:
                    if L == 0:
                        dve.wait_ge(ld["x"], 16)
                    elif L == 4:
                        dve.wait_ge(s["x_new"], XN_FFN + t // 2 + 1)
                    else:
                        dve.wait_ge(s["x_new"], XN[L] - 1 + hf)
                    ch.step(v.bn_stats(lnst[:, t, :], X[:, t, :]))
                base = ch.n - 4
                for k, t in enumerate(tiles):
                    ch.wait(base + k + 1)
                    v.bn_aggr(lnmv[:, t, :], lnst[:, t, :]).then_inc(s["ln_mv"], 1)

            def ln_apply(L, hf):
                dve.wait_ge(s["ln_rstd"], 2 * L + hf + 1)
                for t in range(4 * hf, 4 * hf + 4):
                    v.tensor_scalar(H[:, t, :], X[:, t, :], lnmv[:, t, 0:1], lnrs[:, t:t + 1], ALU.subtract,
                                    ALU.mult).then_inc(s["ln_h"], 1)

            def ln_tr_copy(i, hf):
                dve.wait_ge(s["ln_tr_mm"], 4 * i + 2 * hf + 2)
                v.tensor_copy(hT[:, 1, 512 * hf:512 * hf + 512], ps[:, TR_BANK[i][hf] + 1, :]).then_inc(s["ln_tr_dve"], 1)

            def residual(bank0, ready, count, hf):
                dve.wait_ge(s[ready], count)
                x = X[:, 4 * hf:4 * hf + 4, :].rearrange("p t d -> p (t d)")
                v.tensor_tensor(x, x, ps[:, bank0 + 2 * hf:bank0 + 2 * hf + 2, :].rearrange("p a b -> p (a b)"),
                                ALU.add).then_inc(s["x_new"], 1)

            both = (0, 1)
            lw(0)
            for hf in both:
                ln_stats(0, hf)
            u_calc(0, u_half(0))
            for hf in both:
                ln_apply(0, hf)
            for hf in both:
                ln_tr_copy(0, hf)
            delta_max(0)
            delta_round(0)
            delta_sum(0)
            delta_u(0)

            dve.wait_ge(s["qkv0_copied"], NT)
            dve.wait_ge(ld["rope0"], 32)
            qk = Q0[:, :, 0:NQK0]
            tb = lambda a: a.rearrange("p (b h) n -> p b h n", h=2)
            ch.step(v.tensor_tensor(tb(RA), tb(qk), cos0.unsqueeze(1).broadcast_to([P, B, 2, NQK0]), ALU.mult))
            for hf in range(2):
                for x in range(2):
                    pick = lambda a, y: tb(a)[:, :, hf, :].rearrange("p b (n d) -> p b n d", d=D0)[:, :, :, 16 * y:16 * y + 16]
                    sn = sin0[:, hf, :].rearrange("p (n d) -> p n d", d=D0)[:, :, 16 * x:16 * x + 16]
                    ch.step(v.tensor_tensor(pick(RB, x), pick(qk, 1 - x), sn.unsqueeze(1).broadcast_to([P, B, H0 + KV0, 16]), ALU.mult))
            ch.wait()
            ch.link(v.tensor_tensor(qk, RA, RB, ALU.add))
            nh = NT * NQKV0 // D0
            q3 = Q0.rearrange("p t (n d) -> p (t n) d", d=D0)
            wide = lambda a: a.unsqueeze(2).broadcast_to([P, nh, D0])
            ch.link(v.tensor_reduce(st0[:, 0, :], q3, AX.X, ALU.add))
            ch.link(v.tensor_scalar(st0[:, 0, :], st0[:, 0, :], 1.0 / D0, None, ALU.mult))
            v.tensor_tensor(q3, q3, wide(st0[:, 0, :]), ALU.subtract).then_inc(s["rope0_rot"], 1)
            dve.wait_ge(s["rope0_sq"], 1)
            ch.link(v.tensor_reduce(st0[:, 1, :], SQ0.rearrange("p (n d) -> p n d", d=D0), AX.X, ALU.add))
            ch.link(v.tensor_scalar(st0[:, 1, :], st0[:, 1, :], 1.0 / D0, 1e-6, ALU.mult, ALU.add))
            ch.link(v.tensor_single_scalar(st0[:, 2, :].bitcast(I32), st0[:, 1, :].bitcast(I32), 1, ALU.arith_shift_right))
            ch.link(v.tensor_scalar(st0[:, 2, :].bitcast(I32), st0[:, 2, :].bitcast(I32), -1.0, float(0x5F3759DF), ALU.mult, ALU.add))
            for _ in range(4):
                ch.link(v.tensor_tensor(st0[:, 3, :], st0[:, 2, :], st0[:, 2, :], ALU.mult))
                ch.link(v.scalar_tensor_tensor(st0[:, 3, :], st0[:, 3, :], -0.5, st0[:, 1, :], ALU.mult, ALU.mult))
                ch.link(v.scalar_tensor_tensor(st0[:, 2, :], st0[:, 3, :], 1.5, st0[:, 2, :], ALU.add, ALU.mult))
            v.tensor_tensor(q3, q3, wide(st0[:, 2, :]), ALU.mult).then_inc(s["rope0_done"], 1)

            def at0(u):
                b, g = u // KV0, u % KV0
                dve.wait_ge(s["pv0_mm"], u + 1)
                ch.link(v.reciprocal(rden0, ps[:, 5, 0:S]))
                v.tensor_tensor(aT0[:, g, S * b:S * b + S], ps[:, 4, 0:S], rden0, ALU.mult).then_inc(s["at0_ready"], 1)

            for n in range(DS):
                ssm_step(0, n)
                if n % 2 == 1:
                    at0(n // 2)
            lw(1)
            for hf in both:
                residual(0, "o0_mm", hf + 1, hf)
                ln_stats(1, hf)

            def gate(l):
                dve.wait_ge(s["ssm_acc"], DS * (l + 1))
                for hf in both:
                    ln_apply(1 + 3 * l, hf)
                for hf in both:
                    dve.wait_ge(s["gate_tanh"], 2 * l + hf + 1)
                    flat = H[:, 4 * hf:4 * hf + 4, :].rearrange("p a b -> p (a b)")
                    ch.link(v.scalar_tensor_tensor(flat, hT[:, hf, :], 1.0, flat, ALU.add, ALU.mult))
                    for d in range(DT):
                        gt = H[:, 4 * hf:4 * hf + 4, :].rearrange("p (b h) n -> p b h n", h=2)[:, :, d, :]
                        a = bands(ACC[:, d, :])[:, 2 * hf:2 * hf + 2, :]
                        v.scalar_tensor_tensor(a, a, 0.5, gt, ALU.mult, ALU.mult).then_inc(s["gate_y"], 1)
                for hf in both:
                    residual(0, "gate_mm", 2 * l + hf + 1, hf)
                    ln_stats(2 + 3 * l, hf)

            gate(0)
            u1 = u_half(1)
            for hf in both:
                ln_apply(2, hf)
            for hf in both:
                ln_tr_copy(1, hf)
            u_calc(1, u1)
            dve.wait_ge(ld["ffn"], 48)
            ch.link(v.tensor_scalar(fsc[:, 2, :], fsc[:, 0, :], 0.5, None, ALU.mult))
            v.tensor_tensor(fsc[:, 1, :], fsc[:, 1, :], fsc[:, 2, :], ALU.mult).then_inc(s["fsc_ready"], 1)

            def w1_means():
                dve.wait_ge(ld["wqkv1"], 16)
                for c in range(HC):
                    ch.step(v.tensor_reduce(wmean[:, c, :], WB[:, c, 0:NQ1 + NK1].rearrange("p (h d) -> p h d", d=D1), AX.X, ALU.add))
                ch.wait()
                v.tensor_scalar(wmean[:], wmean[:], -1.0 / D1, None, ALU.mult).then_inc(s["w1_mean"], 1)

            def tables():
                dve.wait_ge(ld["rope1"], 32)
                for x in range(2):
                    row = lambda i: gains[:, 4 * x + i, :].unsqueeze(1).broadcast_to([P, 2, D1])
                    cs, sn = rope1[:, 2 * x, :, :], rope1[:, 2 * x + 1, :, :]
                    t = lambda i: tabs[:, 3 * x + i, :, :]
                    ch.step(v.tensor_tensor(t(0), cs, row(0), ALU.mult))
                    ch.step(v.tensor_tensor(t(1), sn, row(2), ALU.mult))
                    ch.step(v.tensor_tensor(t(2), cs, row(1), ALU.mult))
                    ch.link(v.tensor_tensor(sn, sn, row(3), ALU.mult))
                    last = v.tensor_tensor(t(2), t(2), sn, ALU.add)
                    ch.step(last)
                ch.wait()

            step = iter(range(DS))
            for j in range(2 * NI):
                m, i, hf = mlen(j // 2), j // 2, j % 2
                dve.wait_ge(s["fsc_ready"], 1)
                dve.wait_ge(s["f_tanh"], j + 1)
                v.scalar_tensor_tensor(ft1[j % 2][0:m, :], fth[j % 2][0:m, :], 1.0, ps[0:m, 2 * (j % 2), :], ALU.add,
                                       ALU.mult).then_inc(s["f_hid"], 1)
                dve.wait_ge(s["f_hid"], 2 * j + 1)
                v.scalar_tensor_tensor(hid0[0:m, i, 512 * hf:512 * hf + 512], ps[0:m, 2 * (j % 2) + 1, :], fsc[0:m, 1, i:i + 1],
                                       ft1[j % 2][0:m, :], ALU.mult, ALU.mult).then_inc(s["f_hid"], 1)
                if j == 1:
                    w1_means()
                if j == PREP_DT:
                    delta_max(1)
                if j == PREP_DT + 1:
                    delta_round(1)
                if j == PREP_DT + 2:
                    delta_sum(1)
                if j == PREP_DT + 3:
                    delta_u(1)
                if j == 10:
                    tables()
                if j in FFN_SSM_AT:
                    ssm_step(1, next(step))
            for n in step:
                if n < SSM1_IN_FFN:
                    ssm_step(1, n)
            residual(4, "fd_mm", 2, 0)
            ln_stats(3, 0)
            ln_apply(3, 0)
            ln_tr_copy(2, 0)
            residual(4, "fd_mm", 4, 1)
            ln_stats(3, 1)
            ln_apply(3, 1)

            def job(b, i):
                j, x = JOB[b, i], 0 if i else 1
                k = job_bank(j)
                pj = ps[:, k:k + 2, :].rearrange("p t (h d) -> p t h d", d=D1)
                bc = lambda a: a.unsqueeze(2).broadcast_to([P, 2, REP1, a.shape[-1]])
                h4 = lambda a: a.rearrange("p t (h d) -> p t h d", d=D1)
                dve.wait_ge(s["job_sq"], j + 1)
                if j > 1:
                    dve.wait_ge(s["job_rope"], 8 * j)
                hd = D1 // 2
                v.tensor_tensor(h4(job_a(j)), pj, bc(tabs[:, 3 * x, :, :]), ALU.mult).then_inc(s["job_rot"], 1)
                for y in range(2):
                    v.tensor_tensor(h4(job_b(j))[:, :, :, hd * y:hd * y + hd], pj[:, :, :, hd * (1 - y):hd * (1 - y) + hd],
                                    bc(tabs[:, 3 * x + 1, :, hd * y:hd * y + hd]), ALU.mult).then_inc(s["job_rot"], 1)

            def job_sum(b, i):
                j = JOB[b, i]
                if j >= 2:
                    dve.wait_ge(s["job_rope"], 8 * (j - 1))
                dve.wait_ge(s["job_sq"], j + 1)
                v.tensor_reduce(jst[:, j % 2, 0, :], job_s(j).rearrange("p t (h d) -> p (t h) d", d=D1), AX.X, ALU.add).then_inc(s["job_sum"], 1)

            def job_rope(b, i):
                j, x = JOB[b, i], 0 if i else 1
                dve.wait_ge(s["job_add"], j + 1)
                dve.wait_ge(s["job_rstd"], j + 1)
                if j:
                    dve.wait_ge(s["job_tr_mm"], 2 * j)
                for t in range(2):
                    for h in range(REP1):
                        c = slice(D1 * h, D1 * h + D1)
                        v.scalar_tensor_tensor(R[:, t, c], job_a(j)[:, t, c], jst[:, j % 2, 2, REP1 * t + h:REP1 * t + h + 1],
                                               tabs[:, 3 * x + 2, t, :], ALU.mult, ALU.add).then_inc(s["job_rope"], 1)

            def max1(u):
                p = u % 2
                dve.wait_ge(s["s1_mm"], u + 1)
                if u >= 2:
                    dve.wait_ge(s["s1_exp"], 2 * (u - 1))
                ch.step(v.tensor_reduce(nm1[:, p, 0:1], ps[:, 3 + p, 0:P], AX.X, ALU.max, negate=True))
                v.tensor_reduce(nm1[:, p, 1:2], ps[:, 3 + p, P:3 * P], AX.X, ALU.max, negate=True).then_inc(s["s1_max"], 1)

            def norm1(u):
                p = u % 2
                dve.wait_ge(s["s1_exp"], 2 * (u + 1))
                ch.link(v.reciprocal(rc1[:, p, :], sum1[:, p, :]))
                v.tensor_scalar(P1[p][:, 0:P], P1[p][:, 0:P], rc1[:, p, 0:1], None, ALU.mult).then_inc(s["s1_norm"], 1)
                v.tensor_scalar(P1[p][:, P:3 * P], P1[p][:, P:3 * P], rc1[:, p, 1:2], None, ALU.mult).then_inc(s["s1_norm"], 1)

            for kind, a in ATT1_PLAN:
                if kind == "rot":
                    job(*a)
                elif kind == "ln1":
                    ln_tr_copy(2, 1)
                elif kind == "sum":
                    job_sum(*a)
                elif kind == "rope":
                    job_rope(*a)
                elif kind == "max":
                    max1(a)
                elif kind == "norm":
                    norm1(a)
                elif kind == "dbu":
                    ssm_dbu(1, a)
                elif kind == "scan":
                    ssm_scan(1, a)
                elif kind == "res":
                    dve.wait_ge(s["o1_mm"], H1 * (a + 1))
                    x = X[:, 2 * a:2 * a + 2, :].rearrange("p t d -> p (t d)")
                    v.tensor_tensor(x, x, ps[:, 7, :], ALU.add).then_inc(s["x_new"], 1)
            for hf in both:
                ln_stats(4, hf)
            gate(1)
            for hf in both:
                ln_apply(5, hf)
            for hf in both:
                ln_tr_copy(3, hf)

            z = slice(0, 512)
            dve.wait_ge(s["h_hi"], 1)
            v.tensor_tensor(hTl[:, :, z], hT[:, :, z], hTh[:, :, z].bitcast(F32), ALU.subtract).then_inc(s["h_lo_dve"], 1)

            for z in (rGW, rMS, rT8, rE8):
                ch.step(v.memset(z, -1.0))
            dve.wait_ge(s["r_tr"], 1)
            v.tensor_scalar(rS, ps[:, 6, 0:NT * E].rearrange("p (t e) -> p t e", t=NT), 1.0, None, ALU.add).then_inc(s["r_sum"], 1)
            dve.wait_ge(s["r_sum"], 1)
            ch.link(v.reciprocal(rS, rS))
            q4 = rS.rearrange("p t (g e) -> p (t g) e", e=EPG)
            col = lambda i: q4[:, :, i]
            ch.step(v.tensor_tensor(rg[0], col(0), col(1), ALU.max))
            ch.step(v.tensor_tensor(rg[1], col(0), col(1), ALU.min))
            ch.step(v.tensor_tensor(rg[2], col(2), col(3), ALU.max))
            ch.link(v.tensor_tensor(rg[3], col(2), col(3), ALU.min))
            ch.step(v.tensor_tensor(rg[4], rg[0], rg[2], ALU.max))
            ch.step(v.tensor_tensor(rg[5], rg[0], rg[2], ALU.min))
            ch.link(v.tensor_tensor(rg[1], rg[1], rg[3], ALU.max))
            ch.link(v.tensor_tensor(rg[1], rg[1], rg[5], ALU.max))
            ch.link(v.tensor_tensor(rGW[:, :, 0:G], rg[4].rearrange("p (t g) -> p t g", g=G),
                                    rg[1].rearrange("p (t g) -> p t g", g=G), ALU.add))
            for t in range(NT):
                ch.step(v.max(rM8[:, t, :], rGW[:, t, 0:G]))
            ch.wait()
            ch.link(v.tensor_copy(rT8[:, :, 0:KG], rM8[:, :, 0:KG]))
            for t in range(NT):
                ch.step(v.match_replace(rGM[:, t, :], rT8[:, t, :], rGW[:, t, :], -2.0))
            ch.wait()
            ch.link(v.tensor_scalar(rGM, rGM, -2.0, None, ALU.is_equal))
            ch.link(v.tensor_tensor(rW.rearrange("p t (g e) -> p t g e", e=EPG), rS.rearrange("p t (g e) -> p t g e", e=EPG),
                                    rGM[:, :, 0:G].unsqueeze(3).broadcast_to([P, NT, G, EPG]), ALU.mult))
            ch.link(v.tensor_copy(rMS[:, :, 0:E], rW))
            for t in range(NT):
                ch.step(v.max(rM8[:, t, :], rMS[:, t, 0:E]))
            ch.wait()
            ch.link(v.tensor_copy(rE8[:, :, 0:K], rM8[:, :, 0:K]))
            for t in range(NT):
                ch.step(v.match_replace(rME[:, t, :], rE8[:, t, :], rMS[:, t, :], -2.0))
            ch.wait()
            ch.link(v.tensor_scalar(rME, rME, -2.0, None, ALU.is_equal))
            ch.link(v.tensor_tensor(rW, rS, rME[:, :, 0:E], ALU.mult))
            ch.link(v.tensor_reduce(rsum[:, 0, :], rW, AX.X, ALU.add))
            ch.link(v.tensor_scalar(rsum[:, 0, :], rsum[:, 0, :], 1e-20, None, ALU.add))
            ch.link(v.reciprocal(rsum[:, 1, :], rsum[:, 0, :]))
            ch.link(v.tensor_tensor(rW, rW, rsum[:, 1, :].unsqueeze(2).broadcast_to([P, NT, E]), ALU.mult))
            v.tensor_scalar(rGate, rW, ROUTE_SCALE, None, ALU.mult).then_inc(s["r_gate"], 1)
            with dve.Fori(0, E // WRING, 1) as i:
                for k in range(WRING):
                    p = k % 2
                    f = ps[:, 2 * p:2 * p + 2, :].rearrange("p a b -> p (a b)")
                    dve.wait_ge(ld_gb[k], 16 * i + 16)
                    dve.wait_ge(s["m_relu"], WRING * i + (k + 3))
                    v.scalar_tensor_tensor(MG[p], f, 0.0, GB[k], ALU.max, ALU.mult).then_inc(s["m_gated"], 1)
                    dve.wait_ge(s["m_gated"], WRING * i + (k + 1))
                    dve.wait_ge(s["m_lo"], WRING * i + (k + 1))
                    v.tensor_tensor(MH[p], MG[p], MR[p], ALU.mult).then_inc(s["m_hid"], 1)
            for hf in both:
                residual(4, "m_out", E + 2, hf)

        @block.tensor
        def _(pe):
            mm, tr = nc.tensor.matmul, nc.tensor.transpose

            def conv(l):
                pe.wait_ge(s["lw_ready"], l + 1)
                pe.wait_ge(ld["ctx"], 16)
                for d in range(DT):
                    for hf in range(2):
                        for k in range(DC):
                            last = mm(ps[:, CONV_BANK[l] + 2 * d + hf, :], LW[l][:, k, P * d:P * d + P], ctxp[:, 2 * hf:2 * hf + 2, k:k + S],
                                      start=(k == 0), stop=(k == DC - 1))
                    last.then_inc(s["conv_mm"], 1)

            def xdbl(l):
                pe.wait_ge(s["u_ready"], DT * (l + 1))
                xp = pk[l][:, PK_X:PK_N].rearrange("p (d n) -> p d n", d=DT)
                for bank, c0, n in ((0, 0, DR), (2, DR, 2 * DS)):
                    for hf in range(2):
                        for d in range(DT):
                            last = mm(ps[0:n, CONV_BANK[l] + bank + hf, :], xp[:, d, c0:c0 + n], U[:, d, 512 * hf:512 * hf + 512],
                                      start=(d == 0), stop=(d == DT - 1))
                    last.then_inc(s["xdbl_mm"], 1)

            def dtpre(l):
                pe.wait_ge(s["dt_low_copied"], l + 1)
                pe.wait_ge(s["bc_copied"], l + 1)
                for d in range(DT):
                    for hf in range(2):
                        last = mm(ps[:, CONV_BANK[l] + 2 * d + hf, :], dtw[l][:, P * d:P * d + P], dA[0][0:DR, 0, 512 * hf:512 * hf + 512],
                                  start=True, stop=True)
                    last.then_inc(s["dtpre_mm"], 1)

            def ln_tr(i, halves=(0, 1)):
                L = TR_LNS[i]
                for hf in halves:
                    pe.wait_ge(s["ln_h"], NT * L + 4 * hf + 4)
                    for c in range(HC):
                        for t in range(4):
                            last = tr(ps[:, TR_BANK[i][hf] + c, P * t:P * t + P], H[:, 4 * hf + t, P * c:P * c + P], ident[:])
                        last.then_inc(s["ln_tr_mm"], 1)

            def ln_ready(i, hf):
                pe.wait_ge(s["ln_tr_act"], 2 * i + hf + 1)
                pe.wait_ge(s["ln_tr_dve"], 2 * i + hf + 1)

            conv(0)
            pe.wait_ge(ld["ident"], 16)
            ln_tr(0)
            xdbl(0)
            pe.wait_ge(ld["wqkv0"], 16)
            dtpre(0)
            for t in range(NT):
                ln_ready(0, 1)
                if t >= 4:
                    pe.wait_ge(s["qkv0_copied"], t - 3)
                for c in range(HC):
                    last = mm(ps[:, 4 + t % 4, 0:NQKV0], hT[:, c, P * t:P * t + P], WQKV0[:, c, :], start=(c == 0), stop=(c == HC - 1))
                last.then_inc(s["qkv0_mm"], 1)
            pe.wait_ge(s["rope0_done"], 1)
            for i in range(8):
                g, part, hf = i // 4, (i // 2) % 2, i % 2
                pe.wait_ge(s["tr0_copied"], i - 3) if i >= 4 else pe.wait_ge(s["qkv0_copied"], NT)
                for t in range(4):
                    tile = Q0[:, 4 * hf + t, :]
                    if part == 0:
                        src = tile[:, P * g:P * g + P]
                    else:
                        pe.wait_ge(s["k4_ready"], g + 1)
                        src = K40[:, 4 * hf + t, g, :]
                    last = tr(ps[:, 4 + i % 4, P * t:P * t + P], src, ident[:])
                last.then_inc(s["tr0_mm"], 1)
            pe.wait_ge(ld["masks"], 48)
            pe.wait_ge(s["delta_ready"], 1)

            def s0(u):
                b, g = u // KV0, u % KV0
                pe.wait_ge(s["tr0_copied"], 4 * g + 4)
                if u:
                    pe.wait_ge(s["s0_tanh"], u)
                q0 = S * b
                for r in range(REP0):
                    rows = slice(D0 * r, D0 * r + D0)
                    mm(ps[:, r, 0:W0 + P], identb[:], mask0[:], start=True, stop=True, skip_group_check=True)
                    mm(ps[:, r, 0:W0], kT0[rows, g, q0:q0 + P], qT0[rows, g, q0:q0 + W0], start=False, stop=True, skip_group_check=True)
                    last = mm(ps[:, r, W0:W0 + P], kT0[rows, g, q0 + P:q0 + S], qT0[rows, g, q0 + P:q0 + S], start=False, stop=True,
                              skip_group_check=True)
                last.then_inc(s["s0_mm"], 1)

            def pv0(u):
                b, g = u // KV0, u % KV0
                pe.wait_ge(s["s0_exp"], 2 * (u + 1))
                pe.wait_ge(s["init"], 3)
                pe.wait_ge(s["at0_ready"], u) if u else pe.wait_ge(s["tr0_copied"], 8)
                vc = NQK0 + D0 * g
                for r in range(REP0):
                    for kb_ in range(2):
                        w = PT0[u % 2][:, r, kb_, :]
                        mm(ps[D0 * r:D0 * r + D0, 4, 0:S], Q0[:, 2 * b + kb_, vc:vc + D0], w, start=(kb_ == 0), stop=(kb_ == 1))
                        last = mm(ps[D0 * r:D0 * r + D0, 5, 0:S], ones32[:], w, start=(kb_ == 0), stop=(kb_ == 1))
                last.then_inc(s["pv0_mm"], 1)

            s0(0)
            for u in range(B * KV0):
                if u + 1 < B * KV0:
                    s0(u + 1)
                pv0(u)
            pe.wait_ge(ld["wo0"], 16)
            pe.wait_ge(s["s0_tanh"], B * KV0)
            pe.wait_ge(s["at0_ready"], B * KV0)
            for t in range(NT):
                for g in range(KV0):
                    last = mm(ps[:, t // 2, 256 * (t % 2):256 * (t % 2) + 256], aT0[:, g, P * t:P * t + P], WO0[:, g, :],
                              start=(g == 0), stop=(g == KV0 - 1))
                if t % 4 == 3:
                    last.then_inc(s["o0_mm"], 1)

            def gate_tr(l):
                for hf in range(2):
                    pe.wait_ge(s["gate_y"], 2 * DT * l + DT * (hf + 1))
                    for t in range(4 * hf, 4 * hf + 4):
                        for d in range(DT):
                            last = tr(ps[:, t // 2, 256 * (t % 2) + P * d:256 * (t % 2) + P * d + P], ACC[:, d, P * t:P * t + P], ident[:])
                    last.then_inc(s["gate_mm"], 1)

            conv(1)
            pe.wait_ge(s["x_new"], XN_ATT0)
            gate_tr(0)
            ln_tr(1)
            pe.wait_ge(ld["ffn"], 48)
            for j in range(2 * NI):
                m, i, hf = mlen(j // 2), j // 2, j % 2
                ln_ready(1, min(j, 1))
                if j >= 2:
                    pe.wait_ge(s["f_hid"], 2 * (j - 1))
                for x in range(2):
                    for c in range(HC):
                        last = mm(ps[0:m, 2 * (j % 2) + x, :], WGU[:, c, INTER * x + P * i:INTER * x + P * i + m],
                                  hT[:, c, 512 * hf:512 * hf + 512], start=(c == 0), stop=(c == HC - 1))
                last.then_inc(s["f_mm"], 1)
                if j == PREP_XDBL:
                    xdbl(1)
                if j == PREP_DT:
                    dtpre(1)
            pe.wait_ge(s["delta_ready"], 2)
            pe.wait_ge(s["f_hid"], 4 * NI)
            pe.wait_ge(s["wdn_ready"], NI)
            for t in range(NT):
                for i in range(NI):
                    m = mlen(i)
                    last = mm(ps[:, 4 + t // 2, 256 * (t % 2):256 * (t % 2) + 256], hid0[0:m, i, P * t:P * t + P], WDN[0:m, i, :],
                              start=(i == 0), stop=(i == NI - 1))
                if t % 2 == 1:
                    last.then_inc(s["fd_mm"], 1)
            ln_tr(2, (0,))
            ln_ready(2, 0)
            pe.wait_ge(s["w1_centered"], HC)

            def project(b, c0, bank):
                if b == B // 2:
                    ln_ready(2, 1)
                for t in range(2):
                    for c in range(HC):
                        last = mm(ps[:, bank + t, :], hT[:, c, P * (2 * b + t):P * (2 * b + t) + P], WB[:, c, c0:c0 + 512],
                                  start=(c == 0), stop=(c == HC - 1))
                return last

            def v_job(b):
                if b == 0:
                    ln_ready(2, 1)
                if b:
                    pe.wait_ge(s["job_rot"], 3 * V_AFTER[b])
                    pe.wait_ge(s["job_sq"], V_AFTER[b])
                project(b, NQ1 + NK1, v_bank(b)).then_inc(s["v_mm"], 1)

            def rope_job(b, i):
                j = JOB[b, i]
                if any(k <= j for k in V_AFTER[1:]):
                    pe.wait_ge(s["v_copied"], sum(k <= j for k in V_AFTER))
                if j == 1:
                    pe.wait_ge(s["x_new"], XN_FFN)
                if j > 1:
                    pe.wait_ge(s["job_rot"], 3 * j)
                    pe.wait_ge(s["job_sq"], j)
                project(b, NQ1 if i == 0 else NK1 * (i - 1), job_bank(j)).then_inc(s["job_mm"], 1)

            def job_tr(b, i, x):
                j = JOB[b, i]
                pe.wait_ge(s["job_rope"], 8 * (j + 1))
                if j == 0:
                    ln_ready(2, 1)
                if j or x:
                    pe.wait_ge(s["job_tr_copied"], 2 * j + x)
                for h in range(2):
                    for t in range(2):
                        last = tr(ps[:, 2, S * h + P * t:S * h + P * t + P], R[:, t, D1 * (2 * x + h):D1 * (2 * x + h) + D1], ident[:])
                last.then_inc(s["job_tr_mm"], 1)

            def s1(u):
                b, h = u // H1, u % H1
                g, p = h // REP1, u % 2
                pe.wait_ge(s["job_tr_copied"], 2 * max(JOB[b, 0], JOB[b, 1 + g]) + 2)
                if u < 2:
                    pe.wait_ge(s["v_copied"], 1)
                else:
                    pe.wait_ge(s["s1_exp"], 2 * (u - 1))
                q, k = QT[(4 * b + g) % 2], KT[b % 2]
                mm(ps[:, 3 + p, 0:3 * P], identb[:], mask1[:], start=True, stop=True, skip_group_check=True)
                mm(ps[:, 3 + p, 0:P], q[:, h % REP1, 0:P], k[:, g, 0:P], start=False, stop=True, skip_group_check=True)
                mm(ps[:, 3 + p, P:3 * P], q[:, h % REP1, P:S], k[:, g, :], start=False, stop=True, skip_group_check=True).then_inc(s["s1_mm"], 1)

            def pt1(u):
                pe.wait_ge(s["s1_norm"], 2 * (u + 1))
                if u:
                    pe.wait_ge(s["pt1_copied"], u)
                for x in range(3):
                    last = tr(ps[:, 5, P * x:P * x + P], P1[u % 2][:, P * x:P * x + P], ident[:])
                last.then_inc(s["pt1_mm"], 1)

            def pv1(u):
                b, h = u // H1, u % H1
                g = h // REP1
                pe.wait_ge(s["pt1_copied"], u + 1)
                pe.wait_ge(s["v_copied"], b + 1)
                if u:
                    pe.wait_ge(s["at1_copied"], u)
                va = V1[b % 2]
                mm(ps[:, 6, 0:S], va[:, 0, D1 * g:D1 * g + D1], PT1[u % 2][:, 0:S], start=True, stop=True, skip_group_check=True)
                mm(ps[:, 6, P:S], va[:, 1, D1 * g:D1 * g + D1], PT1[u % 2][:, S:3 * P], start=False, stop=True,
                   skip_group_check=True).then_inc(s["pv1_mm"], 1)

            def o1(u):
                b, h = u // H1, u % H1
                pe.wait_ge(s["at1_copied"], u + 1)
                if u == 0:
                    pe.wait_ge(ld["wo1"], 16)
                if h == 0 and b:
                    pe.wait_ge(s["x_new"], XN_FFN + b)
                for t in range(2):
                    last = mm(ps[:, 7, 256 * t:256 * t + 256], aT1[u % 2][:, P * t:P * t + P], WO1[:, h, :], start=(h == 0 and t == 0),
                              stop=(h == H1 - 1), skip_group_check=True)
                last.then_inc(s["o1_mm"], 1)

            for kind, a in ATT1_PLAN:
                if kind == "v":
                    v_job(a)
                elif kind == "ln1":
                    ln_tr(2, (1,))
                elif kind == "proj":
                    rope_job(*a)
                elif kind == "tr":
                    job_tr(*a)
                elif kind == "s":
                    s1(a)
                elif kind == "pt":
                    pt1(a)
                elif kind == "pv":
                    pv1(a)
                elif kind == "o":
                    o1(a)
            gate_tr(1)
            ln_tr(3)
            pe.wait_ge(ld["route"], 32)
            for hf in range(2):
                ln_ready(3, hf)
                for c in range(HC):
                    last = mm(ps[0:E, 4 + hf, :], WRT[:, c, :], hT[:, c, 512 * hf:512 * hf + 512], start=(c == 0), stop=(c == HC - 1))
            last.then_inc(s["r_mm"], 1)

            def in_parts(out, wh, wl, xh, xl, start, stop, **kw):
                mm(out, wh, xh, start=start, stop=False, **kw)
                mm(out, wh, xl, start=False, stop=False, **kw)
                return mm(out, wl, xh, start=False, stop=stop, **kw)

            def w1(p, slot):
                for hf in range(2):
                    z = slice(512 * hf, 512 * hf + 512)
                    for c in range(HC):
                        m = slice(M * c, M * c + M)
                        last = in_parts(ps[:, 2 * p + hf, :], Wh[:, slot, m], Wl[:, slot, m], hTh[:, c, z], hTl[:, c, z],
                                        start=(c == 0), stop=(c == HC - 1))
                last.then_inc(s["m_mm"], 1)

            def w2(p, slot, first=False, final=False):
                w = slice(HC * M, HC * M + HID)
                for t in range(NT):
                    z = slice(P * t, P * t + P)
                    last = in_parts(ps[:, 4 + t // 2, 256 * (t % 2):256 * (t % 2) + 256], MHh[:, p, z], MHl[:, p, z],
                                    Wh[:, slot, w], Wl[:, slot, w], start=(first and t % 2 == 0), stop=final, skip_group_check=True)
                last.then_inc(s["m_out"], 1)

            pe.wait_ge(s["h_lo_dve"], 1)
            pe.wait_ge(s["h_lo_pool"], 1)
            pe.wait_ge(s["w_lo"], 1)
            w1(0, 0)
            pe.wait_ge(s["r_exp"], 1)
            for t in range(NT):
                last = tr(ps[:, 6, E * t:E * t + E], rET[:, P * t:P * t + P], ident[0:E, 0:E])
            last.then_inc(s["r_tr"], 1)
            pe.wait_ge(s["w_lo"], 2)
            w1(1, 1)
            pe.wait_ge(s["m_lo"], 1)
            pe.wait_ge(s["r_sum"], 1)
            w2(0, 0, first=True)
            pe.wait_ge(s["w_lo"], 3)
            w1(0, 2)
            pe.wait_ge(s["m_lo"], 2)
            w2(1, 1)
            pe.wait_ge(s["r_gate"], 1)
            for t in range(NT):
                last = tr(ps[0:E, 2 + t // 4, P * (t % 4):P * (t % 4) + P], rGate[:, t, :], ident[:])
            last.then_inc(s["gt_mm"], 1)
            pe.wait_ge(s["gt_copied"], 1)
            pe.wait_ge(s["w_lo"], 4)
            w1(1, 3)
            with pe.Fori(0, E // WRING - 1, 1) as i:
                for k in range(WRING):
                    pe.wait_ge(s["w_lo"], WRING * i + (k + 5))
                    pe.wait_ge(s["m_gated"], WRING * i + (k + 1))
                    w1(k % 2, k)
                    pe.wait_ge(s["m_lo"], WRING * i + (k + 3))
                    w2(k % 2, (k + 2) % WRING)
            for e in range(E - WRING, E):
                if e + 2 < E:
                    pe.wait_ge(s["w_lo"], e + 5)
                    pe.wait_ge(s["m_gated"], e + 1)
                    w1(e % 2, e % WRING)
                pe.wait_ge(s["m_lo"], e + 3)
                w2(e % 2, (e + 2) % WRING, final=(e == E - 1))


SSM1_IN_FFN = 3
FFN_SSM_AT = [10]
PREP_XDBL, PREP_DT = 1, 3


def att1_plan():
    units = B * H1
    parts = {}

    def at(slot, *p):
        parts.setdefault(slot, []).append(p)

    def rope_job(slot, b, i):
        at(slot, "proj", (b, i))
        at(slot, "sq", (b, i))
        at(slot + 1, "rot", (b, i))
        at(slot + 1, "sum", (b, i))
        at(slot + 3, "rope", (b, i))
        for x in range(2):
            at(slot + 4, "tr", (b, i, x))
            at(slot + 4, "trc", (b, i, x))

    def v_job(slot, b):
        at(slot, "v", b)
        at(slot, "vc", b)

    rope_job(-8, 0, 0)
    rope_job(-7, 0, 1)
    at(-7, "wo1", 0)
    at(-6, "ln1", 0)
    v_job(-5, 0)
    for b in range(B):
        for g in range(KV1):
            u = H1 * b + REP1 * g
            if b or g:
                rope_job(u - 6, b, g + 1)
        if b + 1 < B:
            rope_job(H1 * b + REP1, b + 1, 0)
            v_job(H1 * b + 2 * REP1, b + 1)
    cost = {"rot": 2.4, "sum": 1.2, "rope": 1.7, "dbu": 2.2, "scan": 2.2}
    ssm = []
    for n in range(SSM1_IN_FFN, DS):
        ssm += [("da", n), ("dbu", n), ("scan", n)]
    price = lambda p: cost.get(p[0], 0) * (2 if p[0] == "scan" and p[1] in C_ON_DVE[1] else 1)
    total = sum(price(p) for u in range(units) for p in parts.get(u, [])) + sum(price(p) for p in ssm)
    plan = []
    spent = 0.0
    ok = lambda q: 0 <= q < units
    for u in range(min(parts), units + 4):
        mine = parts.get(u, [])
        pick = lambda *kinds: [p for kind in kinds for p in mine if p[0] == kind]
        tr, trc = pick("tr"), pick("trc")
        if ok(u - 4) and (u - 4) % H1 == H1 - 1:
            plan.append(("res", (u - 4) // H1))
        if ok(u + 1) or u == -1:
            plan.append(("s", u + 1))
        plan += tr[:1] + trc[:1]
        if ok(u):
            plan += [("max", u), ("exp", u)]
        if ok(u - 1):
            plan.append(("norm", u - 1))
        if ok(u - 2):
            plan += [("pv", u - 2), ("at", u - 2)]
        if ok(u - 3):
            plan.append(("o", u - 3))
        plan += tr[1:] + trc[1:]
        plan += pick("ln1", "v", "vc", "proj")
        if ok(u - 1):
            plan += [("pt", u - 1), ("ptc", u - 1)]
        plan += pick("sq", "wo1", "rope", "rot", "sum")
        if ok(u):
            spent += sum(price(p) for p in mine)
            while ssm and spent + price(ssm[0]) / 2 < total * (u + 1) / (0.9 * units):
                spent += price(ssm[0])
                plan.append(ssm.pop(0))
    return plan + ssm


ATT1_PLAN = att1_plan()
JOB = {a: j for j, a in enumerate(a for kind, a in ATT1_PLAN if kind == "proj")}
V_AFTER = [sum(kind == "proj" for kind, a in ATT1_PLAN[:ATT1_PLAN.index(("v", b))]) for b in range(B)]

_ORDER = ["x", "ctxp", "pk0", "pk1", "dtw0", "dtw1", "ident", "identb", "mask0", "mask1", "cos0", "sin0", "rope1", "gains",
          "wqkv0", "wo0", "ffn", "wdn", "skip", "fsc", "dsc", "wqkv1", "wo1", "we", "wrt", "br"]


def _layout(i):
    bf16 = mybir.dt.np(BF16)
    f = np.float32
    a = {k: np.asarray(v) for k, v in i.items()}
    o = {"x": a["x"]}
    c = np.zeros((P, B, S + DC - 1), f)
    c[:, :, DC - 1:] = a["ctx_1024"].transpose(2, 0, 1)
    o["ctxp"] = c
    chan = lambda z: z.reshape(DT, P, -1).transpose(1, 0, 2).reshape(P, -1)
    rows = lambda z: np.broadcast_to(z.reshape(1, -1), (P, z.size))
    for l in range(2):
        q = lambda n: a[f"L{l}_xattn_{n}"]
        cw = q("conv_w").reshape(DI, DC)
        xp = q("x_proj_w")
        order = list(range(DR)) + [DR + DS * r + n for n in range(DS) for r in range(2)]
        o[f"pk{l}"] = np.concatenate([q("in_proj_w").T, rows(cw.T), chan(q("conv_b")), chan(q("dt_proj_b")),
                                      chan(q("A_log")), chan(xp[order].T)], 1)
        o[f"dtw{l}"] = q("dt_proj_w").T
    wt = lambda w: w.T.reshape(-1, P, w.shape[0]).transpose(1, 0, 2)
    o["wqkv0"] = wt(np.concatenate([a["L0_attn_Wq"], a["L0_attn_Wk"], a["L0_attn_Wv"]], 0))
    o["wo0"] = wt(a["L0_attn_Wo"])
    gu = wt(np.concatenate([a["L0_ffn_gate_w"], a["L0_ffn_up_w"]], 0)).reshape(P, -1)
    dn = np.zeros((NI * P, HID), f)
    dn[:INTER] = a["L0_ffn_down_w"].T
    o["ffn"], o["wdn"] = gu, dn.reshape(NI, P, HID).transpose(1, 0, 2)
    o["skip"] = np.stack([chan(a[f"L{l}_xattn_D"]) for l in range(2)], 1)
    sc = np.zeros((2, NI * P), f)
    sc[0, :INTER], sc[1, :INTER] = a["L0_ffn_gate_s"], a["L0_ffn_up_s"]
    o["fsc"] = sc.reshape(2, NI, P).transpose(2, 0, 1)
    o["dsc"] = rows(a["L0_ffn_down_s"])
    o["wqkv1"] = wt(a["L1_attn_w_qkv"])
    o["wo1"] = wt(a["L1_attn_w_o"])
    w1 = np.concatenate([a["L1_ffn_W1"], a["L1_ffn_Ws1"].reshape(2, M, HID)], 0)
    w2 = np.concatenate([a["L1_ffn_W2"], a["L1_ffn_Ws2"].reshape(HID, 2, M).transpose(1, 0, 2)], 0)
    w1 = w1.transpose(0, 2, 1).reshape(E + 2, HC, P, M).transpose(0, 2, 1, 3).reshape(E + 2, P, HC * M)
    o["we"] = np.concatenate([w1, w2.transpose(0, 2, 1)], 2)
    o["wrt"] = wt(a["L1_ffn_Wr"])
    o["br"] = a["L1_ffn_br"].reshape(E, 1)
    g = [a["L1_attn_" + n] for n in ("qn_g", "qn_b", "kn_g", "kn_b")]
    sw = lambda z: np.concatenate([z[D1 // 2:], z[:D1 // 2]])
    o["gains"] = np.stack([rows(z) for z in (g[0], g[1], sw(g[0]), sw(g[1]), g[2], g[3], sw(g[2]), sw(g[3]))], 1)
    o["ident"] = np.eye(P, dtype=f)
    o["identb"] = np.eye(P).astype(bf16)
    k, qn = np.arange(P)[:, None], np.arange(W0)[None, :]
    m0 = np.where((k <= qn) & (k > qn - WIN0), 0.0, -100.0)
    o["mask0"] = np.concatenate([m0, m0[:, :P]], 1).astype(bf16)
    tri = np.where(np.arange(P)[None, :] <= k, 0.0, -1e30)
    o["mask1"] = np.concatenate([tri, np.zeros((P, P)), tri], 1).astype(bf16)

    def rope(dim):
        inv = (f(1.0) / (f(1e6) ** (np.arange(0, dim, 2, dtype=f) / f(dim)))).astype(f)
        fr = np.arange(S, dtype=f)[:, None] * inv[None, :]
        cs, sn = np.cos(fr), np.sin(fr)
        return np.concatenate([cs, cs], 1).astype(f), np.concatenate([-sn, sn], 1).astype(f)

    half = lambda z: z.reshape(2, P, -1).transpose(1, 0, 2)
    cs, sn = rope(D0)
    o["cos0"], o["sin0"] = half(np.tile(cs, (1, H0 + KV0))), half(np.tile(sn, (1, H0 + KV0)))
    cs, sn = rope(D1)
    qs = f(D1 ** -0.5)
    o["rope1"] = np.stack([half(cs * qs), half(sn * qs), half(cs), half(sn)], 1)
    return {n: np.ascontiguousarray(o[n]) for n in _ORDER}


def kernel(**inputs):
    import concourse.bacc as bacc
    from concourse.bass_utils import run_bass_kernel_spmd as run

    arrays = _layout(inputs)
    nc = bacc.Bacc("TRN2", target_bir_lowering=False, num_devices=1)
    io = {n: nc.dram_tensor("in_" + n, z.shape, mybir.dt.from_np(z.dtype), kind="ExternalInput").ap() for n, z in arrays.items()}
    out = nc.dram_tensor("out_0", (B, S, HID), F32, kind="ExternalOutput").ap()
    build(nc, io, out)
    r = run(nc, [{"in_" + n: z for n, z in arrays.items()}], core_ids=[0])
    return r.results[0]["out_0"]
```

```python
from contextlib import ExitStack

import concourse.bass as bass
import numpy as np
from concourse import mybir

F32 = mybir.dt.float32
BF16 = mybir.dt.bfloat16
F32R = mybir.dt.float32r
I32 = mybir.dt.int32
ALU = mybir.AluOpType
ACT = mybir.ActivationFunctionType
AX = mybir.AxisListType

P = 128
B, S, HID = 4, 256, 256
T = B * S
NT = T // P
HC = HID // P
DM, DI, DS, DC, DR = 128, 256, 16, 4, 8
DT = DI // P
H0, KV0, D0, WIN0 = 8, 2, 32, 64
REP0 = H0 // KV0
NQK0 = (H0 + KV0) * D0
NQKV0 = NQK0 + KV0 * D0
SCORE0 = 256.0 / (D0 ** 0.5) / 30.0
SOFTCAP = 30.0
W0 = P + WIN0
INTER = 704
NI = (INTER + P - 1) // P
H1, KV1, D1 = 16, 4, 128
REP1 = H1 // KV1
NQ1, NK1 = H1 * D1, KV1 * D1
E, G, KG, K, M, SH = 32, 8, 4, 6, 128, 256
EPG = E // G
ROUTE_SCALE = 2.5
SB_LOADS = 2
WRING = 4

PK_IN = 0
PK_CW = PK_IN + DI
PK_CB = PK_CW + DC * DI
PK_DB = PK_CB + DT
PK_A = PK_DB + DT
PK_X = PK_A + DT * DS
PK_N = PK_X + DT * (DR + 2 * DS)

C_ON_DVE = {0: [n for n in range(DS) if n not in (3, 7, 11)], 1: [n for n in range(DS) if n % 3 == 1]}


def c_step(g):
    mine = lambda q: q % DS in C_ON_DVE[q // DS]
    return ("c_dve" if mine(g) else "c_pool"), sum(mine(q) == mine(g) for q in range(g + 1))


def mlen(i):
    return min(P, INTER - i * P)


class Chain:

    def __init__(self, eng, sem):
        self.eng, self.sem, self.n = eng, sem, 0

    def step(self, ins):
        self.n += 1
        ins.then_inc(self.sem, 1)
        return self.n

    def wait(self, mark=None):
        self.eng.wait_ge(self.sem, self.n if mark is None else mark)

    def link(self, ins):
        self.step(ins)
        self.wait()


def build(nc, io, out):
    ctx = ExitStack()
    with ctx:
        def sb(name, shape, dt=F32):
            return ctx.enter_context(nc.sbuf_tensor(name, shape, dt))

        def sem(name):
            return ctx.enter_context(nc.semaphore(name))

        X = sb("X", [P, NT, HID])
        H = sb("H", [P, NT, HID])
        hT = sb("hT", [P, HC, T])
        ctxp = sb("ctxp", [P, B, S + DC - 1])
        pkb = sb("pkb", [P, PK_N])
        pk = [pkb, pkb]
        skip = sb("skip", [P, 2, DT])
        dtw = [sb(f"dtw{l}", [DR, DI]) for l in range(2)]
        LW = [pk[l][:, PK_CW:PK_CW + DC * DI].rearrange("p (k n) -> p k n", k=DC) for l in range(2)]
        scan_base = nc.sbuf_base
        DEL = sb("DEL", [P, DT, T])
        DU = sb("DU", [P, DT, T])
        ACC = sb("ACC", [P, DT, T])
        U = ACC
        dA = [sb(f"dA{s}", [P, DT, T]) for s in range(2)]
        hS = [sb(f"hS{s}", [P, DT, T]) for s in range(2)]
        BCb = [sb(f"BCb{s}", [P, 2, T]) for s in range(SB_LOADS)]
        def split(name, place, shape):
            return nc.alloc_sbuf_tensor_at(name, shape, F32R, offset=scan_base + place * DT * T * 4)

        hTh, hTl = split("hTh", 0, [P, HC, T]), split("hTl", 1, [P, HC, T])
        MHh, MHl = split("MHh", 2, [P, 2, T]), split("MHl", 3, [P, 2, T])
        Wh, Wl = split("Wh", 4, [P, WRING, 512]), split("Wl", 5, [P, WRING, 512])
        negA = sb("negA", [P, DT * DS])
        cbh = sb("cbh", [P, DT])
        ident = sb("ident", [P, P])
        identb = sb("identb", [P, P], BF16)
        mask0 = sb("mask0", [P, W0 + P], BF16)
        mask1 = sb("mask1", [P, 3 * P], BF16)
        tabs = sb("tabs", [P, 6, 2, D1])
        lnst = sb("lnst", [P, NT, 6])
        lnmv = sb("lnmv", [P, NT, 2])
        lnve = sb("lnve", [P, NT])
        lnrs = sb("lnrs", [P, NT])
        mhalf = sb("mhalf", [P, NT])
        WA = sb("WA", [P, H1 * HID])
        WGU = WA[:, 0:HC * 2 * INTER].rearrange("p (c n) -> p c n", c=HC)
        WO1 = WA[:, 0:H1 * HID].rearrange("p (h n) -> p h n", h=H1)
        fsc = sb("fsc", [P, 3, NI])
        dsc = sb("dsc", [P, HID])
        WB = sb("WB", [P, HC, NQ1 + 2 * NK1])
        WQKV0 = WB[:, 0, 0:HC * NQKV0].rearrange("p (c n) -> p c n", c=HC)
        WO0 = WB[:, 0, HC * NQKV0:HC * NQKV0 + HC * HID].rearrange("p (c n) -> p c n", c=HC)
        WE = [WB[:, 0, 512 * s:512 * s + 512] for s in range(WRING)]
        WS = [WB[:, 1, 512 * s:512 * s + 512] for s in range(2)]
        WRT = WB[:, 1, 1024:1024 + HC * E].rearrange("p (c e) -> p c e", c=HC)
        BR = WB[0:E, 1, 1024 + HC * E:1024 + HC * E + 1]
        wmean = sb("wmean", [P, HC, H1 + KV1])
        arena = sb("arena", [P, 48 * 256])
        kb = 256

        def ar(k0, n):
            return arena[:, int(k0 * kb):int(k0 * kb) + n]

        Q0 = ar(0, NT * NQKV0).rearrange("p (t n) -> p t n", t=NT)
        RA = ar(12, NT * NQK0).rearrange("p (t n) -> p t n", t=NT)
        RB = ar(22, NT * NQK0).rearrange("p (t n) -> p t n", t=NT)
        SQ0 = ar(12, NT * NQKV0)
        K40 = ar(12, NT * KV0 * P).rearrange("p (t g n) -> p t g n", t=NT, g=KV0)
        cos0 = ar(32, 2 * NQK0).rearrange("p (h n) -> p h n", h=2)
        sin0 = ar(35, 2 * NQK0).rearrange("p (h n) -> p h n", h=2)
        qT0 = ar(32, KV0 * T).rearrange("p (g t) -> p g t", g=KV0)
        kT0 = ar(40, KV0 * T).rearrange("p (g t) -> p g t", g=KV0)
        TH0 = ar(12, REP0 * (W0 + P)).rearrange("p (r n) -> p r n", r=REP0)
        PT0 = [z.rearrange("p (r k q) -> p r k q", r=REP0, k=2) for z in (WB[:, 1, 0:REP0 * 2 * S], ar(22.5, REP0 * 2 * S))]
        st0 = ar(30, 4 * NT * NQKV0 // D0).rearrange("p (i n) -> p i n", i=4)
        V0 = ar(20, NT * (2 * D0 + 1)).rearrange("p (t n) -> p t n", t=NT)
        rden0 = sb("rden0", [P, 2 * REP0])
        O0 = tabs[0:D0 + 1, :, :, :].rearrange("p a b c -> p (a b c)")[:, 0:REP0 * S]
        aT0 = hT
        QK0, QKV0 = Q0[:, :, 0:NQK0], Q0.rearrange("p t (n d) -> p (t n) d", d=D0)
        nh0 = NT * NQKV0 // D0
        heads0 = lambda a: a.unsqueeze(2).broadcast_to([P, nh0, D0])
        tb0 = lambda a: a.rearrange("p (b h) n -> p b h n", h=2)
        WDN = ar(40, NI * HID).rearrange("p (i n) -> p i n", i=NI)
        hid0 = ar(0, NI * T).rearrange("p (i t) -> p i t", i=NI)
        fth = [ar(24 + 2 * s, 512) for s in range(2)]
        ft1 = [ar(28 + 2 * s, 512) for s in range(2)]
        rope1 = ar(32, 8 * D1).rearrange("p (i h d) -> p i h d", i=4, h=2)
        gains = ar(36, 8 * D1).rearrange("p (i d) -> p i d", i=8)
        SQ = ar(0, 1024).rearrange("p (t n) -> p t n", t=2)
        JA = ar(4, 1024).rearrange("p (t n) -> p t n", t=2)
        JB = ar(8, 1024).rearrange("p (t n) -> p t n", t=2)
        R = ar(12, 1024).rearrange("p (t n) -> p t n", t=2)
        KT = [ar(16 + 4 * s, 1024).rearrange("p (h q) -> p h q", h=KV1) for s in range(2)]
        QT = [ar(24 + 4 * s, 1024).rearrange("p (h q) -> p h q", h=REP1) for s in range(2)]
        V1 = [ar(32 + 4 * s, 1024).rearrange("p (t n) -> p t n", t=2) for s in range(2)]
        P1 = [ar(40 + 1.5 * s, 384) for s in range(2)]
        PT1 = [ar(43 + 1.5 * s, 384) for s in range(2)]
        aT1 = [ar(46 + s, 256) for s in range(2)]
        jst = sb("jst", [P, 2, 3, 8])
        nm1 = sb("nm1", [P, 2, 2])
        sum1 = sb("sum1", [P, 2, 2])
        rc1 = sb("rc1", [P, 2, 2])
        job_bank = lambda j: 6 if j == 1 else 0
        job_a = lambda j: (KT[1].rearrange("p h q -> p (h q)").rearrange("p (t n) -> p t n", t=2)) if j == 1 else JA
        job_b = lambda j: V1[1] if j == 1 else JB
        job_s = lambda j: (QT[1].rearrange("p h q -> p (h q)").rearrange("p (t n) -> p t n", t=2)) if j == 1 else SQ
        v_bank = lambda b: 0 if b else 3
        GB = [ar(4 * s, T) for s in range(WRING)]
        MR = [ar(16 + 4 * s, T) for s in range(2)]
        MG = [ar(24 + 4 * s, T) for s in range(2)]
        MH = [ar(32 + 4 * s, T) for s in range(2)]
        gT = ar(40, T)[0:E, :]
        rET = ar(44, T)[0:E, :]
        at = [0]

        def router(*shape):
            n = int(np.prod(shape))
            at[0] += n
            z = arena[:, at[0] - n:at[0]]
            return z if len(shape) == 1 else z.rearrange("p (t n) -> p t n", t=shape[0])

        rS, rW, rGate = router(NT, E), router(NT, E), router(NT, E)
        rg = [router(NT * G) for i in range(6)]
        rGW, rGM = router(NT, G + 4), router(NT, G + 4)
        rMS, rME = router(NT, E + 2), router(NT, E + 2)
        rM8, rT8, rE8 = router(NT, 8), router(NT, 8), router(NT, 8)
        rsum = router(2, NT)
        ps = ctx.enter_context(nc.psum_tensor("ps", [P, 8, 512], F32))

        bc_dram = nc.dram_tensor("bc_dram", [2, DS, 2, T], F32, kind="Internal").ap()
        gate_dram = nc.dram_tensor("gate_dram", [E, T], F32, kind="Internal").ap()

        ld = {n: sem("ld_" + n) for n in ("ctx", "pk0", "pk1", "x", "ident", "masks", "rope0", "rope1", "wqkv0",
                                          "wo0", "ffn", "wdn", "wqkv1", "wo1", "shared", "route")}
        ld_bc = [sem(f"ld_bc{s}") for s in range(SB_LOADS)]
        ld_we = [sem(f"ld_we{s}") for s in range(WRING)]
        ld_gb = [sem(f"ld_gb{s}") for s in range(WRING)]
        names = """act_chain dve_chain pool_chain init lw_ready conv_mm conv_tanh u_ready xdbl_mm xdbl_copied bc_stored
            dtpre_mm sp_abs sp_exp sp_ln delta_ready du_ready acc_ready da_cols_zero da_ready dbu_ready scan_done c_dve c_pool ssm_acc
            ln_mv ln_rstd ln_h ln_tr_mm ln_tr_act ln_tr_dve qkv0_mm qkv0_copied rope0_cos rope0_sin rope0_add rope0_mean rope0_rot rope0_sq rope0_rs rope0_done v0_ready k4_ready tr0_mm tr0_copied
            s0_mm s0_tanh s0_exp pv0_mm pv0_copied pv0_tr at0_den at0_ready a_tr_mm a_tr_act a_tr_dve o0_mm x_new fsc_ready gate_tanh gate_y gate_mm nega_exp nega_ready pt0_fill
            f_mm f_tanh f_hid fd_mm wdn_ready w1_mean w1_centered tabs_ready job_mm job_sq job_rot job_sum job_rstd job_add job_rope
            job_tr_mm job_tr_copied v_mm v_copied s1_mm s1_max s1_exp s1_norm pt1_mm pt1_copied pv1_mm at1_copied o1_mm
            r_bias r_mm r_exp r_tr r_sum r_gate gt_mm gt_copied gate_stored h_hi h_lo_dve h_lo_pool w_hi w_lo
            m_mm m_relu m_sq m_gated m_hid m_hi m_lo m_out m_last out_done""".split()
        s = {n: sem(n) for n in names}
        block = ctx.enter_context(nc.Block())

        bands = lambda a: a.rearrange("p (b s) -> p b s", b=B)
        xr = io["x"].rearrange("b (h p) d -> p (b h) d", p=P)
        outr = out.rearrange("b (h p) d -> p (b h) d", p=P)

        XN_ATT0, XN_GATE0, XN_FFN, XN_ATT1, XN_GATE1 = 2, 4, 6, 10, 12
        XN = {0: 0, 1: XN_ATT0, 2: XN_GATE0, 3: XN_FFN, 4: XN_ATT1, 5: XN_GATE1}
        TR_LNS = [0, 2, 3, 5]
        TR_BANK = [(4, 6), (0, 2), (2, 2), (0, 2)]
        CONV_BANK = [0, 4]

        @block.sync
        def _(sp):
            sp.dma_start(ctxp[:], io["ctxp"]).then_inc(ld["ctx"], 16)
            sp.dma_start(pk[0][:], io["pk0"]).then_inc(ld["pk0"], 16)
            sp.dma_start(dtw[0][:], io["dtw0"]).then_inc(ld["pk0"], 16)
            sp.dma_start(skip[:], io["skip"]).then_inc(ld["pk0"], 16)
            sp.dma_start(X[:], xr).then_inc(ld["x"], 16)
            sp.dma_start(ident[:], io["ident"]).then_inc(ld["ident"], 16)
            sp.dma_start(WQKV0, io["wqkv0"]).then_inc(ld["wqkv0"], 16)
            sp.dma_start(cos0, io["cos0"]).then_inc(ld["rope0"], 16)
            sp.dma_start(sin0, io["sin0"]).then_inc(ld["rope0"], 16)
            sp.dma_start(identb[:], io["identb"]).then_inc(ld["masks"], 16)
            sp.dma_start(mask0[:], io["mask0"]).then_inc(ld["masks"], 16)
            sp.dma_start(mask1[:], io["mask1"]).then_inc(ld["masks"], 16)

            def load_bc(g):
                sp.wait_ge(s["bc_stored"], 16 * (g // DS + 1))
                if g >= SB_LOADS:
                    sp.wait_ge(s["dbu_ready"], g - SB_LOADS + 1)
                    who, count = c_step(g - SB_LOADS)
                    sp.wait_ge(s[who], count)
                src = bc_dram[g // DS, g % DS].rearrange("r t -> (r t)").partition_broadcast(P)
                sp.dma_start(BCb[g % SB_LOADS][:].rearrange("p r t -> p (r t)"), src).then_inc(ld_bc[g % SB_LOADS], 16)

            sp.dma_start(WO0, io["wo0"]).then_inc(ld["wo0"], 16)
            for g in range(SB_LOADS):
                load_bc(g)
            sp.wait_ge(s["delta_ready"], 1)
            sp.wait_ge(s["sp_exp"], 1)
            sp.wait_ge(s["nega_exp"], 1)
            sp.dma_start(pk[1][:], io["pk1"]).then_inc(ld["pk1"], 16)
            sp.dma_start(dtw[1][:], io["dtw1"]).then_inc(ld["pk1"], 16)
            sp.dma_start(WA[:, 0:HC * 2 * INTER], io["ffn"]).then_inc(ld["ffn"], 16)
            sp.dma_start(fsc[:, 0:2, :], io["fsc"]).then_inc(ld["ffn"], 16)
            sp.dma_start(dsc[:], io["dsc"]).then_inc(ld["ffn"], 16)
            for g in range(SB_LOADS, DS):
                load_bc(g)
            sp.wait_ge(s["o0_mm"], 2)
            sp.dma_start(WDN, io["wdn"]).then_inc(ld["wdn"], 16)
            sp.dma_start(rope1, io["rope1"]).then_inc(ld["rope1"], 16)
            sp.dma_start(gains, io["gains"]).then_inc(ld["rope1"], 16)
            sp.dma_start(WB[:], io["wqkv1"]).then_inc(ld["wqkv1"], 16)
            for g in range(DS, 2 * DS):
                load_bc(g)
            sp.wait_ge(s["job_mm"], len(JOB))
            sp.wait_ge(s["v_mm"], B)
            for i in range(2):
                sp.dma_start(WS[i], io["we"][E + i]).then_inc(ld["shared"], 16)
            sp.dma_start(WRT, io["wrt"]).then_inc(ld["route"], 16)
            sp.dma_start(BR, io["br"]).then_inc(ld["route"], 16)
            for e in range(WRING):
                sp.dma_start(WE[e], io["we"][e]).then_inc(ld_we[e], 16)
            sp.wait_ge(s["gate_stored"], 16)
            for e in range(WRING):
                sp.dma_start(GB[e], gate_dram[e].partition_broadcast(P)).then_inc(ld_gb[e], 16)
            with sp.Fori(1, E // WRING, 1) as i:
                for k in range(WRING):
                    sp.wait_ge(s["m_lo"], WRING * i + (k - WRING + 3))
                    sp.dma_start(WE[k], io["we"][bass.ds(WRING * i + k, 1)].rearrange("a p n -> (a p) n")).then_inc(ld_we[k], 16)
                    sp.dma_start(GB[k], gate_dram[bass.ds(WRING * i + k, 1)].rearrange("a t -> (a t)").partition_broadcast(P)).then_inc(ld_gb[k], 16)
            for hf in range(2):
                sp.wait_ge(s["x_new"], XN_GATE1 + 1 + hf)
                sp.dma_start(outr[:, 4 * hf:4 * hf + 4, :], X[:, 4 * hf:4 * hf + 4, :]).then_inc(s["out_done"], 16)
            sp.wait_ge(s["out_done"], 32)

        @block.gpsimd
        def _(pool):
            gp = nc.gpsimd
            ch = Chain(pool, s["pool_chain"])
            gp.memset(mhalf[:], -0.5).then_inc(s["init"], 1)
            floor = float(np.exp(np.float32(-SOFTCAP)))
            gp.memset(PT0[0][:, :, 0, W0:S], floor).then_inc(s["pt0_fill"], 1)
            gp.memset(PT0[0][:, :, 1, 0:P], floor).then_inc(s["pt0_fill"], 1)
            pool.wait_ge(s["init"], 1)

            def ln_rstd(L):
                for hf in range(2):
                    z = slice(4 * hf, 4 * hf + 4)
                    pool.wait_ge(s["ln_mv"], NT * L + 4 * hf + 4)
                    ch.link(gp.tensor_scalar(lnve[:, z], lnmv[:, z, 1], 1e-5, None, ALU.add))
                    gp.tensor_tensor(lnrs[:, z], lnve[:, z], mhalf[:, z], ALU.pow).then_inc(s["ln_rstd"], 1)

            def zero_cols(l, slot):
                if slot == 0:
                    pool.wait_ge(s["bc_stored"], 16 * (l + 1))
                    pool.wait_ge(s["dtpre_mm"], DT * (l + 1))
                else:
                    pool.wait_ge(s["delta_ready"], l + 1)
                gp.memset(dA[slot][:].rearrange("p d (b s) -> p (d b) s", b=B)[:, :, 0:1], 0.0).then_inc(s["da_cols_zero"], 1)

            def ssm_step(l, n):
                g = DS * l + n
                h = hS[g % 2]
                cb = BCb[g % SB_LOADS][:, 1, :]
                if n in C_ON_DVE[l]:
                    pool.wait_ge(s["c_dve"], c_step(g)[1])
                else:
                    pool.wait_ge(s["scan_done"], g + 1)
                    pool.wait_ge(ld_bc[g % SB_LOADS], 16 * (g // SB_LOADS + 1))
                    gp.tensor_tensor(h[:], h[:], cb.unsqueeze(1).broadcast_to([P, DT, T]), ALU.mult).then_inc(s["c_pool"], 1)
                    pool.wait_ge(s["c_pool"], c_step(g)[1])
                if n == 0:
                    pool.wait_ge(s["acc_ready"], l + 1)
                if g:
                    pool.wait_ge(s["ssm_acc"], g)
                gp.tensor_tensor(ACC[:], ACC[:], h[:], ALU.add).then_inc(s["ssm_acc"], 1)

            ln_rstd(0)
            zero_cols(0, 0)
            pool.wait_ge(s["qkv0_copied"], NT)
            pool.wait_ge(ld["rope0"], 32)
            for hf in range(2):
                for x in range(2):
                    pick = lambda a, y: tb0(a)[:, :, hf, :].rearrange("p b (n d) -> p b n d", d=D0)[:, :, :, 16 * y:16 * y + 16]
                    sn = sin0[:, hf, :].rearrange("p (n d) -> p n d", d=D0)[:, :, 16 * x:16 * x + 16]
                    gp.tensor_tensor(pick(RB, x), pick(QK0, 1 - x), sn.unsqueeze(1).broadcast_to([P, B, H0 + KV0, 16]),
                                     ALU.mult).then_inc(s["rope0_sin"], 1)
                    if hf == 0 and x == 1:
                        zero_cols(0, 1)
            pool.wait_ge(s["rope0_sin"], 4)
            pool.wait_ge(s["rope0_cos"], 1)
            gp.tensor_tensor(QK0, RA, RB, ALU.add).then_inc(s["rope0_add"], 1)
            ssm_step(0, 0)
            pool.wait_ge(s["rope0_mean"], 1)
            gp.tensor_tensor(QKV0, QKV0, heads0(st0[:, 0, :]), ALU.subtract).then_inc(s["rope0_rot"], 1)
            ssm_step(0, 1)
            pool.wait_ge(s["rope0_rs"], 1)
            gp.tensor_tensor(QKV0, QKV0, heads0(st0[:, 2, :]), ALU.mult).then_inc(s["rope0_done"], 1)
            pool.wait_ge(s["rope0_done"], 1)
            gp.memset(PT0[1][:, :, 0, W0:S], floor).then_inc(s["pt0_fill"], 1)
            gp.memset(PT0[1][:, :, 1, 0:P], floor).then_inc(s["pt0_fill"], 1)
            gp.memset(V0[:, :, D0:D0 + 1], 1.0).then_inc(s["pt0_fill"], 1)
            for n in range(2, DS):
                ssm_step(0, n)
            ln_rstd(1)
            ln_rstd(2)
            pool.wait_ge(ld["wdn"], 16)
            pool.wait_ge(ld["ffn"], 48)
            for i in range(NI):
                m = mlen(i)
                gp.tensor_tensor(WDN[0:m, i, :], WDN[0:m, i, :], dsc[0:m, :], ALU.mult).then_inc(s["wdn_ready"], 1)
            pool.wait_ge(s["w1_mean"], 1)
            for c in range(HC):
                w = WB[:, c, 0:NQ1 + NK1].rearrange("p (h d) -> p h d", d=D1)
                gp.tensor_tensor(w, w, wmean[:, c, :].unsqueeze(2).broadcast_to([P, H1 + KV1, D1]), ALU.add).then_inc(s["w1_centered"], 1)
            zero_cols(1, 0)
            zero_cols(1, 1)
            step = iter(range(DS))
            for _ in range(SSM1_IN_FFN - 1):
                ssm_step(1, next(step))
            ln_rstd(3)

            def job(j):
                pool.wait_ge(s["job_sum"], j + 1)
                st = jst[:, j % 2]
                ch.link(gp.tensor_scalar(st[:, 1, :], st[:, 0, :], 1.0 / D1, 1e-5, ALU.mult, ALU.add))
                gp.tensor_tensor(st[:, 2, :], st[:, 1, :], mhalf[:], ALU.pow).then_inc(s["job_rstd"], 1)
                pool.wait_ge(s["job_rot"], 3 * (j + 1))
                gp.tensor_tensor(job_a(j), job_a(j), job_b(j), ALU.add).then_inc(s["job_add"], 1)

            left = DS - SSM1_IN_FFN
            for kind, a in ATT1_PLAN:
                if kind == "sum":
                    job(JOB[a])
                    if JOB[a] == 2:
                        ssm_step(1, SSM1_IN_FFN - 1)
                if kind == "scan":
                    ssm_step(1, a)
            ln_rstd(4)

            def w_low(x, src):
                slot = x % WRING
                gp.tensor_tensor(Wl[:, slot, :], src, Wh[:, slot, :].bitcast(F32), ALU.subtract).then_inc(s["w_lo"], 1)

            def hid_low(p):
                gp.tensor_tensor(MHl[:, p, :], MH[p], MHh[:, p, :].bitcast(F32), ALU.subtract).then_inc(s["m_lo"], 1)

            for x in range(2):
                pool.wait_ge(s["w_hi"], x + 1)
                w_low(x, WS[x])
            ln_rstd(5)
            pool.wait_ge(s["h_hi"], 2)
            z = slice(512, 1024)
            gp.tensor_tensor(hTl[:, :, z], hT[:, :, z], hTh[:, :, z].bitcast(F32), ALU.subtract).then_inc(s["h_lo_pool"], 1)
            for x in range(2, 4):
                pool.wait_ge(s["w_hi"], x + 1)
                w_low(x, WE[x - 2])
            for x in range(2):
                pool.wait_ge(s["m_hi"], x + 1)
                hid_low(x)
            with pool.Fori(0, E // WRING - 1, 1) as i:
                for k in range(WRING):
                    pool.wait_ge(s["w_hi"], WRING * i + (k + 5))
                    w_low(k, WE[(k + 2) % WRING])
                    pool.wait_ge(s["m_hi"], WRING * i + (k + 3))
                    hid_low(k % 2)
            for e in range(E - WRING, E):
                if e + 2 < E:
                    pool.wait_ge(s["w_hi"], e + 5)
                    w_low(e, WE[(e + 2) % WRING])
                pool.wait_ge(s["m_hi"], e + 3)
                hid_low(e % 2)

        @block.scalar
        def _(act):
            sc = nc.scalar
            ch = Chain(act, s["act_chain"])

            def conv_tanh(l, d):
                act.wait_ge(s["conv_mm"], DT * l + d + 1)
                act.wait_ge(s["lw_ready"], l + 1)
                c0 = CONV_BANK[l] + 2 * d
                if l:
                    act.wait_ge(s["da_ready"], 2 * DS)
                sc.activation(DEL[:, d, :], ps[:, c0:c0 + 2, :].rearrange("p a b -> p (a b)"), ACT.Tanh,
                              bias=cbh[:, d:d + 1], scale=0.5).then_inc(s["conv_tanh"], 1)

            def xdbl_copy(l):
                act.wait_ge(s["xdbl_mm"], l + 1)
                c0 = CONV_BANK[l]
                sc.copy(dA[0][0:DR + 2 * DS, 0, :], ps[0:DR + 2 * DS, c0:c0 + 2, :].rearrange("p a b -> p (a b)")).then_inc(s["xdbl_copied"], 1)
                act.wait_ge(s["xdbl_copied"], l + 1)
                act.dma_start(bc_dram[l].rearrange("n r t -> (n r) t"), dA[0][DR:DR + 2 * DS, 0, :]).then_inc(s["bc_stored"], 16)

            def softplus(l):
                for d in range(DT):
                    act.wait_ge(s["dtpre_mm"], DT * l + d + 1)
                    c0 = CONV_BANK[l] + 2 * d
                    sc.activation(hS[0][:, d, :], ps[:, c0:c0 + 2, :].rearrange("p a b -> p (a b)"), ACT.Abs,
                                  bias=pk[l][:, PK_DB + d:PK_DB + d + 1]).then_inc(s["sp_abs"], 1)
                act.wait_ge(s["sp_abs"], DT * (l + 1))
                sc.activation(hS[0][:], hS[0][:], ACT.Exp, scale=-1.0).then_inc(s["sp_exp"], 1)

            def softplus_ln(l):
                act.wait_ge(s["sp_exp"], l + 1)
                sc.activation(dA[1][:], hS[0][:], ACT.Ln, bias=1.0).then_inc(s["sp_ln"], 1)

            def neg_a(l):
                act.wait_ge(ld[f"pk{l}"], 48 - 16 * l)
                if l:
                    act.wait_ge(s["da_ready"], 2 * DS)
                sc.activation(negA[:], pk[l][:, PK_A:PK_A + DT * DS], ACT.Exp).then_inc(s["nega_exp"], 1)
                act.wait_ge(s["nega_exp"], l + 1)
                sc.mul(negA[:], negA[:], -1.0).then_inc(s["nega_ready"], 1)

            def ssm_step(l, n, tiles=range(DT)):
                g = DS * l + n
                if n == 0:
                    act.wait_ge(s["delta_ready"], l + 1)
                    act.wait_ge(s["nega_ready"], l + 1)
                if n < 2:
                    act.wait_ge(s["da_cols_zero"], 2 * l + n + 1)
                if n >= 2:
                    act.wait_ge(s["scan_done"], g - 1)
                for d in tiles:
                    o = bands(dA[g % 2][:, d, :])[:, :, 1:S]
                    sc.activation(o, bands(DEL[:, d, :])[:, :, 1:S], ACT.Exp,
                                  scale=negA[:, d * DS + n:d * DS + n + 1]).then_inc(s["da_ready"], 1)

            def ln_tr_copy(i, halves=(0, 1)):
                for hf in halves:
                    act.wait_ge(s["ln_tr_mm"], 4 * i + 2 * hf + 1)
                    sc.copy(hT[:, 0, 512 * hf:512 * hf + 512], ps[:, TR_BANK[i][hf], :]).then_inc(s["ln_tr_act"], 1)

            neg_a(0)
            for d in range(DT):
                conv_tanh(0, d)
            ln_tr_copy(0)
            xdbl_copy(0)
            softplus(0)
            softplus_ln(0)
            for t in range(NT):
                act.wait_ge(s["qkv0_mm"], t + 1)
                sc.copy(Q0[:, t, :], ps[:, 4 + t % 4, 0:NQKV0]).then_inc(s["qkv0_copied"], 1)
            step = iter(range(DS))

            def steps_to(n):
                for k in step:
                    ssm_step(0, k)
                    if k == n:
                        break

            steps_to(1)
            act.wait_ge(s["rope0_rot"], 1)
            sc.activation(SQ0, Q0.rearrange("p t n -> p (t n)"), ACT.Square).then_inc(s["rope0_sq"], 1)
            steps_to(3)
            act.wait_ge(s["rope0_done"], 1)
            for g in range(KV0):
                c = H0 * D0 + D0 * g
                sc.copy(K40[:, :, g, :].rearrange("p t (r d) -> p t r d", d=D0),
                        Q0[:, :, c:c + D0].unsqueeze(2).broadcast_to([P, NT, 4, D0])).then_inc(s["k4_ready"], 1)
            for g in range(KV0):
                c = NQK0 + D0 * g
                sc.copy(V0[:, :, (D0 + 1) * g:(D0 + 1) * g + D0], Q0[:, :, c:c + D0]).then_inc(s["v0_ready"], 1)
            for i in range(8):
                act.wait_ge(s["tr0_mm"], i + 1)
                g, part, hf = i // 4, (i // 2) % 2, i % 2
                dst = (qT0, kT0)[part][:, g, 512 * hf:512 * hf + 512]
                sc.copy(dst, ps[:, 4 + i % 4, :]).then_inc(s["tr0_copied"], 1)
            def a_tr_copy(hf):
                act.wait_ge(s["a_tr_mm"], 2 * hf + 1)
                sc.copy(aT0[:, 0, 512 * hf:512 * hf + 512], ps[:, 4, :]).then_inc(s["a_tr_act"], 1)

            steps_to(5)
            def pv0_copy(u):
                act.wait_ge(s["pv0_mm"], u + 1)
                if u:
                    act.wait_ge(s["pv0_tr"], u)
                sc.copy(O0, ps[0:D0 + 1, 4:6, :].rearrange("p a b -> p (a b)")).then_inc(s["pv0_copied"], 1)

            for u in range(B * KV0):
                act.wait_ge(s["s0_mm"], u + 1)
                if u:
                    act.wait_ge(s["s0_exp"], 2 * u)
                sc.activation(TH0, ps[:, 0:REP0, 0:W0 + P], ACT.Tanh, scale=SCORE0).then_inc(s["s0_tanh"], 1)
                act.wait_ge(s["s0_tanh"], u + 1)
                act.wait_ge(s["pt0_fill"], 5)
                if u >= 2:
                    act.wait_ge(s["pv0_mm"], u - 1)
                pt = PT0[u % 2]
                sc.activation(pt[:, :, 0, 0:W0], TH0[:, :, 0:W0], ACT.Exp, scale=SOFTCAP).then_inc(s["s0_exp"], 1)
                sc.activation(pt[:, :, 1, P:S], TH0[:, :, W0:W0 + P], ACT.Exp, scale=SOFTCAP).then_inc(s["s0_exp"], 1)
                if u:
                    pv0_copy(u - 1)
                    if u - 1 == A_TR_UNIT:
                        a_tr_copy(0)
                if AT0_AT[u] > 6:
                    steps_to(AT0_AT[u] - 1)
            pv0_copy(B * KV0 - 1)
            steps_to(DS - 1)
            a_tr_copy(1)

            def gate_tanh(l):
                for hf in range(2):
                    act.wait_ge(s["ln_h"], NT * (3 * l + 1) + 4 * hf + 4)
                    sc.activation(hT[:, hf, :], H[:, 4 * hf:4 * hf + 4, :].rearrange("p a b -> p (a b)"), ACT.Tanh,
                                  scale=0.5).then_inc(s["gate_tanh"], 1)

            neg_a(1)
            gate_tanh(0)
            for d in range(DT):
                conv_tanh(1, d)
            ln_tr_copy(1)
            step = iter(range(DS))
            for j in range(2 * NI):
                m = mlen(j // 2)
                act.wait_ge(s["f_mm"], j + 1)
                act.wait_ge(s["fsc_ready"], 1)
                if j >= 2:
                    act.wait_ge(s["f_hid"], 2 * (j - 1))
                sc.activation(fth[j % 2][0:m, :], ps[0:m, 2 * (j % 2), :], ACT.Tanh,
                              scale=fsc[0:m, 2, j // 2:j // 2 + 1]).then_inc(s["f_tanh"], 1)
                if j == PREP_XDBL:
                    xdbl_copy(1)
                if j == PREP_DT:
                    softplus(1)
                if j == PREP_DT + 1:
                    softplus_ln(1)
                if j in FFN_SSM_AT:
                    ssm_step(1, next(step))
            for n in step:
                if n < SSM1_IN_FFN:
                    ssm_step(1, n)
            ln_tr_copy(2, (0,))

            def job_sq(j):
                act.wait_ge(s["job_mm"], j + 1)
                if j:
                    act.wait_ge(s["job_sum"], j)
                k = job_bank(j)
                sc.activation(job_s(j), ps[:, k:k + 2, :], ACT.Square).then_inc(s["job_sq"], 1)

            def job_copy(b, i, x):
                j = JOB[b, i]
                dst = KT[b % 2] if i == 0 else QT[(4 * b + i - 1) % 2]
                act.wait_ge(s["job_tr_mm"], 2 * j + x + 1)
                if i == 0 and b >= 2:
                    act.wait_ge(s["s1_mm"], H1 * (b - 1))
                if i > 0 and 4 * b + i - 1 >= 2:
                    act.wait_ge(s["s1_mm"], 4 * (4 * b + i - 2))
                sc.copy(dst[:, 2 * x:2 * x + 2, :].rearrange("p a b -> p (a b)"), ps[:, 2, :]).then_inc(s["job_tr_copied"], 1)

            def v_copy(b):
                act.wait_ge(s["v_mm"], b + 1)
                if b >= 2:
                    act.wait_ge(s["pv1_mm"], H1 * (b - 1))
                k = v_bank(b)
                sc.copy(V1[b % 2], ps[:, k:k + 2, :]).then_inc(s["v_copied"], 1)

            def exp1(u):
                p = u % 2
                act.wait_ge(s["s1_max"], u + 1)
                if u >= 2:
                    act.wait_ge(s["pt1_mm"], u - 1)
                sc.activation(P1[p][:, 0:P], ps[:, 3 + p, 0:P], ACT.Exp, bias=nm1[:, p, 0:1],
                              accum_out=sum1[:, p, 0:1]).then_inc(s["s1_exp"], 1)
                sc.activation(P1[p][:, P:3 * P], ps[:, 3 + p, P:3 * P], ACT.Exp, bias=nm1[:, p, 1:2],
                              accum_out=sum1[:, p, 1:2]).then_inc(s["s1_exp"], 1)

            def pt_copy(u):
                act.wait_ge(s["pt1_mm"], u + 1)
                if u >= 2:
                    act.wait_ge(s["pv1_mm"], u - 1)
                sc.copy(PT1[u % 2], ps[:, 5, 0:3 * P]).then_inc(s["pt1_copied"], 1)

            def at_copy(u):
                act.wait_ge(s["pv1_mm"], u + 1)
                if u >= 2:
                    act.wait_ge(s["o1_mm"], u - 1)
                sc.copy(aT1[u % 2], ps[:, 6, 0:S]).then_inc(s["at1_copied"], 1)

            for kind, a in ATT1_PLAN:
                if kind == "vc":
                    v_copy(a)
                elif kind == "ln1":
                    ln_tr_copy(2, (1,))
                elif kind == "wo1":
                    act.wait_ge(s["fd_mm"], 4)
                    act.dma_start(WO1, io["wo1"]).then_inc(ld["wo1"], 16)
                elif kind == "sq":
                    job_sq(JOB[a])
                elif kind == "trc":
                    job_copy(*a)
                elif kind == "exp":
                    exp1(a)
                elif kind == "ptc":
                    pt_copy(a)
                elif kind == "at":
                    at_copy(a)
                elif kind == "da":
                    ssm_step(1, a[0], (a[1],))
            gate_tanh(1)

            def w_high(x, src):
                sc.copy(Wh[:, x % WRING, :], src).then_inc(s["w_hi"], 1)

            act.wait_ge(ld["shared"], 32)
            for x in range(2):
                w_high(x, WS[x])
            for x in range(2, 4):
                act.wait_ge(ld_we[x - 2], 16)
                w_high(x, WE[x - 2])
            ln_tr_copy(3)
            for hf in range(2):
                act.wait_ge(s["ln_tr_dve"], 6 + hf + 1)
                act.wait_ge(s["ln_tr_act"], 6 + hf + 1)
                z = slice(512 * hf, 512 * hf + 512)
                sc.copy(hTh[:, :, z], hT[:, :, z]).then_inc(s["h_hi"], 1)

            def relu(p):
                sc.activation(MR[p], ps[:, 2 * p:2 * p + 2, :].rearrange("p a b -> p (a b)"), ACT.Relu).then_inc(s["m_relu"], 1)

            def hid_high(p):
                sc.copy(MHh[:, p, :], MH[p]).then_inc(s["m_hi"], 1)

            act.wait_ge(ld["route"], 32)
            sc.mul(BR, BR, -1.0).then_inc(s["r_bias"], 1)
            act.wait_ge(s["r_mm"], 1)
            act.wait_ge(s["r_bias"], 1)
            sc.activation(rET, ps[0:E, 4:6, :].rearrange("p a b -> p (a b)"), ACT.Exp, scale=-1.0, bias=BR).then_inc(s["r_exp"], 1)
            for x in range(2):
                act.wait_ge(s["m_mm"], x + 1)
                relu(x)
                act.wait_ge(s["m_relu"], x + 1)
                sc.activation(MH[x], MR[x], ACT.Square).then_inc(s["m_sq"], 1)
                act.wait_ge(s["m_sq"], x + 1)
                hid_high(x)
            act.wait_ge(s["gt_mm"], 1)
            sc.copy(gT, ps[0:E, 2:4, :].rearrange("p a b -> p (a b)")).then_inc(s["gt_copied"], 1)
            act.wait_ge(s["gt_copied"], 1)
            act.dma_start(gate_dram, gT).then_inc(s["gate_stored"], 16)

            def expert(e, k, load_count, ahead=True, first=False):
                act.wait_ge(s["m_mm"], e + 3)
                if not first:
                    act.wait_ge(s["m_hid"], e - 1)
                relu(k % 2)
                act.wait_ge(s["m_out"], e + 1)
                if ahead:
                    act.wait_ge(ld_we[(k + 2) % WRING], load_count)
                    w_high(k, WE[(k + 2) % WRING])
                act.wait_ge(s["m_hid"], e + 1)
                hid_high(k % 2)

            for e in range(WRING):
                expert(e, e, 16 * ((e + 2) // WRING + 1), first=(e < 2))
            with act.Fori(1, E // WRING - 1, 1) as i:
                for k in range(WRING):
                    expert(WRING * i + k, k, 16 * i + (16 if k < 2 else 32))
            for e in range(E - WRING, E):
                expert(e, e % WRING, 16 * ((e + 2) // WRING + 1), ahead=(e + 2 < E))

        @block.vector
        def _(dve):
            v = nc.vector
            ch = Chain(dve, s["dve_chain"])

            def lw(l):
                dve.wait_ge(ld[f"pk{l}"], 48 - 16 * l)
                if l:
                    dve.wait_ge(s["conv_tanh"], DT)
                ch.step(v.tensor_scalar(cbh[:], pk[l][:, PK_CB:PK_CB + DT], 0.5, None, ALU.mult))
                w = pk[l][:, PK_IN:PK_IN + DI].unsqueeze(1).broadcast_to([P, DC, DI])
                ch.wait()
                v.tensor_tensor(LW[l], LW[l], w, ALU.mult).then_inc(s["lw_ready"], 1)

            def u_half(l, d):
                dve.wait_ge(s["conv_tanh"], DT * l + d + 1)
                c0 = CONV_BANK[l] + 2 * d
                return ch.step(v.tensor_scalar(DU[:, d, :], ps[:, c0:c0 + 2, :].rearrange("p a b -> p (a b)"),
                                               pk[l][:, PK_CB + d:PK_CB + d + 1], 0.5, ALU.add, ALU.mult))

            def u_calc(l, d, mark):
                ch.wait(mark)
                v.scalar_tensor_tensor(U[:, d, :], DEL[:, d, :], 1.0, DU[:, d, :], ALU.add, ALU.mult).then_inc(s["u_ready"], 1)

            def delta_max(l):
                for d in range(DT):
                    dve.wait_ge(s["sp_abs"], DT * l + d + 1)
                    c0 = CONV_BANK[l] + 2 * d
                    ch.step(v.tensor_scalar(DEL[:, d, :], ps[:, c0:c0 + 2, :].rearrange("p a b -> p (a b)"),
                                            pk[l][:, PK_DB + d:PK_DB + d + 1], 0.0, ALU.add, ALU.max))

            def delta_round(l):
                dve.wait_ge(s["sp_exp"], l + 1)
                ch.link(v.tensor_scalar(hS[1][:], hS[0][:], 1.0, None, ALU.add))
                ch.link(v.scalar_tensor_tensor(hS[1][:].rearrange("p a b -> p (a b)"), hS[1][:].rearrange("p a b -> p (a b)"), -1.0,
                                               hS[0][:].rearrange("p a b -> p (a b)"), ALU.add, ALU.subtract))
                ch.step(v.tensor_tensor(DEL[:], DEL[:], hS[1][:], ALU.subtract))

            def delta_sum(l):
                ch.wait()
                dve.wait_ge(s["sp_ln"], l + 1)
                v.tensor_tensor(DEL[:], DEL[:], dA[1][:], ALU.add).then_inc(s["delta_ready"], 1)

            def delta_u(l):
                dve.wait_ge(s["delta_ready"], l + 1)
                v.tensor_tensor(DU[:], DEL[:], U[:], ALU.mult).then_inc(s["du_ready"], 1)

            def d_u(l):
                dve.wait_ge(s["du_ready"], l + 1)
                for d in range(DT):
                    last = v.tensor_scalar(ACC[:, d, :], U[:, d, :], skip[:, l, d:d + 1], None, ALU.mult)
                last.then_inc(s["acc_ready"], 1)

            def ssm_dbu(l, n):
                g = DS * l + n
                bcb, h = BCb[g % SB_LOADS], hS[g % 2]
                dve.wait_ge(ld_bc[g % SB_LOADS], 16 * (g // SB_LOADS + 1))
                if n == 0:
                    dve.wait_ge(s["du_ready"], l + 1)
                if g >= 2:
                    dve.wait_ge(s["ssm_acc"], g - 1)
                v.tensor_tensor(h[:], DU[:], bcb[:, 0:1, :].broadcast_to([P, DT, T]), ALU.mult).then_inc(s["dbu_ready"], 1)

            def ssm_scan(l, n):
                g = DS * l + n
                bcb, h, a = BCb[g % SB_LOADS], hS[g % 2], dA[g % 2]
                dve.wait_ge(s["dbu_ready"], g + 1)
                dve.wait_ge(s["da_ready"], 2 * (g + 1))
                f = lambda z: z[:].rearrange("p d t -> p (d t)")
                v.tensor_tensor_scan(f(h), f(a), f(h), 0.0, ALU.mult, ALU.add).then_inc(s["scan_done"], 1)
                if n in C_ON_DVE[l]:
                    dve.wait_ge(s["scan_done"], g + 1)
                    v.tensor_tensor(h[:], h[:], bcb[:, 1:2, :].broadcast_to([P, DT, T]), ALU.mult).then_inc(s["c_dve"], 1)

            def ssm_step(l, n):
                ssm_dbu(l, n)
                ssm_scan(l, n)

            def ln_stats(L, hf):
                tiles = range(4 * hf, 4 * hf + 4)
                for t in tiles:
                    if L == 0:
                        dve.wait_ge(ld["x"], 16)
                    elif L == 4:
                        dve.wait_ge(s["x_new"], XN_FFN + t // 2 + 1)
                    else:
                        dve.wait_ge(s["x_new"], XN[L] - 1 + hf)
                    ch.step(v.bn_stats(lnst[:, t, :], X[:, t, :]))
                base = ch.n - 4
                for k, t in enumerate(tiles):
                    ch.wait(base + k + 1)
                    v.bn_aggr(lnmv[:, t, :], lnst[:, t, :]).then_inc(s["ln_mv"], 1)

            def ln_apply(L, hf):
                dve.wait_ge(s["ln_rstd"], 2 * L + hf + 1)
                for t in range(4 * hf, 4 * hf + 4):
                    v.tensor_scalar(H[:, t, :], X[:, t, :], lnmv[:, t, 0:1], lnrs[:, t:t + 1], ALU.subtract,
                                    ALU.mult).then_inc(s["ln_h"], 1)

            def ln_tr_copy(i, hf):
                dve.wait_ge(s["ln_tr_mm"], 4 * i + 2 * hf + 2)
                v.tensor_copy(hT[:, 1, 512 * hf:512 * hf + 512], ps[:, TR_BANK[i][hf] + 1, :]).then_inc(s["ln_tr_dve"], 1)

            def residual(bank0, ready, count, hf):
                dve.wait_ge(s[ready], count)
                x = X[:, 4 * hf:4 * hf + 4, :].rearrange("p t d -> p (t d)")
                v.tensor_tensor(x, x, ps[:, bank0 + 2 * hf:bank0 + 2 * hf + 2, :].rearrange("p a b -> p (a b)"),
                                ALU.add).then_inc(s["x_new"], 1)

            both = (0, 1)
            lw(0)
            for hf in both:
                ln_stats(0, hf)
            for hf in both:
                ln_apply(0, hf)
            for d in range(DT):
                u_calc(0, d, u_half(0, d))
            for hf in both:
                ln_tr_copy(0, hf)
            delta_max(0)
            delta_round(0)
            delta_sum(0)
            delta_u(0)
            ssm_dbu(0, 0)
            d_u(0)
            dve.wait_ge(s["qkv0_copied"], NT)
            dve.wait_ge(ld["rope0"], 32)
            v.tensor_tensor(tb0(RA), tb0(QK0), cos0.unsqueeze(1).broadcast_to([P, B, 2, NQK0]), ALU.mult).then_inc(s["rope0_cos"], 1)
            ssm_scan(0, 0)
            dve.wait_ge(s["rope0_add"], 1)
            ch.link(v.tensor_reduce(st0[:, 0, :], QKV0, AX.X, ALU.add))
            v.tensor_scalar(st0[:, 0, :], st0[:, 0, :], 1.0 / D0, None, ALU.mult).then_inc(s["rope0_mean"], 1)
            ssm_step(0, 1)
            dve.wait_ge(s["rope0_sq"], 1)
            ch.link(v.tensor_reduce(st0[:, 1, :], SQ0.rearrange("p (n d) -> p n d", d=D0), AX.X, ALU.add))
            ch.link(v.tensor_scalar(st0[:, 1, :], st0[:, 1, :], 1.0 / D0, 1e-6, ALU.mult, ALU.add))
            ch.link(v.tensor_single_scalar(st0[:, 2, :].bitcast(I32), st0[:, 1, :].bitcast(I32), 1, ALU.arith_shift_right))
            ch.link(v.tensor_scalar(st0[:, 2, :].bitcast(I32), st0[:, 2, :].bitcast(I32), -1.0, float(0x5F3759DF), ALU.mult, ALU.add))
            for k in range(4):
                ch.link(v.tensor_tensor(st0[:, 3, :], st0[:, 2, :], st0[:, 2, :], ALU.mult))
                ch.link(v.scalar_tensor_tensor(st0[:, 3, :], st0[:, 3, :], -0.5, st0[:, 1, :], ALU.mult, ALU.mult))
                last = v.scalar_tensor_tensor(st0[:, 2, :], st0[:, 3, :], 1.5, st0[:, 2, :], ALU.add, ALU.mult)
                if k < 3:
                    ch.link(last)
            last.then_inc(s["rope0_rs"], 1)

            def at0(u):
                b, g = u // KV0, u % KV0
                dve.wait_ge(s["pv0_tr"], u + 1)
                if u:
                    dve.wait_ge(s["at0_ready"], u)
                o = ps[:, 6 + u % 2, 0:2 * REP0 * (D0 + 1)].rearrange("p (h d) -> p h d", d=D0 + 1)
                v.reciprocal(rden0[:], o[:, :, D0 * (1 - g)]).then_inc(s["at0_den"], 1)
                dve.wait_ge(s["at0_den"], u + 1)
                v.tensor_tensor(H[:, 2 * b:2 * b + 2, P * g:P * g + P].rearrange("p t (r d) -> p t r d", d=D0),
                                o[:, :, g:g + D0].rearrange("p (t r) d -> p t r d", t=2),
                                rden0[:].rearrange("p (t r) -> p t r", t=2).unsqueeze(3).broadcast_to([P, 2, REP0, D0]),
                                ALU.mult).then_inc(s["at0_ready"], 1)

            def a_tr_copy(hf):
                dve.wait_ge(s["a_tr_mm"], 2 * hf + 2)
                v.tensor_copy(aT0[:, 1, 512 * hf:512 * hf + 512], ps[:, 5, :]).then_inc(s["a_tr_dve"], 1)

            for n in range(2, DS):
                ssm_step(0, n)
                for u in range(B * KV0):
                    if AT0_AT[u] == n:
                        at0(u)
                        if u == A_TR_UNIT:
                            a_tr_copy(0)
            a_tr_copy(1)
            lw(1)
            for hf in both:
                residual(0, "o0_mm", hf + 1, hf)
                ln_stats(1, hf)

            def gate(l):
                dve.wait_ge(s["ssm_acc"], DS * (l + 1))
                for hf in both:
                    ln_apply(1 + 3 * l, hf)
                for hf in both:
                    dve.wait_ge(s["gate_tanh"], 2 * l + hf + 1)
                    flat = H[:, 4 * hf:4 * hf + 4, :].rearrange("p a b -> p (a b)")
                    ch.link(v.scalar_tensor_tensor(flat, hT[:, hf, :], 1.0, flat, ALU.add, ALU.mult))
                    for d in range(DT):
                        gt = H[:, 4 * hf:4 * hf + 4, :].rearrange("p (b h) n -> p b h n", h=2)[:, :, d, :]
                        a = bands(ACC[:, d, :])[:, 2 * hf:2 * hf + 2, :]
                        v.scalar_tensor_tensor(a, a, 0.5, gt, ALU.mult, ALU.mult).then_inc(s["gate_y"], 1)
                for hf in both:
                    residual(0, "gate_mm", 2 * l + hf + 1, hf)
                    ln_stats(2 + 3 * l, hf)

            gate(0)
            for hf in both:
                ln_apply(2, hf)
            for hf in both:
                ln_tr_copy(1, hf)
            marks = [u_half(1, d) for d in range(DT)]
            for d in range(DT):
                u_calc(1, d, marks[d])
            dve.wait_ge(ld["ffn"], 48)
            ch.link(v.tensor_scalar(fsc[:, 2, :], fsc[:, 0, :], 0.5, None, ALU.mult))
            v.tensor_tensor(fsc[:, 1, :], fsc[:, 1, :], fsc[:, 2, :], ALU.mult).then_inc(s["fsc_ready"], 1)

            def w1_means():
                dve.wait_ge(ld["wqkv1"], 16)
                for c in range(HC):
                    ch.step(v.tensor_reduce(wmean[:, c, :], WB[:, c, 0:NQ1 + NK1].rearrange("p (h d) -> p h d", d=D1), AX.X, ALU.add))
                ch.wait()
                v.tensor_scalar(wmean[:], wmean[:], -1.0 / D1, None, ALU.mult).then_inc(s["w1_mean"], 1)

            def tables():
                dve.wait_ge(ld["rope1"], 32)
                for x in range(2):
                    row = lambda i: gains[:, 4 * x + i, :].unsqueeze(1).broadcast_to([P, 2, D1])
                    cs, sn = rope1[:, 2 * x, :, :], rope1[:, 2 * x + 1, :, :]
                    t = lambda i: tabs[:, 3 * x + i, :, :]
                    ch.step(v.tensor_tensor(t(0), cs, row(0), ALU.mult))
                    ch.step(v.tensor_tensor(t(1), sn, row(2), ALU.mult))
                    ch.step(v.tensor_tensor(t(2), cs, row(1), ALU.mult))
                    ch.link(v.tensor_tensor(sn, sn, row(3), ALU.mult))
                    last = v.tensor_tensor(t(2), t(2), sn, ALU.add)
                    ch.step(last)
                ch.wait()

            step = iter(range(DS))
            for j in range(2 * NI):
                m, i, hf = mlen(j // 2), j // 2, j % 2
                dve.wait_ge(s["fsc_ready"], 1)
                dve.wait_ge(s["f_tanh"], j + 1)
                v.scalar_tensor_tensor(ft1[j % 2][0:m, :], fth[j % 2][0:m, :], 1.0, ps[0:m, 2 * (j % 2), :], ALU.add,
                                       ALU.mult).then_inc(s["f_hid"], 1)
                dve.wait_ge(s["f_hid"], 2 * j + 1)
                v.scalar_tensor_tensor(hid0[0:m, i, 512 * hf:512 * hf + 512], ps[0:m, 2 * (j % 2) + 1, :], fsc[0:m, 1, i:i + 1],
                                       ft1[j % 2][0:m, :], ALU.mult, ALU.mult).then_inc(s["f_hid"], 1)
                if j == 1:
                    w1_means()
                if j == PREP_DT:
                    delta_max(1)
                if j == PREP_DT + 1:
                    delta_round(1)
                if j == PREP_DT + 2:
                    delta_sum(1)
                if j == PREP_DT + 3:
                    delta_u(1)
                    d_u(1)
                if j in FFN_SSM_AT:
                    ssm_step(1, next(step))
            ssm_step(1, 0)
            tables()
            residual(4, "fd_mm", 2, 0)
            ln_stats(3, 0)
            ssm_step(1, 1)
            ln_apply(3, 0)
            ln_tr_copy(2, 0)
            residual(4, "fd_mm", 4, 1)
            ln_stats(3, 1)
            ln_apply(3, 1)

            def job(b, i):
                j, x = JOB[b, i], 0 if i else 1
                k = job_bank(j)
                pj = ps[:, k:k + 2, :].rearrange("p t (h d) -> p t h d", d=D1)
                bc = lambda a: a.unsqueeze(2).broadcast_to([P, 2, REP1, a.shape[-1]])
                h4 = lambda a: a.rearrange("p t (h d) -> p t h d", d=D1)
                dve.wait_ge(s["job_sq"], j + 1)
                if j > 1:
                    dve.wait_ge(s["job_rope"], 8 * (j if j > 2 else 1))
                hd = D1 // 2
                v.tensor_tensor(h4(job_a(j)), pj, bc(tabs[:, 3 * x, :, :]), ALU.mult).then_inc(s["job_rot"], 1)
                for y in range(2):
                    v.tensor_tensor(h4(job_b(j))[:, :, :, hd * y:hd * y + hd], pj[:, :, :, hd * (1 - y):hd * (1 - y) + hd],
                                    bc(tabs[:, 3 * x + 1, :, hd * y:hd * y + hd]), ALU.mult).then_inc(s["job_rot"], 1)

            def job_sum(b, i):
                j = JOB[b, i]
                if j >= 2:
                    dve.wait_ge(s["job_rope"], 8 * (j - 1))
                dve.wait_ge(s["job_sq"], j + 1)
                v.tensor_reduce(jst[:, j % 2, 0, :], job_s(j).rearrange("p t (h d) -> p (t h) d", d=D1), AX.X, ALU.add).then_inc(s["job_sum"], 1)

            def job_rope(b, i):
                j, x = JOB[b, i], 0 if i else 1
                dve.wait_ge(s["job_add"], j + 1)
                dve.wait_ge(s["job_rstd"], j + 1)
                if j:
                    dve.wait_ge(s["job_tr_mm"], 2 * j)
                for t in range(2):
                    for h in range(REP1):
                        c = slice(D1 * h, D1 * h + D1)
                        v.scalar_tensor_tensor(R[:, t, c], job_a(j)[:, t, c], jst[:, j % 2, 2, REP1 * t + h:REP1 * t + h + 1],
                                               tabs[:, 3 * x + 2, t, :], ALU.mult, ALU.add).then_inc(s["job_rope"], 1)

            def max1(u):
                p = u % 2
                dve.wait_ge(s["s1_mm"], u + 1)
                if u >= 2:
                    dve.wait_ge(s["s1_exp"], 2 * (u - 1))
                ch.step(v.tensor_reduce(nm1[:, p, 0:1], ps[:, 3 + p, 0:P], AX.X, ALU.max, negate=True))
                v.tensor_reduce(nm1[:, p, 1:2], ps[:, 3 + p, P:3 * P], AX.X, ALU.max, negate=True).then_inc(s["s1_max"], 1)

            def norm1(u):
                p = u % 2
                dve.wait_ge(s["s1_exp"], 2 * (u + 1))
                ch.link(v.reciprocal(rc1[:, p, :], sum1[:, p, :]))
                v.tensor_scalar(P1[p][:, 0:P], P1[p][:, 0:P], rc1[:, p, 0:1], None, ALU.mult).then_inc(s["s1_norm"], 1)
                v.tensor_scalar(P1[p][:, P:3 * P], P1[p][:, P:3 * P], rc1[:, p, 1:2], None, ALU.mult).then_inc(s["s1_norm"], 1)

            for kind, a in ATT1_PLAN:
                if kind == "rot":
                    job(*a)
                elif kind == "ln1":
                    ln_tr_copy(2, 1)
                elif kind == "sum":
                    job_sum(*a)
                elif kind == "rope":
                    job_rope(*a)
                elif kind == "max":
                    max1(a)
                elif kind == "norm":
                    norm1(a)
                elif kind == "dbu":
                    ssm_dbu(1, a)
                elif kind == "scan":
                    ssm_scan(1, a)
                elif kind == "res":
                    dve.wait_ge(s["o1_mm"], H1 * (a + 1))
                    x = X[:, 2 * a:2 * a + 2, :].rearrange("p t d -> p (t d)")
                    v.tensor_tensor(x, x, ps[:, 7, :], ALU.add).then_inc(s["x_new"], 1)
            for hf in both:
                ln_stats(4, hf)
            gate(1)
            for hf in both:
                ln_apply(5, hf)
            for hf in both:
                ln_tr_copy(3, hf)

            z = slice(0, 512)
            dve.wait_ge(s["h_hi"], 1)
            v.tensor_tensor(hTl[:, :, z], hT[:, :, z], hTh[:, :, z].bitcast(F32), ALU.subtract).then_inc(s["h_lo_dve"], 1)

            for z in (rGW, rMS, rT8, rE8):
                ch.step(v.memset(z, -1.0))
            dve.wait_ge(s["r_tr"], 1)
            v.tensor_scalar(rS, ps[:, 6, 0:NT * E].rearrange("p (t e) -> p t e", t=NT), 1.0, None, ALU.add).then_inc(s["r_sum"], 1)
            dve.wait_ge(s["r_sum"], 1)
            ch.link(v.reciprocal(rS, rS))
            q4 = rS.rearrange("p t (g e) -> p (t g) e", e=EPG)
            col = lambda i: q4[:, :, i]
            ch.step(v.tensor_tensor(rg[0], col(0), col(1), ALU.max))
            ch.step(v.tensor_tensor(rg[1], col(0), col(1), ALU.min))
            ch.step(v.tensor_tensor(rg[2], col(2), col(3), ALU.max))
            ch.link(v.tensor_tensor(rg[3], col(2), col(3), ALU.min))
            ch.step(v.tensor_tensor(rg[4], rg[0], rg[2], ALU.max))
            ch.step(v.tensor_tensor(rg[5], rg[0], rg[2], ALU.min))
            ch.link(v.tensor_tensor(rg[1], rg[1], rg[3], ALU.max))
            ch.link(v.tensor_tensor(rg[1], rg[1], rg[5], ALU.max))
            ch.link(v.tensor_tensor(rGW[:, :, 0:G], rg[4].rearrange("p (t g) -> p t g", g=G),
                                    rg[1].rearrange("p (t g) -> p t g", g=G), ALU.add))
            for t in range(NT):
                ch.step(v.max(rM8[:, t, :], rGW[:, t, 0:G]))
            ch.wait()
            ch.link(v.tensor_copy(rT8[:, :, 0:KG], rM8[:, :, 0:KG]))
            for t in range(NT):
                ch.step(v.match_replace(rGM[:, t, :], rT8[:, t, :], rGW[:, t, :], -2.0))
            ch.wait()
            ch.link(v.tensor_scalar(rGM, rGM, -2.0, None, ALU.is_equal))
            ch.link(v.tensor_tensor(rW.rearrange("p t (g e) -> p t g e", e=EPG), rS.rearrange("p t (g e) -> p t g e", e=EPG),
                                    rGM[:, :, 0:G].unsqueeze(3).broadcast_to([P, NT, G, EPG]), ALU.mult))
            ch.link(v.tensor_copy(rMS[:, :, 0:E], rW))
            for t in range(NT):
                ch.step(v.max(rM8[:, t, :], rMS[:, t, 0:E]))
            ch.wait()
            ch.link(v.tensor_copy(rE8[:, :, 0:K], rM8[:, :, 0:K]))
            for t in range(NT):
                ch.step(v.match_replace(rME[:, t, :], rE8[:, t, :], rMS[:, t, :], -2.0))
            ch.wait()
            ch.link(v.tensor_scalar(rME, rME, -2.0, None, ALU.is_equal))
            ch.link(v.tensor_tensor(rW, rS, rME[:, :, 0:E], ALU.mult))
            ch.link(v.tensor_reduce(rsum[:, 0, :], rW, AX.X, ALU.add))
            ch.link(v.tensor_scalar(rsum[:, 0, :], rsum[:, 0, :], 1e-20, None, ALU.add))
            ch.link(v.reciprocal(rsum[:, 1, :], rsum[:, 0, :]))
            ch.link(v.tensor_tensor(rW, rW, rsum[:, 1, :].unsqueeze(2).broadcast_to([P, NT, E]), ALU.mult))
            v.tensor_scalar(rGate, rW, ROUTE_SCALE, None, ALU.mult).then_inc(s["r_gate"], 1)
            with dve.Fori(0, E // WRING, 1) as i:
                for k in range(WRING):
                    p = k % 2
                    f = ps[:, 2 * p:2 * p + 2, :].rearrange("p a b -> p (a b)")
                    dve.wait_ge(ld_gb[k], 16 * i + 16)
                    dve.wait_ge(s["m_relu"], WRING * i + (k + 3))
                    v.scalar_tensor_tensor(MG[p], f, 0.0, GB[k], ALU.max, ALU.mult).then_inc(s["m_gated"], 1)
                    dve.wait_ge(s["m_gated"], WRING * i + (k + 1))
                    dve.wait_ge(s["m_lo"], WRING * i + (k + 1))
                    v.tensor_tensor(MH[p], MG[p], MR[p], ALU.mult).then_inc(s["m_hid"], 1)
            for hf in both:
                residual(4, "m_last", hf + 1, hf)

        @block.tensor
        def _(pe):
            mm, tr = nc.tensor.matmul, nc.tensor.transpose

            def conv(l):
                pe.wait_ge(s["lw_ready"], l + 1)
                pe.wait_ge(ld["ctx"], 16)
                for d in range(DT):
                    for hf in range(2):
                        for k in range(DC):
                            last = mm(ps[:, CONV_BANK[l] + 2 * d + hf, :], LW[l][:, k, P * d:P * d + P], ctxp[:, 2 * hf:2 * hf + 2, k:k + S],
                                      start=(k == 0), stop=(k == DC - 1))
                    last.then_inc(s["conv_mm"], 1)

            def xdbl(l):
                pe.wait_ge(s["u_ready"], DT * (l + 1))
                xp = pk[l][:, PK_X:PK_N].rearrange("p (d n) -> p d n", d=DT)
                for hf in range(2):
                    for d in range(DT):
                        last = mm(ps[0:DR + 2 * DS, CONV_BANK[l] + hf, :], xp[:, d, :], U[:, d, 512 * hf:512 * hf + 512],
                                  start=(d == 0), stop=(d == DT - 1))
                last.then_inc(s["xdbl_mm"], 1)

            def dtpre(l):
                pe.wait_ge(s["xdbl_copied"], l + 1)
                for d in range(DT):
                    for hf in range(2):
                        last = mm(ps[:, CONV_BANK[l] + 2 * d + hf, :], dtw[l][:, P * d:P * d + P], dA[0][0:DR, 0, 512 * hf:512 * hf + 512],
                                  start=True, stop=True)
                    last.then_inc(s["dtpre_mm"], 1)

            def ln_tr(i, halves=(0, 1)):
                L = TR_LNS[i]
                for hf in halves:
                    pe.wait_ge(s["ln_h"], NT * L + 4 * hf + 4)
                    for c in range(HC):
                        for t in range(4):
                            last = tr(ps[:, TR_BANK[i][hf] + c, P * t:P * t + P], H[:, 4 * hf + t, P * c:P * c + P], ident[:])
                        last.then_inc(s["ln_tr_mm"], 1)

            def ln_ready(i, hf):
                pe.wait_ge(s["ln_tr_act"], 2 * i + hf + 1)
                pe.wait_ge(s["ln_tr_dve"], 2 * i + hf + 1)

            conv(0)
            pe.wait_ge(ld["ident"], 16)
            ln_tr(0)
            xdbl(0)
            pe.wait_ge(ld["wqkv0"], 16)
            dtpre(0)
            for t in range(NT):
                ln_ready(0, 1)
                if t >= 4:
                    pe.wait_ge(s["qkv0_copied"], t - 3)
                for c in range(HC):
                    last = mm(ps[:, 4 + t % 4, 0:NQKV0], hT[:, c, P * t:P * t + P], WQKV0[:, c, :], start=(c == 0), stop=(c == HC - 1))
                last.then_inc(s["qkv0_mm"], 1)
            pe.wait_ge(s["rope0_done"], 1)
            for i in range(8):
                g, part, hf = i // 4, (i // 2) % 2, i % 2
                pe.wait_ge(s["tr0_copied"], i - 3) if i >= 4 else pe.wait_ge(s["qkv0_copied"], NT)
                for t in range(4):
                    tile = Q0[:, 4 * hf + t, :]
                    if part == 0:
                        src = tile[:, P * g:P * g + P]
                    else:
                        pe.wait_ge(s["k4_ready"], g + 1)
                        src = K40[:, 4 * hf + t, g, :]
                    last = tr(ps[:, 4 + i % 4, P * t:P * t + P], src, ident[:])
                last.then_inc(s["tr0_mm"], 1)
            pe.wait_ge(ld["masks"], 48)
            pe.wait_ge(s["delta_ready"], 1)

            def s0(u):
                b, g = u // KV0, u % KV0
                pe.wait_ge(s["tr0_copied"], 4 * g + 4)
                if u:
                    pe.wait_ge(s["s0_tanh"], u)
                q0 = S * b
                for r in range(REP0):
                    rows = slice(D0 * r, D0 * r + D0)
                    mm(ps[:, r, 0:W0 + P], identb[:], mask0[:], start=True, stop=True, skip_group_check=True)
                    mm(ps[:, r, 0:W0], kT0[rows, g, q0:q0 + P], qT0[rows, g, q0:q0 + W0], start=False, stop=True, skip_group_check=True)
                    last = mm(ps[:, r, W0:W0 + P], kT0[rows, g, q0 + P:q0 + S], qT0[rows, g, q0 + P:q0 + S], start=False, stop=True,
                              skip_group_check=True)
                last.then_inc(s["s0_mm"], 1)

            def pv0(u):
                b, g = u // KV0, u % KV0
                pe.wait_ge(s["s0_exp"], 2 * (u + 1))
                pe.wait_ge(s["v0_ready"], KV0)
                if u:
                    pe.wait_ge(s["pv0_copied"], u)
                else:
                    pe.wait_ge(s["tr0_copied"], 8)
                for x in range(2):
                    for kb_ in range(2):
                        last = mm(ps[0:D0 + 1, 4 + x, :], V0[:, 2 * b + kb_, D0 * g:D0 * g + D0 + 1],
                                  PT0[u % 2][:, 2 * x:2 * x + 2, kb_, :], start=(kb_ == 0), stop=(kb_ == 1))
                last.then_inc(s["pv0_mm"], 1)

            def pv0_tr(u):
                pe.wait_ge(s["pv0_copied"], u + 1)
                pe.wait_ge(s["at0_ready"], u - 1) if u >= 2 else pe.wait_ge(s["tr0_copied"], 8)
                for t in range(2):
                    for r in range(REP0):
                        c = (REP0 * t + r) * (D0 + 1)
                        last = tr(ps[:, 6 + u % 2, c:c + D0 + 1], O0[:, S * r + P * t:S * r + P * t + P], ident[0:D0 + 1, 0:D0 + 1])
                last.then_inc(s["pv0_tr"], 1)

            def a_tr(hf):
                pe.wait_ge(s["at0_ready"], B * KV0 // 2 * (hf + 1))
                for c in range(HC):
                    for t in range(4):
                        last = tr(ps[:, 4 + c, P * t:P * t + P], H[:, 4 * hf + t, P * c:P * c + P], ident[:])
                    last.then_inc(s["a_tr_mm"], 1)

            s0(0)
            for u in range(B * KV0):
                if u + 1 < B * KV0:
                    s0(u + 1)
                if u:
                    pv0_tr(u - 1)
                if u - 1 == A_TR_UNIT:
                    a_tr(0)
                    pe.wait_ge(s["a_tr_act"], 1)
                    pe.wait_ge(s["a_tr_dve"], 1)
                pv0(u)
            pv0_tr(B * KV0 - 1)

            def o0(hf):
                pe.wait_ge(s["a_tr_act"], hf + 1)
                pe.wait_ge(s["a_tr_dve"], hf + 1)
                for t in range(4 * hf, 4 * hf + 4):
                    for g in range(KV0):
                        last = mm(ps[:, t // 2, 256 * (t % 2):256 * (t % 2) + 256], aT0[:, g, P * t:P * t + P], WO0[:, g, :],
                                  start=(g == 0), stop=(g == KV0 - 1))
                last.then_inc(s["o0_mm"], 1)

            pe.wait_ge(ld["wo0"], 16)
            pe.wait_ge(s["s0_tanh"], B * KV0)
            o0(0)
            a_tr(1)
            o0(1)

            def gate_tr(l):
                for hf in range(2):
                    pe.wait_ge(s["gate_y"], 2 * DT * l + DT * (hf + 1))
                    for t in range(4 * hf, 4 * hf + 4):
                        for d in range(DT):
                            last = tr(ps[:, t // 2, 256 * (t % 2) + P * d:256 * (t % 2) + P * d + P], ACC[:, d, P * t:P * t + P], ident[:])
                    last.then_inc(s["gate_mm"], 1)

            conv(1)
            pe.wait_ge(s["x_new"], XN_ATT0)
            gate_tr(0)
            ln_tr(1)
            pe.wait_ge(ld["ffn"], 48)
            for j in range(2 * NI):
                m, i, hf = mlen(j // 2), j // 2, j % 2
                ln_ready(1, min(j, 1))
                if j >= 2:
                    pe.wait_ge(s["f_hid"], 2 * (j - 1))
                for x in range(2):
                    for c in range(HC):
                        last = mm(ps[0:m, 2 * (j % 2) + x, :], WGU[:, c, INTER * x + P * i:INTER * x + P * i + m],
                                  hT[:, c, 512 * hf:512 * hf + 512], start=(c == 0), stop=(c == HC - 1))
                last.then_inc(s["f_mm"], 1)
                if j == PREP_XDBL:
                    xdbl(1)
                if j == PREP_DT:
                    dtpre(1)
            pe.wait_ge(s["delta_ready"], 2)
            pe.wait_ge(s["f_hid"], 4 * NI)
            pe.wait_ge(s["wdn_ready"], NI)
            for t in range(NT):
                for i in range(NI):
                    m = mlen(i)
                    last = mm(ps[:, 4 + t // 2, 256 * (t % 2):256 * (t % 2) + 256], hid0[0:m, i, P * t:P * t + P], WDN[0:m, i, :],
                              start=(i == 0), stop=(i == NI - 1))
                if t % 2 == 1:
                    last.then_inc(s["fd_mm"], 1)
            ln_tr(2, (0,))
            ln_ready(2, 0)
            pe.wait_ge(s["w1_centered"], HC)

            def project(b, c0, bank):
                if b == B // 2:
                    ln_ready(2, 1)
                for t in range(2):
                    for c in range(HC):
                        last = mm(ps[:, bank + t, :], hT[:, c, P * (2 * b + t):P * (2 * b + t) + P], WB[:, c, c0:c0 + 512],
                                  start=(c == 0), stop=(c == HC - 1))
                return last

            def v_job(b):
                if b == 0:
                    ln_ready(2, 1)
                if b:
                    pe.wait_ge(s["job_rot"], 3 * V_AFTER[b])
                    pe.wait_ge(s["job_sq"], V_AFTER[b])
                project(b, NQ1 + NK1, v_bank(b)).then_inc(s["v_mm"], 1)

            def rope_job(b, i):
                j = JOB[b, i]
                if any(k <= j for k in V_AFTER[1:]):
                    pe.wait_ge(s["v_copied"], sum(k <= j for k in V_AFTER))
                if j == 1:
                    pe.wait_ge(s["x_new"], XN_FFN)
                if j > 1:
                    pe.wait_ge(s["job_rot"], 3 * j)
                    pe.wait_ge(s["job_sq"], j)
                project(b, NQ1 if i == 0 else NK1 * (i - 1), job_bank(j)).then_inc(s["job_mm"], 1)

            def job_tr(b, i, x):
                j = JOB[b, i]
                pe.wait_ge(s["job_rope"], 8 * (j + 1))
                if j == 0:
                    ln_ready(2, 1)
                if j or x:
                    pe.wait_ge(s["job_tr_copied"], 2 * j + x)
                for h in range(2):
                    for t in range(2):
                        last = tr(ps[:, 2, S * h + P * t:S * h + P * t + P], R[:, t, D1 * (2 * x + h):D1 * (2 * x + h) + D1], ident[:])
                last.then_inc(s["job_tr_mm"], 1)

            def s1(u):
                b, h = u // H1, u % H1
                g, p = h // REP1, u % 2
                pe.wait_ge(s["job_tr_copied"], 2 * max(JOB[b, 0], JOB[b, 1 + g]) + 2)
                if u < 2:
                    pe.wait_ge(s["v_copied"], 1)
                else:
                    pe.wait_ge(s["s1_exp"], 2 * (u - 1))
                q, k = QT[(4 * b + g) % 2], KT[b % 2]
                mm(ps[:, 3 + p, 0:3 * P], identb[:], mask1[:], start=True, stop=True, skip_group_check=True)
                mm(ps[:, 3 + p, 0:P], q[:, h % REP1, 0:P], k[:, g, 0:P], start=False, stop=True, skip_group_check=True)
                mm(ps[:, 3 + p, P:3 * P], q[:, h % REP1, P:S], k[:, g, :], start=False, stop=True, skip_group_check=True).then_inc(s["s1_mm"], 1)

            def pt1(u):
                pe.wait_ge(s["s1_norm"], 2 * (u + 1))
                if u:
                    pe.wait_ge(s["pt1_copied"], u)
                for x in range(3):
                    last = tr(ps[:, 5, P * x:P * x + P], P1[u % 2][:, P * x:P * x + P], ident[:])
                last.then_inc(s["pt1_mm"], 1)

            def pv1(u):
                b, h = u // H1, u % H1
                g = h // REP1
                pe.wait_ge(s["pt1_copied"], u + 1)
                pe.wait_ge(s["v_copied"], b + 1)
                if u:
                    pe.wait_ge(s["at1_copied"], u)
                va = V1[b % 2]
                mm(ps[:, 6, 0:S], va[:, 0, D1 * g:D1 * g + D1], PT1[u % 2][:, 0:S], start=True, stop=True, skip_group_check=True)
                mm(ps[:, 6, P:S], va[:, 1, D1 * g:D1 * g + D1], PT1[u % 2][:, S:3 * P], start=False, stop=True,
                   skip_group_check=True).then_inc(s["pv1_mm"], 1)

            def o1(u):
                b, h = u // H1, u % H1
                pe.wait_ge(s["at1_copied"], u + 1)
                if u == 0:
                    pe.wait_ge(ld["wo1"], 16)
                if h == 0 and b:
                    pe.wait_ge(s["x_new"], XN_FFN + b)
                for t in range(2):
                    last = mm(ps[:, 7, 256 * t:256 * t + 256], aT1[u % 2][:, P * t:P * t + P], WO1[:, h, :], start=(h == 0 and t == 0),
                              stop=(h == H1 - 1), skip_group_check=True)
                last.then_inc(s["o1_mm"], 1)

            for kind, a in ATT1_PLAN:
                if kind == "v":
                    v_job(a)
                elif kind == "ln1":
                    ln_tr(2, (1,))
                elif kind == "proj":
                    rope_job(*a)
                elif kind == "tr":
                    job_tr(*a)
                elif kind == "s":
                    s1(a)
                elif kind == "pt":
                    pt1(a)
                elif kind == "pv":
                    pv1(a)
                elif kind == "o":
                    o1(a)
            gate_tr(1)
            ln_tr(3)
            pe.wait_ge(ld["route"], 32)
            for hf in range(2):
                ln_ready(3, hf)
                for c in range(HC):
                    last = mm(ps[0:E, 4 + hf, :], WRT[:, c, :], hT[:, c, 512 * hf:512 * hf + 512], start=(c == 0), stop=(c == HC - 1))
            last.then_inc(s["r_mm"], 1)

            def in_parts(out, wh, wl, xh, xl, start, stop, **kw):
                mm(out, wh, xh, start=start, stop=False, **kw)
                mm(out, wh, xl, start=False, stop=False, **kw)
                return mm(out, wl, xh, start=False, stop=stop, **kw)

            def w1(p, slot):
                for hf in range(2):
                    z = slice(512 * hf, 512 * hf + 512)
                    for c in range(HC):
                        m = slice(M * c, M * c + M)
                        last = in_parts(ps[:, 2 * p + hf, :], Wh[:, slot, m], Wl[:, slot, m], hTh[:, c, z], hTl[:, c, z],
                                        start=(c == 0), stop=(c == HC - 1))
                last.then_inc(s["m_mm"], 1)

            def w2(p, slot, first=False, final=False):
                w = slice(HC * M, HC * M + HID)
                for t in range(NT):
                    z = slice(P * t, P * t + P)
                    last = in_parts(ps[:, 4 + t // 2, 256 * (t % 2):256 * (t % 2) + 256], MHh[:, p, z], MHl[:, p, z],
                                    Wh[:, slot, w], Wl[:, slot, w], start=(first and t % 2 == 0), stop=final, skip_group_check=True)
                    if final and t % 4 == 3:
                        last.then_inc(s["m_last"], 1)
                if not final:
                    last.then_inc(s["m_out"], 1)

            pe.wait_ge(s["r_exp"], 1)
            for t in range(NT):
                last = tr(ps[:, 6, E * t:E * t + E], rET[:, P * t:P * t + P], ident[0:E, 0:E])
            last.then_inc(s["r_tr"], 1)
            pe.wait_ge(s["h_lo_dve"], 1)
            pe.wait_ge(s["h_lo_pool"], 1)
            pe.wait_ge(s["w_lo"], 2)
            w1(0, 0)
            w1(1, 1)
            pe.wait_ge(s["m_lo"], 1)
            pe.wait_ge(s["r_sum"], 1)
            w2(0, 0, first=True)
            pe.wait_ge(s["r_gate"], 1)
            pe.wait_ge(s["m_relu"], 2)
            for t in range(NT):
                last = tr(ps[0:E, 2 + t // 4, P * (t % 4):P * (t % 4) + P], rGate[:, t, :], ident[:])
            last.then_inc(s["gt_mm"], 1)
            pe.wait_ge(s["w_lo"], 3)
            w1(0, 2)
            pe.wait_ge(s["m_lo"], 2)
            w2(1, 1)
            pe.wait_ge(s["gt_copied"], 1)
            pe.wait_ge(s["w_lo"], 4)
            w1(1, 3)
            with pe.Fori(0, E // WRING - 1, 1) as i:
                for k in range(WRING):
                    pe.wait_ge(s["w_lo"], WRING * i + (k + 5))
                    pe.wait_ge(s["m_gated"], WRING * i + (k + 1))
                    w1(k % 2, k)
                    pe.wait_ge(s["m_lo"], WRING * i + (k + 3))
                    w2(k % 2, (k + 2) % WRING)
            for e in range(E - WRING, E):
                if e + 2 < E:
                    pe.wait_ge(s["w_lo"], e + 5)
                    pe.wait_ge(s["m_gated"], e + 1)
                    w1(e % 2, e % WRING)
                pe.wait_ge(s["m_lo"], e + 3)
                w2(e % 2, (e + 2) % WRING, final=(e == E - 1))


AT0_AT = [7, 8, 10, 11, 12, 14, 15, 15]
A_TR_UNIT = 4

SSM1_IN_FFN = 2
FFN_SSM_AT = []
PREP_XDBL, PREP_DT = 1, 3


def att1_plan():
    units = B * H1
    parts = {}

    def at(slot, *p):
        parts.setdefault(slot, []).append(p)

    def rope_job(slot, b, i, late=0):
        at(slot, "proj", (b, i))
        at(slot, "sq", (b, i))
        at(slot + 1, "rot", (b, i))
        at(slot + 1, "sum", (b, i))
        at(slot + late + 3, "rope", (b, i))
        for x in range(2):
            at(slot + late + 4, "tr", (b, i, x))
            at(slot + late + 4, "trc", (b, i, x))

    def v_job(slot, b):
        at(slot, "v", b)
        at(slot, "vc", b)

    rope_job(-8, 0, 0)
    rope_job(-7, 0, 1)
    rope_job(-5, 0, 2, late=3)
    at(-7, "wo1", 0)
    at(-6, "ln1", 0)
    v_job(-5, 0)
    for b in range(B):
        for g in range(KV1):
            u = H1 * b + REP1 * g
            if b or g > 1:
                rope_job(u - 6, b, g + 1)
        if b + 1 < B:
            rope_job(H1 * b + REP1, b + 1, 0)
            v_job(H1 * b + 2 * REP1, b + 1)
    cost = {"rot": 2.4, "sum": 1.2, "rope": 1.7, "dbu": 2.2, "scan": 2.2}
    ssm = []
    for n in range(SSM1_IN_FFN, DS):
        ahead = [("da", (n + 1, d)) for d in range(DT)] if n + 1 < DS else [None] * DT
        ssm += [("dbu", n), ahead[0], ("scan", n), ahead[1]]
    ssm = [("da", (SSM1_IN_FFN, d)) for d in range(DT)] + [p for p in ssm if p]
    price = lambda p: cost.get(p[0], 0) * (2 if p[0] == "scan" and p[1] in C_ON_DVE[1] else 1)
    total = sum(price(p) for u in range(units) for p in parts.get(u, [])) + sum(price(p) for p in ssm)
    plan = []
    spent = 0.0
    ok = lambda q: 0 <= q < units
    for u in range(min(parts), units + 4):
        mine = parts.get(u, [])
        pick = lambda *kinds: [p for kind in kinds for p in mine if p[0] == kind]
        tr, trc = pick("tr"), pick("trc")
        if ok(u - 4) and (u - 4) % H1 == H1 - 1:
            plan.append(("res", (u - 4) // H1))
        if ok(u + 1) or u == -1:
            plan.append(("s", u + 1))
        plan += tr[:1] + trc[:1]
        if ok(u):
            plan += [("max", u), ("exp", u)]
        if ok(u - 1):
            plan.append(("norm", u - 1))
        if ok(u - 2):
            plan += [("pv", u - 2), ("at", u - 2)]
        if ok(u - 3):
            plan.append(("o", u - 3))
        plan += tr[1:] + trc[1:]
        plan += pick("ln1", "v", "vc", "proj", "sq")
        now = []
        if ok(u):
            spent += sum(price(p) for p in mine)
            while ssm and spent + price(ssm[0]) / 2 < total * (u + 1) / (0.9 * units):
                spent += price(ssm[0])
                now.append(ssm.pop(0))
        plan += [p for p in now if p[0] == "da"]
        if ok(u - 1):
            plan += [("pt", u - 1), ("ptc", u - 1)]
        plan += pick("wo1", "rope", "rot", "sum") + [p for p in now if p[0] != "da"]
    return plan + ssm


ATT1_PLAN = att1_plan()
JOB = {a: j for j, a in enumerate(a for kind, a in ATT1_PLAN if kind == "proj")}
V_AFTER = [sum(kind == "proj" for kind, a in ATT1_PLAN[:ATT1_PLAN.index(("v", b))]) for b in range(B)]

_ORDER = ["x", "ctxp", "pk0", "pk1", "dtw0", "dtw1", "ident", "identb", "mask0", "mask1", "cos0", "sin0", "rope1", "gains",
          "wqkv0", "wo0", "ffn", "wdn", "skip", "fsc", "dsc", "wqkv1", "wo1", "we", "wrt", "br"]


def _layout(i):
    bf16 = mybir.dt.np(BF16)
    f = np.float32
    a = {k: np.asarray(v) for k, v in i.items()}
    o = {"x": a["x"]}
    c = np.zeros((P, B, S + DC - 1), f)
    c[:, :, DC - 1:] = a["ctx_1024"].transpose(2, 0, 1)
    o["ctxp"] = c
    chan = lambda z: z.reshape(DT, P, -1).transpose(1, 0, 2).reshape(P, -1)
    rows = lambda z: np.broadcast_to(z.reshape(1, -1), (P, z.size))
    for l in range(2):
        q = lambda n: a[f"L{l}_xattn_{n}"]
        cw = q("conv_w").reshape(DI, DC)
        xp = q("x_proj_w")
        order = list(range(DR)) + [DR + DS * r + n for n in range(DS) for r in range(2)]
        o[f"pk{l}"] = np.concatenate([q("in_proj_w").T, rows(cw.T), chan(q("conv_b")), chan(q("dt_proj_b")),
                                      chan(q("A_log")), chan(xp[order].T)], 1)
        o[f"dtw{l}"] = q("dt_proj_w").T
    wt = lambda w: w.T.reshape(-1, P, w.shape[0]).transpose(1, 0, 2)
    o["wqkv0"] = wt(np.concatenate([a["L0_attn_Wq"], a["L0_attn_Wk"], a["L0_attn_Wv"]], 0))
    o["wo0"] = wt(a["L0_attn_Wo"])
    gu = wt(np.concatenate([a["L0_ffn_gate_w"], a["L0_ffn_up_w"]], 0)).reshape(P, -1)
    dn = np.zeros((NI * P, HID), f)
    dn[:INTER] = a["L0_ffn_down_w"].T
    o["ffn"], o["wdn"] = gu, dn.reshape(NI, P, HID).transpose(1, 0, 2)
    o["skip"] = np.stack([chan(a[f"L{l}_xattn_D"]) for l in range(2)], 1)
    sc = np.zeros((2, NI * P), f)
    sc[0, :INTER], sc[1, :INTER] = a["L0_ffn_gate_s"], a["L0_ffn_up_s"]
    o["fsc"] = sc.reshape(2, NI, P).transpose(2, 0, 1)
    o["dsc"] = rows(a["L0_ffn_down_s"])
    o["wqkv1"] = wt(a["L1_attn_w_qkv"])
    o["wo1"] = wt(a["L1_attn_w_o"])
    w1 = np.concatenate([a["L1_ffn_W1"], a["L1_ffn_Ws1"].reshape(2, M, HID)], 0)
    w2 = np.concatenate([a["L1_ffn_W2"], a["L1_ffn_Ws2"].reshape(HID, 2, M).transpose(1, 0, 2)], 0)
    w1 = w1.transpose(0, 2, 1).reshape(E + 2, HC, P, M).transpose(0, 2, 1, 3).reshape(E + 2, P, HC * M)
    o["we"] = np.concatenate([w1, w2.transpose(0, 2, 1)], 2)
    o["wrt"] = wt(a["L1_ffn_Wr"])
    o["br"] = a["L1_ffn_br"].reshape(E, 1)
    g = [a["L1_attn_" + n] for n in ("qn_g", "qn_b", "kn_g", "kn_b")]
    sw = lambda z: np.concatenate([z[D1 // 2:], z[:D1 // 2]])
    o["gains"] = np.stack([rows(z) for z in (g[0], g[1], sw(g[0]), sw(g[1]), g[2], g[3], sw(g[2]), sw(g[3]))], 1)
    o["ident"] = np.eye(P, dtype=f)
    o["identb"] = np.eye(P).astype(bf16)
    k, qn = np.arange(P)[:, None], np.arange(W0)[None, :]
    m0 = np.where((k <= qn) & (k > qn - WIN0), 0.0, -100.0)
    o["mask0"] = np.concatenate([m0, m0[:, :P]], 1).astype(bf16)
    tri = np.where(np.arange(P)[None, :] <= k, 0.0, -1e30)
    o["mask1"] = np.concatenate([tri, np.zeros((P, P)), tri], 1).astype(bf16)

    def rope(dim):
        inv = (f(1.0) / (f(1e6) ** (np.arange(0, dim, 2, dtype=f) / f(dim)))).astype(f)
        fr = np.arange(S, dtype=f)[:, None] * inv[None, :]
        cs, sn = np.cos(fr), np.sin(fr)
        return np.concatenate([cs, cs], 1).astype(f), np.concatenate([-sn, sn], 1).astype(f)

    half = lambda z: z.reshape(2, P, -1).transpose(1, 0, 2)
    cs, sn = rope(D0)
    o["cos0"], o["sin0"] = half(np.tile(cs, (1, H0 + KV0))), half(np.tile(sn, (1, H0 + KV0)))
    cs, sn = rope(D1)
    qs = f(D1 ** -0.5)
    o["rope1"] = np.stack([half(cs * qs), half(sn * qs), half(cs), half(sn)], 1)
    return {n: np.ascontiguousarray(o[n]) for n in _ORDER}


def kernel(**inputs):
    import concourse.bacc as bacc
    from concourse.bass_utils import run_bass_kernel_spmd as run

    arrays = _layout(inputs)
    nc = bacc.Bacc("TRN2", target_bir_lowering=False, num_devices=1)
    io = {n: nc.dram_tensor("in_" + n, z.shape, mybir.dt.from_np(z.dtype), kind="ExternalInput").ap() for n, z in arrays.items()}
    out = nc.dram_tensor("out_0", (B, S, HID), F32, kind="ExternalOutput").ap()
    build(nc, io, out)
    r = run(nc, [{"in_" + n: z for n, z in arrays.items()}], core_ids=[0])
    return r.results[0]["out_0"]
```
